# Optimizing a Trainium2 kernel written in Bass

```python
import numpy as np
import jax
import jax.numpy as jnp

def _softmax(x, axis=-1):
    return jax.nn.softmax(x, axis=axis)

def _gelu(x):
    return jax.nn.gelu(x, approximate=True)

def _silu(x):
    return jax.nn.silu(x)

def _sigmoid(x):
    return jax.nn.sigmoid(x)

def _layernorm(x, axis=-1, eps=1e-05):
    m = jnp.mean(x, axis=axis, keepdims=True)
    v = jnp.var(x, axis=axis, keepdims=True)
    return (x - m) / jnp.sqrt(v + eps)

def _scatter_add(tgt, idx, src, axis=0):
    return tgt.at[idx].add(src)

def _segment_sum(src, seg, n):
    return jax.ops.segment_sum(src, seg, n)
kernel_name = 'mk_xattn_seq_d4_seqx_r8_62229d'

def setup_inputs(seed: int=0):
    np.random.seed(seed)
    _w = jnp.asarray

    def _rec_inputs():
        import jax
        import jax.numpy as jnp
        _rk = jax.random.key(seed)
        x = -0.0002928 + 1 * jax.random.normal(jax.random.fold_in(_rk, 1), (16, 64, 256), jnp.float32)
        _lenS = 64 - jax.random.randint(jax.random.fold_in(_rk, 7), (16,), 0, max(1, 64 // 4) + 1, jnp.int32)
        _lenS2 = 64 - jax.random.randint(jax.random.fold_in(_rk, 8), (16,), 0, max(1, 64 // 4) + 1, jnp.int32)
        _ctx_2048P = jax.random.normal(jax.random.fold_in(_rk, 11), (16, 16, 256), jnp.float32)
        _ctx_2048c = jax.random.dirichlet(jax.random.fold_in(_rk, 511), 0.3 * jnp.ones((16,), jnp.float32), (16, 64))
        _ctx_2048t = jnp.einsum('bsk,bkd->bsd', _ctx_2048c, _ctx_2048P)
        _ctx_2048t = _ctx_2048t * jax.lax.rsqrt(jnp.mean(jnp.square(_ctx_2048t)) + 1e-12) * 0.953939
        ctx_2048 = -1.39393e-06 + 0.999914 * (_ctx_2048t + 0.3 * jax.random.normal(jax.random.fold_in(_rk, 611), (16, 64, 256), jnp.float32))
        _validS = jnp.arange(64)[None, :] < _lenS[:, None]
        _validS2 = jnp.arange(64)[None, :] < _lenS2[:, None]
        _causal = jnp.tril(jnp.ones((64, 64), dtype=bool))
        mask_BxS2_ik0 = jnp.where(jnp.broadcast_to(_validS2[:, :], (16, 64)), 0, 1).astype(jnp.int32)
        mask_Bx1xSxS2_ff0 = jnp.where(jnp.ones((16, 1, 64, 64), dtype=bool), 0.0, -1000000000.0).astype(jnp.float32)
        return (x, ctx_2048, mask_BxS2_ik0, mask_Bx1xSxS2_ff0)
    x, ctx_2048, mask_BxS2_ik0, mask_Bx1xSxS2_ff0 = _rec_inputs()

    def _L0_xattn_setup():
        import jax, jax.numpy as jnp
        import numpy as np
        EPS = 1e-05

        def _inorm(x):
            m = jnp.mean(x, axis=-1, keepdims=True)
            v = jnp.var(x, axis=-1, keepdims=True)
            return (x - m) * jax.lax.rsqrt(v + EPS)

        def _conv1x1(W, b, x):
            return jnp.einsum('oc,bct->bot', W, x) + b[None, :, None]
        key = jax.random.key(seed)
        ks = jax.random.split(key, 10)
        B, C, T = (4, 64, 256)
        s = 1.0 / np.sqrt(C)
        return {'x_c': jax.random.normal(ks[0], (B, C, T), jnp.float32), 'x_s': jax.random.normal(ks[1], (B, C, T), jnp.float32), 'Wn': jax.random.normal(ks[2], (C, C), jnp.float32) * s, 'bn': jax.random.normal(ks[3], (C,), jnp.float32) * s, 'Wm': jax.random.normal(ks[4], (C, C), jnp.float32) * s, 'bm': jax.random.normal(ks[5], (C,), jnp.float32) * s, 'Wl': jax.random.normal(ks[6], (C, C), jnp.float32) * s, 'bl': jax.random.normal(ks[7], (C,), jnp.float32) * s, 'Wo': jax.random.normal(ks[8], (C, C), jnp.float32) * s, 'bo': jax.random.normal(ks[9], (C,), jnp.float32) * s}
    _L0_xattn_all = _L0_xattn_setup()
    _L0_xattn_in = {k: v for k, v in _L0_xattn_all.items() if k in ('Wn', 'bn', 'Wm', 'bm', 'Wl', 'bl', 'Wo', 'bo')}
    del _L0_xattn_all

    def _L1_xattn_setup():
        import jax, jax.numpy as jnp
        import numpy as np
        H = 256
        B, L, S = (4, 512, 10)
        key = jax.random.key(seed)
        k1, k2, k3, k4, k5, k6 = jax.random.split(key, 6)
        scale = 1.0 / np.sqrt(H)
        return {'h_english': jax.random.normal(k1, (B, L, H), dtype=jnp.float32), 'h_lojban': jax.random.normal(k2, (B, S, H), dtype=jnp.float32), 'w_q': jax.random.normal(k3, (H, H), dtype=jnp.float32) * scale, 'w_k': jax.random.normal(k4, (H, H), dtype=jnp.float32) * scale, 'w_v': jax.random.normal(k5, (H, H), dtype=jnp.float32) * scale, 'w_o': jax.random.normal(k6, (H, H), dtype=jnp.float32) * scale, 'alpha': jnp.float32(0.1)}
    _L1_xattn_all = _L1_xattn_setup()
    _L1_xattn_in = {k: v for k, v in _L1_xattn_all.items() if k in ('w_q', 'w_k', 'w_v', 'w_o', 'alpha')}
    del _L1_xattn_all

    def _L2_xattn_setup():
        import jax, jax.numpy as jnp
        import numpy as np
        B, P, K, H, NH = (4, 256, 32, 256, 16)
        DH = H // NH
        EPS = 1e-06

        def rmsnorm(x, w):
            var = jnp.mean(jnp.square(x), axis=-1, keepdims=True)
            return x * jax.lax.rsqrt(var + EPS) * w
        key = jax.random.key(seed)
        ks = jax.random.split(key, 12)
        s = 0.02
        return {'x': jax.random.normal(ks[0], (B, P, H), jnp.float32), 'latents': jax.random.normal(ks[1], (B, K, H), jnp.float32), 'attention_mask': jax.random.randint(ks[2], (B, P), 0, 2, jnp.int32), 'q_w': s * jax.random.normal(ks[3], (H, H), jnp.float32), 'q_b': jnp.zeros((H,), jnp.float32), 'kv_w': s * jax.random.normal(ks[4], (H, 2 * H), jnp.float32), 'kv_b': jnp.zeros((2 * H,), jnp.float32), 'out_w': s * jax.random.normal(ks[5], (H, H), jnp.float32), 'out_b': jnp.zeros((H,), jnp.float32), 'postnorm_w': jnp.ones((H,), jnp.float32), 'mlp_w1': s * jax.random.normal(ks[6], (H, 4 * H), jnp.float32), 'mlp_b1': jnp.zeros((4 * H,), jnp.float32), 'mlp_w2': s * jax.random.normal(ks[7], (4 * H, H), jnp.float32), 'mlp_b2': jnp.zeros((H,), jnp.float32)}
    _L2_xattn_all = _L2_xattn_setup()
    _L2_xattn_in = {k: v for k, v in _L2_xattn_all.items() if k in ('q_w', 'q_b', 'kv_w', 'kv_b', 'out_w', 'out_b', 'postnorm_w', 'mlp_w1', 'mlp_b1', 'mlp_w2', 'mlp_b2')}
    del _L2_xattn_all

    def _L3_xattn_setup():
        import jax, jax.numpy as jnp
        import numpy as np
        H = 256
        NH = 32
        KVH = 8
        HD = H // NH
        GROUPS = NH // KVH
        EPS = 1e-06
        B, L, S = (4, 128, 128)

        def _gqa_forward(hidden_state, encoder_hidden_state, encoder_attention_mask, Wq, bq, Wk, bk, Wv, bv, Wo, bo, gamma, beta):
            b, l, _ = hidden_state.shape
            s = encoder_hidden_state.shape[1]
            q = hidden_state @ Wq + bq
            k = encoder_hidden_state @ Wk + bk
            v = encoder_hidden_state @ Wv + bv
            q = q.reshape(b, l, KVH, GROUPS, HD).transpose(0, 2, 3, 1, 4)
            k = k.reshape(b, s, KVH, HD).transpose(0, 2, 1, 3)
            v = v.reshape(b, s, KVH, HD).transpose(0, 2, 1, 3)
            scale = 1.0 / jnp.sqrt(jnp.asarray(HD, q.dtype))
            scores = jnp.einsum('bkgld,bksd->bkgls', q, k) * scale
            scores = scores + encoder_attention_mask[:, :, None, :, :]
            attn = jax.nn.softmax(scores, axis=-1)
            out = jnp.einsum('bkgls,bksd->bkgld', attn, v)
            out = out.transpose(0, 3, 1, 2, 4).reshape(b, l, H)
            out = out @ Wo + bo
            x = out + hidden_state
            mu = jnp.mean(x, axis=-1, keepdims=True)
            var = jnp.var(x, axis=-1, keepdims=True)
            return (x - mu) * jax.lax.rsqrt(var + EPS) * gamma + beta
        key = jax.random.key(seed)
        ks = jax.random.split(key, 12)
        sd = 0.02
        return {'hidden_state': jax.random.normal(ks[0], (B, L, H), jnp.float32), 'encoder_hidden_state': jax.random.normal(ks[1], (B, S, H), jnp.float32), 'encoder_attention_mask': jnp.zeros((B, 1, L, S), jnp.float32), 'Wq': jax.random.normal(ks[2], (H, H), jnp.float32) * sd, 'bq': jnp.zeros((H,), jnp.float32), 'Wk': jax.random.normal(ks[3], (H, KVH * HD), jnp.float32) * sd, 'bk': jnp.zeros((KVH * HD,), jnp.float32), 'Wv': jax.random.normal(ks[4], (H, KVH * HD), jnp.float32) * sd, 'bv': jnp.zeros((KVH * HD,), jnp.float32), 'Wo': jax.random.normal(ks[5], (H, H), jnp.float32) * sd, 'bo': jnp.zeros((H,), jnp.float32), 'gamma': jnp.ones((H,), jnp.float32), 'beta': jnp.zeros((H,), jnp.float32)}
    _L3_xattn_all = _L3_xattn_setup()
    _L3_xattn_in = {k: v for k, v in _L3_xattn_all.items() if k in ('Wq', 'bq', 'Wk', 'bk', 'Wv', 'bv', 'Wo', 'bo', 'gamma', 'beta')}
    del _L3_xattn_all
    return {'x': x, 'ctx_2048': ctx_2048, 'mask_BxS2_ik0': mask_BxS2_ik0, 'mask_Bx1xSxS2_ff0': mask_Bx1xSxS2_ff0, 'L0_xattn_Wn': _L0_xattn_in['Wn'], 'L0_xattn_bn': _L0_xattn_in['bn'], 'L0_xattn_Wm': _L0_xattn_in['Wm'], 'L0_xattn_bm': _L0_xattn_in['bm'], 'L0_xattn_Wl': _L0_xattn_in['Wl'], 'L0_xattn_bl': _L0_xattn_in['bl'], 'L0_xattn_Wo': _L0_xattn_in['Wo'], 'L0_xattn_bo': _L0_xattn_in['bo'], 'L1_xattn_w_q': _L1_xattn_in['w_q'], 'L1_xattn_w_k': _L1_xattn_in['w_k'], 'L1_xattn_w_v': _L1_xattn_in['w_v'], 'L1_xattn_w_o': _L1_xattn_in['w_o'], 'L1_xattn_alpha': _L1_xattn_in['alpha'], 'L2_xattn_q_w': _L2_xattn_in['q_w'], 'L2_xattn_q_b': _L2_xattn_in['q_b'], 'L2_xattn_kv_w': _L2_xattn_in['kv_w'], 'L2_xattn_kv_b': _L2_xattn_in['kv_b'], 'L2_xattn_out_w': _L2_xattn_in['out_w'], 'L2_xattn_out_b': _L2_xattn_in['out_b'], 'L2_xattn_postnorm_w': _L2_xattn_in['postnorm_w'], 'L2_xattn_mlp_w1': _L2_xattn_in['mlp_w1'], 'L2_xattn_mlp_b1': _L2_xattn_in['mlp_b1'], 'L2_xattn_mlp_w2': _L2_xattn_in['mlp_w2'], 'L2_xattn_mlp_b2': _L2_xattn_in['mlp_b2'], 'L3_xattn_Wq': _L3_xattn_in['Wq'], 'L3_xattn_bq': _L3_xattn_in['bq'], 'L3_xattn_Wk': _L3_xattn_in['Wk'], 'L3_xattn_bk': _L3_xattn_in['bk'], 'L3_xattn_Wv': _L3_xattn_in['Wv'], 'L3_xattn_bv': _L3_xattn_in['bv'], 'L3_xattn_Wo': _L3_xattn_in['Wo'], 'L3_xattn_bo': _L3_xattn_in['bo'], 'L3_xattn_gamma': _L3_xattn_in['gamma'], 'L3_xattn_beta': _L3_xattn_in['beta']}

def reference(x, ctx_2048, mask_BxS2_ik0, mask_Bx1xSxS2_ff0, L0_xattn_Wn, L0_xattn_bn, L0_xattn_Wm, L0_xattn_bm, L0_xattn_Wl, L0_xattn_bl, L0_xattn_Wo, L0_xattn_bo, L1_xattn_w_q, L1_xattn_w_k, L1_xattn_w_v, L1_xattn_w_o, L1_xattn_alpha, L2_xattn_q_w, L2_xattn_q_b, L2_xattn_kv_w, L2_xattn_kv_b, L2_xattn_out_w, L2_xattn_out_b, L2_xattn_postnorm_w, L2_xattn_mlp_w1, L2_xattn_mlp_b1, L2_xattn_mlp_w2, L2_xattn_mlp_b2, L3_xattn_Wq, L3_xattn_bq, L3_xattn_Wk, L3_xattn_bk, L3_xattn_Wv, L3_xattn_bv, L3_xattn_Wo, L3_xattn_bo, L3_xattn_gamma, L3_xattn_beta):
    import jax
    import jax.numpy as jnp

    def _L0_xattn_ref(x_c, x_s, Wn, bn, Wm, bm, Wl, bl, Wo, bo):
        import jax, jax.numpy as jnp
        import numpy as np
        EPS = 1e-05

        def _inorm(x):
            m = jnp.mean(x, axis=-1, keepdims=True)
            v = jnp.var(x, axis=-1, keepdims=True)
            return (x - m) * jax.lax.rsqrt(v + EPS)

        def _conv1x1(W, b, x):
            return jnp.einsum('oc,bct->bot', W, x) + b[None, :, None]
        Mn = _conv1x1(Wn, bn, _inorm(x_c))
        Mm = _conv1x1(Wm, bm, _inorm(x_s))
        A = jax.nn.softmax(jnp.einsum('bct,bcs->bts', Mn, Mm), axis=-1)
        Ml = _conv1x1(Wl, bl, x_s)
        Mo = jnp.einsum('bcs,bts->bct', Ml, A)
        return _conv1x1(Wo, bo, Mo) + x_c

    def _L1_xattn_ref(h_english, h_lojban, w_q, w_k, w_v, w_o, alpha):
        import jax, jax.numpy as jnp
        import numpy as np
        H = 256
        B, L, S = (4, 512, 10)
        h = h_english.shape[-1]
        q = jnp.einsum('blh,oh->blo', h_english, w_q)
        k = jnp.einsum('bsh,oh->bso', h_lojban, w_k)
        v = jnp.einsum('bsh,oh->bso', h_lojban, w_v)
        scores = jnp.einsum('blh,bsh->bls', q, k) / jnp.sqrt(jnp.float32(h))
        probs = jax.nn.softmax(scores, axis=-1)
        context = jnp.einsum('bls,bsh->blh', probs, v)
        delta = jnp.einsum('blh,oh->blo', context, w_o)
        return h_english + alpha * delta

    def _L2_xattn_ref(x, latents, attention_mask, q_w, q_b, kv_w, kv_b, out_w, out_b, postnorm_w, mlp_w1, mlp_b1, mlp_w2, mlp_b2):
        import jax, jax.numpy as jnp
        import numpy as np
        B, P, K, H, NH = (4, 256, 32, 256, 16)
        DH = H // NH
        EPS = 1e-06

        def rmsnorm(x, w):
            var = jnp.mean(jnp.square(x), axis=-1, keepdims=True)
            return x * jax.lax.rsqrt(var + EPS) * w
        b, p, _ = x.shape
        k_len = latents.shape[1]
        residual = latents
        h = jnp.concatenate([x, latents], axis=1)
        q = (latents @ q_w + q_b).reshape(b, k_len, NH, DH)
        kv = (h @ kv_w + kv_b).reshape(b, p + k_len, NH, DH, 2)
        kmat, v = (kv[..., 0], kv[..., 1])
        attn = jnp.einsum('bkhd,bnhd->bhkn', q, kmat) / DH
        full_mask = jnp.concatenate([attention_mask.astype(bool), jnp.ones((b, k_len), bool)], axis=-1)
        attn = jnp.where(full_mask[:, None, None, :], attn, -jnp.inf)
        attn = jax.nn.softmax(attn.astype(jnp.float32), axis=-1).astype(q.dtype)
        attn_out = jnp.einsum('bhkn,bnhd->bkhd', attn, v).reshape(b, k_len, H)
        attn_out = attn_out @ out_w + out_b + residual
        out = rmsnorm(attn_out, postnorm_w)
        out = jax.nn.gelu(out @ mlp_w1 + mlp_b1) @ mlp_w2 + mlp_b2
        return out + residual

    def _L3_xattn_ref(hidden_state, encoder_hidden_state, encoder_attention_mask, Wq, bq, Wk, bk, Wv, bv, Wo, bo, gamma, beta):
        import jax, jax.numpy as jnp
        import numpy as np
        H = 256
        NH = 32
        KVH = 8
        HD = H // NH
        GROUPS = NH // KVH
        EPS = 1e-06
        B, L, S = (4, 128, 128)

        def _gqa_forward(hidden_state, encoder_hidden_state, encoder_attention_mask, Wq, bq, Wk, bk, Wv, bv, Wo, bo, gamma, beta):
            b, l, _ = hidden_state.shape
            s = encoder_hidden_state.shape[1]
            q = hidden_state @ Wq + bq
            k = encoder_hidden_state @ Wk + bk
            v = encoder_hidden_state @ Wv + bv
            q = q.reshape(b, l, KVH, GROUPS, HD).transpose(0, 2, 3, 1, 4)
            k = k.reshape(b, s, KVH, HD).transpose(0, 2, 1, 3)
            v = v.reshape(b, s, KVH, HD).transpose(0, 2, 1, 3)
            scale = 1.0 / jnp.sqrt(jnp.asarray(HD, q.dtype))
            scores = jnp.einsum('bkgld,bksd->bkgls', q, k) * scale
            scores = scores + encoder_attention_mask[:, :, None, :, :]
            attn = jax.nn.softmax(scores, axis=-1)
            out = jnp.einsum('bkgls,bksd->bkgld', attn, v)
            out = out.transpose(0, 3, 1, 2, 4).reshape(b, l, H)
            out = out @ Wo + bo
            x = out + hidden_state
            mu = jnp.mean(x, axis=-1, keepdims=True)
            var = jnp.var(x, axis=-1, keepdims=True)
            return (x - mu) * jax.lax.rsqrt(var + EPS) * gamma + beta
        return _gqa_forward(hidden_state, encoder_hidden_state, encoder_attention_mask, Wq, bq, Wk, bk, Wv, bv, Wo, bo, gamma, beta)
    x = _L0_xattn_ref(x, ctx_2048, L0_xattn_Wn, L0_xattn_bn, L0_xattn_Wm, L0_xattn_bm, L0_xattn_Wl, L0_xattn_bl, L0_xattn_Wo, L0_xattn_bo)
    x = _L1_xattn_ref(x, ctx_2048, L1_xattn_w_q, L1_xattn_w_k, L1_xattn_w_v, L1_xattn_w_o, L1_xattn_alpha)
    x = _L2_xattn_ref(ctx_2048, x, mask_BxS2_ik0, L2_xattn_q_w, L2_xattn_q_b, L2_xattn_kv_w, L2_xattn_kv_b, L2_xattn_out_w, L2_xattn_out_b, L2_xattn_postnorm_w, L2_xattn_mlp_w1, L2_xattn_mlp_b1, L2_xattn_mlp_w2, L2_xattn_mlp_b2)
    x = _L3_xattn_ref(x, ctx_2048, mask_Bx1xSxS2_ff0, L3_xattn_Wq, L3_xattn_bq, L3_xattn_Wk, L3_xattn_bk, L3_xattn_Wv, L3_xattn_bv, L3_xattn_Wo, L3_xattn_bo, L3_xattn_gamma, L3_xattn_beta)
    return x

_drawn_inputs = setup_inputs


def setup_inputs(seed=0):
    import zlib

    import numpy as np

    out = dict(_drawn_inputs(seed))
    spreads = {'L2_xattn_q_b': (0.0, 0.8),
     'L2_xattn_kv_b': (0.0, 2.0),
     'L2_xattn_out_b': (0.0, 2.0),
     'L2_xattn_postnorm_w': (1.0, 0.6),
     'L2_xattn_mlp_b1': (0.0, 0.321),
     'L2_xattn_mlp_b2': (0.0, 0.1),
     'L3_xattn_bq': (0.0, 2.0),
     'L3_xattn_bk': (0.0, 2.0),
     'L3_xattn_bv': (0.0, 0.391),
     'L3_xattn_bo': (0.0, 0.1),
     'L3_xattn_gamma': (1.0, 0.2),
     'L3_xattn_beta': (0.0, 0.1)}
    factors = {'L0_xattn_bm': 64.0,
     'L0_xattn_bl': 7.812,
     'L0_xattn_bo': 6.811,
     'L2_xattn_q_w': 8.0,
     'L2_xattn_kv_w': 8.0,
     'L2_xattn_out_w': 8.0,
     'L3_xattn_Wq': 8.0,
     'L3_xattn_Wk': 8.0}
    for name, (base, spread) in spreads.items():
        noise = np.random.default_rng([zlib.crc32(name.encode()), seed]).standard_normal(out[name].shape)
        drawn = base * np.exp(spread * noise) if base else spread * noise
        out[name] = jnp.asarray(drawn.astype(out[name].dtype))
    for name, factor in factors.items():
        out[name] = (out[name] * factor).astype(out[name].dtype)
    return out
```

```python
from contextlib import ExitStack

import concourse.bass as bass
from concourse import mybir

F32 = mybir.dt.float32
I32 = mybir.dt.int32
ALU = mybir.AluOpType
ACT = mybir.ActivationFunctionType
AX = mybir.AxisListType

P = 128
B, S, H = 16, 64, 256
KT = H // P
SLOTS = 2
TILES = B * S // P
TRIPS = TILES // SLOTS
BT = P // S
L2_HEADS, L2_D = 16, 16
L2_KEYS = 2 * S
FF = 4 * H
FT = FF // P
KVH, GROUPS, L3_D = 8, 4, 8
L0_EPS, RMS_EPS, LN_EPS = 1e-5, 1e-6, 1e-6
MASKED = -1e30
QUARTERS = 4


def await_unit(engine, signals, i, k, units):
    n = len(signals)
    engine.wait_ge(signals[k % n], units // n * i + (k // n + 1))


def spread(ap, axis, n):
    shape = list(ap.shape)
    return ap.unsqueeze(axis).broadcast_to(shape[:axis] + [n] + shape[axis:])


def build(nc, a, out, dump=None):
    ctx = ExitStack()
    with ctx:
        phase_memory = [ctx.enter_context(ExitStack())]
        phase_sems = []

        def sb(name, shape, dt=F32):
            return ctx.enter_context(nc.sbuf_tensor(name, shape, dt))

        def tb(name, shape):
            return phase_memory[0].enter_context(nc.sbuf_tensor(name, shape, F32))

        def next_phase():
            phase_memory[0].close()
            phase_memory[0] = ctx.enter_context(ExitStack())
            nc.clear_and_free_semaphores(list(phase_sems))
            phase_sems.clear()
            nc.all_engine_barrier()

        def sem(name):
            phase_sems.append(nc.alloc_semaphore(name=name))
            return phase_sems[-1]

        def sems(name, n):
            return [sem(f"{name}{k}") for k in range(n)]

        bank = [ctx.enter_context(nc.psum_tensor(f"bank{k}", [P, 512], F32)) for k in range(8)]

        ident = sb("ident", [P, P])
        quarter_mask = sb("quarter_mask", [P, QUARTERS])
        rsqrt_power = sb("rsqrt_power", [P, 2])
        l0_eps = sb("l0_eps", [P, 2])
        l2_eps = sb("l2_eps", [P, 1])
        l3_eps = sb("l3_eps", [P, 1])
        scratch = sb("scratch", [P, 1])
        kvh_mask = sb("kvh_mask", [P, KVH])
        l0_wn = sb("l0_wn", [P, P])
        l0_wm = sb("l0_wm", [P, P])
        l0_bn = sb("l0_bn", [P, 1])
        l0_bm = sb("l0_bm", [P, 1])
        l0_wl2 = sb("l0_wl2", [S, P])
        l0_woT = sb("l0_woT", [S, S])
        l0_bl = sb("l0_bl", [S, 1])
        l0_bo = sb("l0_bo", [P, S])
        l0_wol = sb("l0_wol", [P, P])
        l0_bias = sb("l0_bias", [P, S])
        l1_wk = sb("l1_wk", [P, KT, H])
        l1_wq = sb("l1_wq", [P, KT, H])
        l1_wv = sb("l1_wv", [P, KT, H])
        l1_woT = sb("l1_woT", [P, KT, H])
        l1_kq = sb("l1_kq", [P, KT, H])
        l1_vo = sb("l1_vo", [P, KT, H])
        l1_alpha = sb("l1_alpha", [P, 1])
        l2_qw = sb("l2_qw", [P, KT, H])
        l2_kw = sb("l2_kw", [P, KT, H])
        l2_vw = sb("l2_vw", [P, KT, H])
        l2_ow = sb("l2_ow", [P, KT, H])
        l2_qb = sb("l2_qb", [P, KT])
        l2_kb = sb("l2_kb", [P, KT])
        l2_pw = sb("l2_pw", [P, KT])
        l2_vb = sb("l2_vb", [P, H])
        l2_ob = sb("l2_ob", [P, H])
        mlp_w1 = sb("mlp_w1", [P, KT, FF])
        mlp_b1 = sb("mlp_b1", [P, FT])
        mlp_w2 = sb("mlp_w2", [P, FT, H])
        mlp_b2 = sb("mlp_b2", [P, H])
        l3_wq = sb("l3_wq", [P, KT, H])
        l3_bq = sb("l3_bq", [P, KT])
        l3_wk = sb("l3_wk", [P, KT, P])
        l3_bk = sb("l3_bk", [P, 1])
        l3_wv = sb("l3_wv", [P, KT, S])
        l3_bv = sb("l3_bv", [P, S])
        l3_wo = sb("l3_wo", [P, KT, H])
        l3_bo = sb("l3_bo", [P, H])
        l3_gamma = sb("l3_gamma", [P, H])
        l3_beta = sb("l3_beta", [P, H])
        key_flags = sb("key_flags", [P, B, S], I32)
        key_bias = sb("key_bias", [P, B, L2_KEYS])
        ff_mask = sb("ff_mask", [P, B, S])

        UNITS = SLOTS * BT * KT
        UT = BT * KT
        qz = sb("qz", [P, SLOTS, KT, BT, 2, S])
        sc = sb("sc", [P, UT, QUARTERS, P])
        pT = sb("pT", [P, UT, QUARTERS, P])
        nmax = sb("nmax", [P, UT, KVH])
        rsum = sb("rsum", [P, SLOTS, 2 * L2_HEADS])
        att = sb("att", [P, SLOTS, H])
        attT = sb("attT", [P, SLOTS, KT, P])
        res = sb("res", [P, SLOTS, H])

        hT = sb("hT", [P, TILES, KT, BT, 2, S])
        k3T = sb("k3T", [P, TILES, BT, S])
        v3 = sb("v3", [P, B, QUARTERS, 2, L3_D + 1])
        x2tok = sb("x2tok", [P, TILES, H])
        x3tok = sb("x3tok", [P, TILES, H])
        yT = sb("yT", [P, KT, TILES * P])

        loads = [
            (ident[:, :], a["ident"]), (l0_wl2[:, :], a["l0_wl2"]), (l0_woT[:, :], a["l0_woT"]),
            (l0_bl[:, :], a["l0_bl"]), (l0_bn[:, :], a["l0_bn"]), (l0_bm[:, :], a["l0_bm"]),
            (l0_bo[:, :], a["l0_bo"].partition_broadcast(P)),
            (l1_wk[:, :, :], a["l1_wk"].rearrange("(k p) n -> p k n", p=P)),
            (l1_wq[:, :, :], a["l1_wq"].rearrange("(k p) n -> p k n", p=P)),
            (l1_wv[:, :, :], a["l1_wv"].rearrange("(k p) n -> p k n", p=P)),
            (l1_woT[:, :, :], a["l1_woT"].rearrange("(k p) n -> p k n", p=P)),
            (l1_alpha[:, :], a["l1_alpha"].partition_broadcast(P)),
        ]
        late_loads = [
            (quarter_mask[:, :], a["quarter_mask"]), (kvh_mask[:, :], a["kvh_mask"]),
            (l2_qb[:, :], a["l2_qb"]), (l2_kb[:, :], a["l2_kb"]), (l2_pw[:, :], a["l2_pw"]),
            (mlp_b1[:, :], a["mlp_b1"]), (l3_bq[:, :], a["l3_bq"]), (l3_bk[:, :], a["l3_bk"]),
            (l3_wk[:, :, :], a["l3_wk"].rearrange("(k p) n -> p k n", p=P)),
            (l3_wv[:, :, :], a["l3_wv"].rearrange("(k p) n -> p k n", p=P)),
            (l3_bv[:, :], a["l3_bv"].partition_broadcast(P)),
            (l2_qw[:, :, :], a["l2_qw"].rearrange("(k p) n -> p k n", p=P)),
            (l2_kw[:, :, :], a["l2_kw"].rearrange("(k p) n -> p k n", p=P)),
            (l2_vw[:, :, :], a["l2_vw"].rearrange("(k p) n -> p k n", p=P)),
            (l2_ow[:, :, :], a["l2_ow"].rearrange("(k p) n -> p k n", p=P)),
            (l2_vb[:, :], a["l2_vb"].partition_broadcast(P)), (l2_ob[:, :], a["l2_ob"].partition_broadcast(P)),
            (mlp_w1[:, :, :], a["mlp_w1"].rearrange("(k p) n -> p k n", p=P)),
            (mlp_w2[:, :, :], a["mlp_w2"].rearrange("(k p) n -> p k n", p=P)),
            (mlp_b2[:, :], a["mlp_b2"].partition_broadcast(P)),
            (l3_wq[:, :, :], a["l3_wq"].rearrange("(k p) n -> p k n", p=P)),
            (l3_wo[:, :, :], a["l3_wo"].rearrange("(k p) n -> p k n", p=P)),
            (l3_bo[:, :], a["l3_bo"].partition_broadcast(P)),
            (l3_gamma[:, :], a["l3_gamma"].partition_broadcast(P)),
            (l3_beta[:, :], a["l3_beta"].partition_broadcast(P)),
            (ff_mask[0:S, :, :], a["ff_mask"].rearrange("b q s -> q b s")),
            (ff_mask[S:P, :, :], a["ff_mask"].rearrange("b q s -> q b s")),
            (key_flags[:, :, :], a["key_flags"].partition_broadcast(P)),
        ]
        early_in = sem("early_in")
        blocks_in = sem("blocks_in")
        late_in = sem("late_in")
        blocks_zeroed = sem("blocks_zeroed")
        zeroed = sem("zeroed")
        w_made = sem("w_made")
        w_kept = sem("w_kept")
        consts_made = sem("consts_made")

        with nc.Block() as block:
            @block.sync
            def _(sp):
                for dst, src in loads:
                    sp.dma_start(dst, src).then_inc(early_in, 16)
                sp.wait_ge(blocks_zeroed, 2)
                for w, name in ((l0_wn, "l0_wnT"), (l0_wm, "l0_wmT")):
                    for b in range(BT):
                        sp.dma_start(w[b * S:(b + 1) * S, b * S:(b + 1) * S], a[name]).then_inc(blocks_in, 16)
                sp.wait_ge(blocks_in, 4 * 16)

            @block.gpsimd
            def _(pool):
                nc.gpsimd.memset(rsqrt_power[:, :], -0.5).then_inc(consts_made, 1)
                nc.gpsimd.memset(l0_eps[:, :], L0_EPS).then_inc(consts_made, 1)
                nc.gpsimd.memset(l2_eps[:, :], H * RMS_EPS).then_inc(consts_made, 1)
                nc.gpsimd.memset(l3_eps[:, :], LN_EPS).then_inc(consts_made, 1)
                nc.gpsimd.memset(l0_wn[:, :], 0.0).then_inc(blocks_zeroed, 1)
                nc.gpsimd.memset(l0_wm[:, :], 0.0).then_inc(blocks_zeroed, 1)
                for dst, src in late_loads:
                    pool.dma_start(dst, src).then_inc(late_in, 16)

            @block.tensor
            def _(pe):
                pe.wait_ge(early_in, 16 * len(loads))
                nc.tensor.matmul(bank[0][:, 0:S], l0_wl2[:, :], l0_woT[:, :], start=True, stop=True).then_inc(w_made, 1)
                nc.tensor.matmul(bank[1][:, 0:S], l0_bl[:, 0:1].broadcast_to([S, P]), l0_woT[:, :],
                                 start=True, stop=True).then_inc(w_made, 1)
                for n, (w, v) in enumerate(((l1_wk, l1_wq), (l1_wv, l1_woT))):
                    for m in range(KT):
                        for k in range(KT):
                            last = nc.tensor.matmul(bank[2 + n][:, m * H:(m + 1) * H], w[:, k, m * P:(m + 1) * P],
                                                    v[:, k, :], start=(k == 0), stop=(k == KT - 1))
                    last.then_inc(w_made, 1)

            @block.scalar
            def _(act):
                act.wait_ge(w_made, 3)
                nc.scalar.mul(l1_kq[:, :, :], bank[2][:, :].rearrange("p (k n) -> p k n", k=KT), 1.0 / 16).then_inc(w_kept, 1)
                act.wait_ge(w_made, 4)
                nc.scalar.copy(l1_vo[:, :, :], bank[3][:, :].rearrange("p (k n) -> p k n", k=KT)).then_inc(w_kept, 1)
                act.wait_ge(late_in, 16 * len(late_loads))
                nc.scalar.mul(l2_qb[:, :], l2_qb[:, :], 1.0 / L2_D).then_inc(consts_made, 1)
                nc.scalar.mul(l3_bq[:, :], l3_bq[:, :], L3_D ** -0.5).then_inc(consts_made, 1)

            @block.vector
            def _(dve):
                nc.vector.memset(l0_wol[:, :], 0.0).then_inc(zeroed, 1)
                nc.vector.memset(key_bias[:, :, :], 0.0).then_inc(zeroed, 1)
                nc.vector.memset(v3[:, :, :, :, :], 0.0).then_inc(zeroed, 1)
                dve.wait_ge(zeroed, 3)
                for b in range(BT):
                    nc.vector.memset(v3[b * S:(b + 1) * S, :, :, b, L3_D:L3_D + 1], 1.0).then_inc(consts_made, 1)
                dve.wait_ge(w_made, 1)
                for b in range(BT):
                    nc.vector.tensor_copy(l0_wol[b * S:(b + 1) * S, b * S:(b + 1) * S],
                                          bank[0][b * S:(b + 1) * S, 0:S]).then_inc(w_kept, 1)
                dve.wait_ge(w_made, 2)
                nc.vector.tensor_tensor(l0_bias[:, :], bank[1][:, 0:S], l0_bo[:, :], ALU.add).then_inc(w_kept, 1)
                dve.wait_ge(late_in, 16 * len(late_loads))
                nc.vector.tensor_scalar(key_bias[:, :, 0:S], key_flags[:, :, :], 0, MASKED,
                                        ALU.is_equal, ALU.mult).then_inc(consts_made, 1)

        UNITS0 = SLOTS * BT
        x_ring = tb("x_ring", [P, SLOTS, H])
        c_ring = tb("c_ring", [P, SLOTS, H])
        stats = tb("stats", [P, SLOTS, 2, 6])
        moments = tb("moments", [P, SLOTS, 2, 2])
        rstd = tb("rstd", [P, SLOTS, 2])
        normed = tb("normed", [P, SLOTS, 2, H])
        xT0 = tb("xT0", [P, SLOTS, KT, BT, S])
        mn = tb("mn", [P, SLOTS, BT, H])
        mm = tb("mm", [P, SLOTS, H])
        vp0 = tb("vp0", [P, SLOTS, KT, BT, S])
        p0 = tb("p0", [P, UNITS0, KT, H])
        p0T = tb("p0T", [P, UNITS0, KT, H])
        nmax0 = tb("nmax0", [P, UNITS0, KT])
        sum0 = tb("sum0", [P, UNITS0, KT])
        rsum0 = tb("rsum0", [P, UNITS0, KT])

        x_in, c_in = sems("x_in", SLOTS), sems("c_in", SLOTS)
        zero0 = sem("zero0")
        with_eps = sems("with_eps_l0_", SLOTS)
        moments_made, rstd_made = sems("moments_made", SLOTS), sems("rstd_made", SLOTS)
        normed_made = sems("normed_made", SLOTS)
        xT_made, cT_made = sems("xT_made", SLOTS), sems("cT_made", SLOTS)
        xT_kept, cT_kept = sems("xT_kept", SLOTS), sems("cT_kept", SLOTS)
        vp_made, vp_kept = sems("vp_made", SLOTS), sems("vp_kept", SLOTS)
        m_made, m_kept = sems("m_made", SLOTS), sems("m_kept", SLOTS)
        s0_made, max0_made, p0_made = sems("s0_made", UNITS0), sems("max0_made", UNITS0), sems("p0_made", UNITS0)
        p0T_made, p0T_kept = sems("p0T_made", UNITS0), sems("p0T_kept", UNITS0)
        o0_made, o0_kept = sems("o0_made", UNITS0), sems("o0_kept", UNITS0)
        chain0 = sem("chain0")
        CHAIN0 = SLOTS + UNITS0

        b_m, b_xT, b_cT, b_vp, b_p0T, b_o0 = (bank[k] for k in (0, 1, 2, 3, 6, 7))
        b_s0 = (bank[4], bank[5])

        with nc.Block() as block:
            @block.sync
            def _(sp):
                with sp.Fori(0, TRIPS) as i:
                    for u in range(SLOTS):
                        n = SLOTS * i + u
                        sp.wait_ge(normed_made[u], 2 * i)
                        sp.wait_ge(xT_made[u], i)
                        sp.wait_ge(cT_made[u], i)
                        sp.wait_ge(vp_made[u], i)
                        sp.dma_start(x_ring[:, u, :], a["x"][n, :, :]).then_inc(x_in[u], 16)
                        sp.dma_start(c_ring[:, u, :], a["ctx"][n, :, :]).then_inc(c_in[u], 16)

            @block.gpsimd
            def _(pool):
                nc.gpsimd.memset(mn[:, :, :, :], 0.0).then_inc(zero0, 1)
                with pool.Fori(0, TRIPS) as i:
                    for u in range(SLOTS):
                        pool.wait_ge(moments_made[u], i + 1)
                        nc.gpsimd.tensor_tensor(rstd[:, u, :], moments[:, u, :, 1], l0_eps[:, :], ALU.add).then_inc(with_eps[u], 1)
                        pool.wait_ge(with_eps[u], i + 1)
                        nc.gpsimd.tensor_tensor(rstd[:, u, :], rstd[:, u, :], rsqrt_power[:, :], ALU.pow).then_inc(rstd_made[u], 1)

            @block.tensor
            def _(pe):
                def prepare(i, u):
                    v = 1 - u
                    before = i + 1 if u else i
                    pe.wait_ge(x_in[u], 16 * (i + 1))
                    pe.wait_ge(xT_kept[v], before)
                    for k in range(KT):
                        last = nc.tensor.transpose(b_xT[:, k * P:(k + 1) * P], x_ring[:, u, k * P:(k + 1) * P], ident[:, :])
                    last.then_inc(xT_made[u], 1)
                    pe.wait_ge(c_in[u], 16 * (i + 1))
                    pe.wait_ge(cT_kept[v], before)
                    for k in range(KT):
                        last = nc.tensor.transpose(b_cT[:, k * P:(k + 1) * P], c_ring[:, u, k * P:(k + 1) * P], ident[:, :])
                    last.then_inc(cT_made[u], 1)
                    pe.wait_ge(vp_kept[v], before)
                    for k in range(KT):
                        last = nc.tensor.matmul(b_vp[:, k * P:(k + 1) * P], c_ring[:, u, k * P:(k + 1) * P], l0_wol[:, :],
                                                start=True, stop=True)
                    last.then_inc(vp_made[u], 1)
                    pe.wait_ge(normed_made[u], 2 * (i + 1))
                    pe.wait_ge(m_kept[v], before)
                    nc.tensor.matmul(b_m[:, 0:H], l0_wn[:, :], normed[:, u, 0, :], start=True, stop=True)
                    nc.tensor.matmul(b_m[:, H:2 * H], l0_wm[:, :], normed[:, u, 1, :], start=True, stop=True)\
                        .then_inc(m_made[u], 1)

                def scores(i, k):
                    u, b = k // BT, k % BT
                    pe.wait_ge(m_kept[u], i + 1)
                    pe.wait_ge(p0_made[(k - 2) % UNITS0], i + 1 if k >= 2 else i)
                    for t in range(KT):
                        last = nc.tensor.matmul(b_s0[k % 2][:, t * H:(t + 1) * H], mn[:, u, b, t * P:(t + 1) * P],
                                                mm[:, u, :], start=True, stop=True)
                    last.then_inc(s0_made[k], 1)

                def turn(i, k):
                    pe.wait_ge(p0_made[k], i + 1)
                    pe.wait_ge(p0T_kept[(k - 1) % UNITS0], i + 1 if k >= 1 else i)
                    for s in range(KT):
                        for t in range(KT):
                            last = nc.tensor.transpose(b_p0T[:, s * H + t * P:s * H + (t + 1) * P],
                                                       p0[:, k, t, s * P:(s + 1) * P], ident[:, :])
                    last.then_inc(p0T_made[k], 1)

                def values(i, k):
                    u, b = k // BT, k % BT
                    pe.wait_ge(p0T_kept[k], i + 1)
                    pe.wait_ge(vp_kept[u], i + 1)
                    pe.wait_ge(o0_kept[(k - 1) % UNITS0], i + 1 if k >= 1 else i)
                    for t in range(KT):
                        for s in range(KT):
                            last = nc.tensor.matmul(b_o0[:, t * S:(t + 1) * S], p0T[:, k, s, t * P:(t + 1) * P],
                                                    vp0[:, u, s, b, :], start=(s == 0), stop=(s == KT - 1))
                    last.then_inc(o0_made[k], 1)

                with pe.Fori(0, TRIPS) as i:
                    prepare(i, 0)
                    scores(i, 0)
                    scores(i, 1)
                    prepare(i, 1)
                    turn(i, 0)
                    scores(i, 2)
                    turn(i, 1)
                    values(i, 0)
                    scores(i, 3)
                    values(i, 1)
                    turn(i, 2)
                    turn(i, 3)
                    values(i, 2)
                    values(i, 3)

            @block.scalar
            def _(act):
                act.wait_ge(zero0, 1)

                def prepare(i, u):
                    n = SLOTS * i + u
                    act.wait_ge(cT_made[u], i + 1)
                    nc.scalar.copy(hT[:, n, :, :, 0, :], b_cT[:, 0:H].rearrange("p (k b s) -> p k b s", k=KT, b=BT))\
                        .then_inc(cT_kept[u], 1)
                    act.wait_ge(vp_made[u], i + 1)
                    act.wait_ge(o0_made[BT * u + 1], i)
                    nc.scalar.copy(vp0[:, u, :, :, :], b_vp[:, 0:H].rearrange("p (k b s) -> p k b s", k=KT, b=BT))\
                        .then_inc(vp_kept[u], 1)
                    act.wait_ge(m_made[u], i + 1)
                    act.wait_ge(s0_made[BT * u + 1], i)
                    for b in range(BT):
                        rows = slice(b * S, (b + 1) * S)
                        nc.scalar.activation(mn[rows, u, b, :], b_m[rows, 0:H], ACT.Identity, bias=l0_bn[rows, 0:1])
                    nc.scalar.activation(mm[:, u, :], b_m[:, H:2 * H], ACT.Identity, bias=l0_bm[:, 0:1])\
                        .then_inc(m_kept[u], 1)

                def exps(i, k):
                    act.wait_ge(max0_made[k], i + 1)
                    act.wait_ge(p0T_made[k], i)
                    act.wait_ge(o0_kept[k], i)
                    for t in range(KT):
                        last = nc.scalar.activation(p0[:, k, t, :], b_s0[k % 2][:, t * H:(t + 1) * H], ACT.Exp,
                                                    bias=nmax0[:, k, t:t + 1], accum_out=sum0[:, k, t:t + 1])
                    last.then_inc(p0_made[k], 1)

                with act.Fori(0, TRIPS) as i:
                    prepare(i, 0)
                    exps(i, 0)
                    exps(i, 1)
                    prepare(i, 1)
                    exps(i, 2)
                    exps(i, 3)

            @block.vector
            def _(dve):
                def prepare(i, u):
                    dve.wait_ge(x_in[u], 16 * (i + 1))
                    nc.vector.bn_stats(stats[:, u, 0, :], x_ring[:, u, :])
                    dve.wait_ge(c_in[u], 16 * (i + 1))
                    nc.vector.bn_stats(stats[:, u, 1, :], c_ring[:, u, :]).then_inc(chain0, 1)
                    dve.wait_ge(chain0, CHAIN0 * i + u + 1)
                    nc.vector.memset(scratch[:, :], 0.0)
                    nc.vector.bn_aggr(moments[:, u, 0, :], stats[:, u, 0, :])
                    nc.vector.bn_aggr(moments[:, u, 1, :], stats[:, u, 1, :]).then_inc(moments_made[u], 1)
                    dve.wait_ge(rstd_made[u], i + 1)
                    dve.wait_ge(m_made[u], i)
                    for j, ring in enumerate((x_ring, c_ring)):
                        nc.vector.tensor_scalar(normed[:, u, j, :], ring[:, u, :], moments[:, u, j, 0:1],
                                                rstd[:, u, j:j + 1], ALU.subtract, ALU.mult).then_inc(normed_made[u], 1)
                    dve.wait_ge(xT_made[u], i + 1)
                    nc.vector.tensor_tensor(xT0[:, u, :, :, :].rearrange("p k b s -> p (k b) s"),
                                            b_xT[:, 0:H].rearrange("p (n s) -> p n s", s=S),
                                            spread(l0_bias[:, :], 1, KT * BT), ALU.add).then_inc(xT_kept[u], 1)

                def maxima(i, k):
                    dve.wait_ge(s0_made[k], i + 1)
                    nc.vector.reduce_max(nmax0[:, k, :], b_s0[k % 2][:, :].rearrange("p (t s) -> p t s", t=KT), AX.X,
                                         negate=True).then_inc(max0_made[k], 1)

                def keep_turned(i, k):
                    dve.wait_ge(p0T_made[k], i + 1)
                    dve.wait_ge(o0_made[k], i)
                    nc.vector.tensor_copy(p0T[:, k, :, :].rearrange("p s t -> p (s t)"), b_p0T[:, :]).then_inc(p0T_kept[k], 1)

                def finish(i, k):
                    u, b = k // BT, k % BT
                    dve.wait_ge(p0_made[k], i + 1)
                    nc.vector.reciprocal(rsum0[:, k, :], sum0[:, k, :]).then_inc(chain0, 1)
                    dve.wait_ge(chain0, CHAIN0 * i + SLOTS + k + 1)
                    dve.wait_ge(o0_made[k], i + 1)
                    for t in range(KT):
                        last = nc.vector.scalar_tensor_tensor(
                            out=hT[:, SLOTS * i + u, t, b, 1, :], in0=b_o0[:, t * S:(t + 1) * S],
                            scalar=rsum0[:, k, t:t + 1], in1=xT0[:, u, t, b, :], op0=ALU.mult, op1=ALU.add)
                    last.then_inc(o0_kept[k], 1)

                with dve.Fori(0, TRIPS) as i:
                    prepare(i, 0)
                    maxima(i, 0)
                    maxima(i, 1)
                    prepare(i, 1)
                    keep_turned(i, 0)
                    maxima(i, 2)
                    keep_turned(i, 1)
                    finish(i, 0)
                    maxima(i, 3)
                    finish(i, 1)
                    keep_turned(i, 2)
                    keep_turned(i, 3)
                    finish(i, 2)
                    finish(i, 3)

        next_phase()
        ring1 = tb("ring1", [P, SLOTS, 2, KT, BT, S])
        kp1 = tb("kp1", [P, SLOTS, KT, P])
        vp1 = tb("vp1", [P, SLOTS, H])
        nmax1 = tb("nmax1", [P, SLOTS])
        sum1 = tb("sum1", [P, SLOTS])
        rsum1 = tb("rsum1", [P, SLOTS])
        p1 = tb("p1", [P, SLOTS, P])
        p1T = tb("p1T", [P, SLOTS, P])

        zero1 = sem("zero1")
        ring_in = sems("ring_in", SLOTS)
        kp_made, kp_kept = sems("kp_made", SLOTS), sems("kp_kept", SLOTS)
        vp1_made, vp1_kept = sems("vp1_made", SLOTS), sems("vp1_kept", SLOTS)
        k3_made, k3_kept = sems("k3_made", SLOTS), sems("k3_kept", SLOTS)
        v3_made, v3_kept = sems("v3_made", SLOTS), sems("v3_kept", SLOTS)
        s1_made, max1_made, p1_made = sems("s1_made", SLOTS), sems("max1_made", SLOTS), sems("p1_made", SLOTS)
        p1_scaled, p1T_made, p1T_kept = sems("p1_scaled", SLOTS), sems("p1T_made", SLOTS), sems("p1T_kept", SLOTS)
        d1_made, x2_kept = sems("d1_made", SLOTS), sems("x2_kept", SLOTS)
        chain1 = sem("chain1")

        b_kp, b_vp1, b_k3, b_v3, b_p1T, b_d1 = (bank[k] for k in (0, 1, 2, 3, 6, 7))
        b_s1 = (bank[4], bank[5])

        with nc.Block() as block:
            @block.sync
            def _(sp):
                with sp.Fori(0, TRIPS) as i:
                    for u in range(SLOTS):
                        sp.wait_ge(x2_kept[u], i)
                        sp.wait_ge(s1_made[u], i)
                        sp.wait_ge(v3_made[u], i)
                        for h in range(2):
                            sp.dma_start(ring1[:, u, h, :, :, :], hT[:, SLOTS * i + u, :, :, h, :]).then_inc(ring_in[u], 16)

            @block.gpsimd
            def _(pool):
                nc.gpsimd.memset(p1[:, :, :], 0.0).then_inc(zero1, 1)

            @block.tensor
            def _(pe):
                def project(i, u):
                    v = 1 - u
                    before = i + 1 if u else i
                    pe.wait_ge(ring_in[u], 32 * (i + 1))
                    pe.wait_ge(kp_kept[v], before)
                    for m in range(KT):
                        for k in range(KT):
                            last = nc.tensor.matmul(b_kp[:, m * P:(m + 1) * P], l1_kq[:, k, m * P:(m + 1) * P],
                                                    ring1[:, u, 0, k, :, :], start=(k == 0), stop=(k == KT - 1))
                    last.then_inc(kp_made[u], 1)
                    pe.wait_ge(vp1_kept[v], before)
                    for k in range(KT):
                        last = nc.tensor.matmul(b_vp1[:, 0:H], ring1[:, u, 0, k, :, :], l1_vo[:, k, :],
                                                start=(k == 0), stop=(k == KT - 1))
                    last.then_inc(vp1_made[u], 1)

                def project_l3(i, u):
                    v = 1 - u
                    before = i + 1 if u else i
                    pe.wait_ge(k3_kept[v], before)
                    for k in range(KT):
                        last = nc.tensor.matmul(b_k3[:, 0:P], l3_wk[:, k, :], ring1[:, u, 0, k, :, :],
                                                start=(k == 0), stop=(k == KT - 1))
                    last.then_inc(k3_made[u], 1)
                    pe.wait_ge(v3_kept[v], before)
                    for b in range(BT):
                        for g in range(2):
                            for k in range(KT):
                                last = nc.tensor.matmul(b_v3[g * S:(g + 1) * S, b * S:(b + 1) * S], ring1[:, u, 0, k, b, :],
                                                        l3_wv[:, k, :], start=(k == 0), stop=(k == KT - 1))
                    last.then_inc(v3_made[u], 1)

                def scores(i, u):
                    pe.wait_ge(kp_kept[u], i + 1)
                    pe.wait_ge(p1_made[u], i)
                    for k in range(KT):
                        last = nc.tensor.matmul(b_s1[u][:, 0:P], ring1[:, u, 1, k, :, :], kp1[:, u, k, :],
                                                start=(k == 0), stop=(k == KT - 1))
                    last.then_inc(s1_made[u], 1)

                def turn(i, u):
                    pe.wait_ge(p1_scaled[u], i + 1)
                    pe.wait_ge(p1T_kept[1 - u], i + 1 if u else i)
                    nc.tensor.transpose(b_p1T[:, 0:P], p1[:, u, :], ident[:, :]).then_inc(p1T_made[u], 1)

                def values(i, u):
                    pe.wait_ge(p1T_kept[u], i + 1)
                    pe.wait_ge(vp1_kept[u], i + 1)
                    pe.wait_ge(x2_kept[1 - u], i + 1 if u else i)
                    for m in range(KT):
                        last = nc.tensor.matmul(b_d1[:, m * P:(m + 1) * P], vp1[:, u, m * P:(m + 1) * P], p1T[:, u, :],
                                                start=True, stop=True)
                    last.then_inc(d1_made[u], 1)

                with pe.Fori(0, TRIPS) as i:
                    project(i, 0)
                    project(i, 1)
                    scores(i, 0)
                    scores(i, 1)
                    project_l3(i, 0)
                    turn(i, 0)
                    project_l3(i, 1)
                    turn(i, 1)
                    values(i, 0)
                    values(i, 1)

            @block.scalar
            def _(act):
                act.wait_ge(zero1, 1)

                def keep(i, u):
                    act.wait_ge(kp_made[u], i + 1)
                    act.wait_ge(s1_made[u], i)
                    nc.scalar.copy(kp1[:, u, :, :], b_kp[:, 0:H].rearrange("p (k n) -> p k n", k=KT)).then_inc(kp_kept[u], 1)
                    act.wait_ge(vp1_made[u], i + 1)
                    act.wait_ge(d1_made[u], i)
                    nc.scalar.copy(vp1[:, u, :], b_vp1[:, 0:H]).then_inc(vp1_kept[u], 1)

                def keep_l3(i, u):
                    act.wait_ge(k3_made[u], i + 1)
                    nc.scalar.activation(k3T[:, SLOTS * i + u, :, :], b_k3[:, 0:P].rearrange("p (b s) -> p b s", b=BT),
                                         ACT.Identity, bias=l3_bk[:, 0:1]).then_inc(k3_kept[u], 1)

                def exps(i, u):
                    act.wait_ge(max1_made[u], i + 1)
                    act.wait_ge(p1T_made[u], i)
                    for b in range(BT):
                        rows = slice(b * S, (b + 1) * S)
                        last = nc.scalar.activation(p1[rows, u, rows], b_s1[u][rows, rows], ACT.Exp,
                                                    bias=nmax1[rows, u:u + 1], accum_out=sum1[rows, u:u + 1])
                    last.then_inc(p1_made[u], 1)

                def keep_turned(i, u):
                    act.wait_ge(p1T_made[u], i + 1)
                    act.wait_ge(d1_made[u], i)
                    nc.scalar.copy(p1T[:, u, :], b_p1T[:, 0:P]).then_inc(p1T_kept[u], 1)

                with act.Fori(0, TRIPS) as i:
                    keep(i, 0)
                    keep(i, 1)
                    exps(i, 0)
                    exps(i, 1)
                    keep_l3(i, 0)
                    keep_turned(i, 0)
                    keep_l3(i, 1)
                    keep_turned(i, 1)

            @block.vector
            def _(dve):
                def maxima(i, u):
                    dve.wait_ge(s1_made[u], i + 1)
                    for b in range(BT):
                        rows = slice(b * S, (b + 1) * S)
                        last = nc.vector.reduce_max(nmax1[rows, u:u + 1], b_s1[u][rows, rows], AX.X, negate=True)
                    last.then_inc(max1_made[u], 1)

                def scale(i, u):
                    dve.wait_ge(p1_made[u], i + 1)
                    nc.vector.reciprocal(rsum1[:, u:u + 1], sum1[:, u:u + 1]).then_inc(chain1, 1)
                    dve.wait_ge(chain1, SLOTS * i + u + 1)
                    nc.vector.tensor_scalar(p1[:, u, :], p1[:, u, :], rsum1[:, u:u + 1], l1_alpha[:, 0:1],
                                            ALU.mult, ALU.mult).then_inc(p1_scaled[u], 1)

                def keep_values(i, u):
                    dve.wait_ge(v3_made[u], i + 1)
                    for g in range(2):
                        rows = slice(g * S, (g + 1) * S)
                        for b in range(BT):
                            last = nc.vector.tensor_tensor(
                                v3[rows, BT * (SLOTS * i + u) + b, :, g, 0:L3_D],
                                b_v3[rows, b * S:(b + 1) * S].rearrange("p (j g d) -> p j g d", j=QUARTERS, g=2)[:, :, g, :],
                                l3_bv[rows, :].rearrange("p (j g d) -> p j g d", j=QUARTERS, g=2)[:, :, g, :], ALU.add)
                    last.then_inc(v3_kept[u], 1)

                def finish(i, u):
                    dve.wait_ge(d1_made[u], i + 1)
                    nc.vector.tensor_tensor(hT[:, SLOTS * i + u, :, :, 1, :],
                                            b_d1[:, 0:H].rearrange("p (k b s) -> p k b s", k=KT, b=BT),
                                            ring1[:, u, 1, :, :, :], ALU.add).then_inc(x2_kept[u], 1)

                with dve.Fori(0, TRIPS) as i:
                    maxima(i, 0)
                    maxima(i, 1)
                    scale(i, 0)
                    scale(i, 1)
                    keep_values(i, 0)
                    keep_values(i, 1)
                    finish(i, 0)
                    finish(i, 1)

        next_phase()
        CHAIN2 = UNITS + SLOTS * 2
        ring = tb("ring", [P, SLOTS, KT, BT, 2, S])
        x_flat = tb("x_flat", [P, SLOTS, KT, BT, S])
        kz = tb("kz", [P, SLOTS, KT, QUARTERS, BT * L2_KEYS])
        v2 = tb("v2", [P, SLOTS, BT, L2_HEADS, L2_D + 1])
        sq = tb("sq", [P, SLOTS, H])
        ssq = tb("ssq", [P, SLOTS])
        rms = tb("rms", [P, SLOTS])

        zero2 = sem("zero2")
        ring2_in = sems("ring2_in", SLOTS)
        k2_made, q2_made, v2_made = sems("k2_made", SLOTS), sems("q2_made", SLOTS), sems("v2_made", SLOTS)
        k2_kept, q2_kept, v2_kept = sems("k2_kept", SLOTS), sems("q2_kept", SLOTS), sems("v2_kept", SLOTS)
        s2_made, s2_kept, s2_less_max = sems("s2_made", UT), sems("s2_kept", UT), sems("s2_less_max", UT)
        p2_made, p2T_made, p2T_kept = sems("p2_made", UT), sems("p2T_made", UT), sems("p2T_kept", UT)
        o2_made, att_made = sems("o2_made", SLOTS), sems("att_made", SLOTS)
        attT_made, attT_kept = sems("attT_made", SLOTS), sems("attT_kept", SLOTS)
        x2tok_made, x2tok_kept = sems("x2tok_made", SLOTS), sems("x2tok_kept", SLOTS)
        ow_made, res_made, ssq_made, y_made = sems("ow_made", SLOTS), sems("res_made", SLOTS), sems("ssq_made", SLOTS), sems("y_made", SLOTS)
        yT_made, yT_kept = sems("yT_made", SLOTS), sems("yT_kept", SLOTS)
        with_eps = sems("with_eps_l2_", SLOTS)
        rms_made = sems("rms_made", SLOTS)
        chain2 = sem("chain2")

        b_k2, b_q2, b_v2, b_p2T, b_o2, b_misc = (bank[k] for k in (0, 1, 2, 5, 6, 7))
        b_s2 = (bank[3], bank[4])

        with nc.Block() as block:
            @block.sync
            def _(sp):
                with sp.Fori(0, TRIPS) as i:
                    for u in range(SLOTS):
                        sp.wait_ge(x2tok_made[u], i)
                        sp.dma_start(ring[:, u, :, :, :, :], hT[:, SLOTS * i + u, :, :, :, :]).then_inc(ring2_in[u], 16)
                        sp.dma_start(x_flat[:, u, :, :, :], hT[:, SLOTS * i + u, :, :, 1, :]).then_inc(ring2_in[u], 16)

            @block.gpsimd
            def _(pool):
                nc.gpsimd.memset(qz[:, :, :, :, :, :], 0.0).then_inc(zero2, 1)
                nc.gpsimd.memset(v2[:, :, :, :, :], 1.0).then_inc(zero2, 1)
                with pool.Fori(0, TRIPS) as i:
                    for u in range(SLOTS):
                        pool.wait_ge(ssq_made[u], i + 1)
                        nc.gpsimd.tensor_tensor(rms[:, u:u + 1], ssq[:, u:u + 1], l2_eps[:, :], ALU.add).then_inc(with_eps[u], 1)
                        pool.wait_ge(with_eps[u], i + 1)
                        nc.gpsimd.tensor_tensor(rms[:, u:u + 1], rms[:, u:u + 1], rsqrt_power[:, 0:1], ALU.pow)\
                            .then_inc(rms_made[u], 1)

            @block.tensor
            def _(pe):
                def project(i, u):
                    v = 1 - u
                    before = i + 1 if u else i
                    pe.wait_ge(ring2_in[u], 32 * (i + 1))
                    pe.wait_ge(k2_kept[v], before)
                    if u == 0:
                        pe.wait_ge(res_made[1], i)
                    for m in range(KT):
                        for k in range(KT):
                            last = nc.tensor.matmul(b_k2[:, m * H:(m + 1) * H], l2_kw[:, k, m * P:(m + 1) * P],
                                                    ring[:, u, k, :, :, :], start=(k == 0), stop=(k == KT - 1))
                    last.then_inc(k2_made[u], 1)
                    pe.wait_ge(x2tok_kept[v], before)
                    for m in range(KT):
                        for k in range(KT):
                            last = nc.tensor.matmul(b_q2[:, m * P:(m + 1) * P], l2_qw[:, k, m * P:(m + 1) * P],
                                                    ring[:, u, k, :, 1, :], start=(k == 0), stop=(k == KT - 1))
                    last.then_inc(q2_made[u], 1)
                    pe.wait_ge(v2_kept[v], before)
                    for b in range(BT):
                        for k in range(KT):
                            last = nc.tensor.matmul(b_v2[:, b * H:(b + 1) * H], ring[:, u, k, b, :, :], l2_vw[:, k, :],
                                                    start=(k == 0), stop=(k == KT - 1))
                    last.then_inc(v2_made[u], 1)

                def stream(i, u):
                    pe.wait_ge(q2_kept[u], i + 1)
                    for k in range(KT):
                        last = nc.tensor.transpose(b_q2[:, k * P:(k + 1) * P], x_flat[:, u, k, :, :], ident[:, :])
                    last.then_inc(x2tok_made[u], 1)

                def scores(i, k):
                    u, b, m = k // UT, k // KT % BT, k % KT
                    pe.wait_ge(k2_kept[u], i + 1)
                    pe.wait_ge(q2_kept[u], i + 1)
                    await_unit(pe, s2_kept, i, k - 2, UNITS)
                    nc.tensor.matmul(b_s2[k % 2][:, :], qz[:, u, m, b, :, :], kz[:, u, m, :, b * L2_KEYS:(b + 1) * L2_KEYS],
                                     start=True, stop=True).then_inc(s2_made[k % UT], 1)

                def turn(i, k):
                    await_unit(pe, p2_made, i, k, UNITS)
                    await_unit(pe, p2T_kept, i, k - 1, UNITS)
                    for h in range(QUARTERS):
                        last = nc.tensor.transpose(b_p2T[:, h * P:(h + 1) * P], sc[:, k % UT, h, :], ident[:, :])
                    last.then_inc(p2T_made[k % UT], 1)

                def values(i, k):
                    u, b, m = k // UT, k // KT % BT, k % KT
                    await_unit(pe, p2T_kept, i, k, UNITS)
                    if k % UT == 0:
                        pe.wait_ge(v2_kept[u], i + 1)
                        pe.wait_ge(att_made[1 - u], i + 1 if u else i)
                    for h in range(QUARTERS):
                        for g in range(2):
                            head = m * 2 * QUARTERS + g * QUARTERS + h
                            last = nc.tensor.matmul(b_o2[b * S:(b + 1) * S, head * (L2_D + 1):(head + 1) * (L2_D + 1)],
                                                    pT[:, k % UT, h, g * S:(g + 1) * S], v2[:, u, b, head, :],
                                                    start=True, stop=True)
                    if k % UT == UT - 1:
                        last.then_inc(o2_made[u], 1)

                def out_project(i, u):
                    pe.wait_ge(att_made[u], i + 1)
                    pe.wait_ge(yT_kept[1 - u], i + 1 if u else i)
                    for k in range(KT):
                        last = nc.tensor.transpose(b_misc[:, k * P:(k + 1) * P], att[:, u, k * P:(k + 1) * P], ident[:, :])
                    last.then_inc(attT_made[u], 1)
                    pe.wait_ge(attT_kept[u], i + 1)
                    if u == 0:
                        pe.wait_ge(k2_kept[1], i + 1)
                    else:
                        pe.wait_ge(res_made[0], i + 1)
                    for k in range(KT):
                        last = nc.tensor.matmul(b_k2[:, 0:H], attT[:, u, k, :], l2_ow[:, k, :],
                                                start=(k == 0), stop=(k == KT - 1))
                    last.then_inc(ow_made[u], 1)

                def turn_y(i, u):
                    pe.wait_ge(y_made[u], i + 1)
                    for k in range(KT):
                        last = nc.tensor.transpose(b_misc[:, k * P:(k + 1) * P], res[:, u, k * P:(k + 1) * P], ident[:, :])
                    last.then_inc(yT_made[u], 1)

                with pe.Fori(0, TRIPS) as i:
                    project(i, 0)
                    scores(i, 0)
                    scores(i, 1)
                    stream(i, 0)
                    turn(i, 0)
                    scores(i, 2)
                    turn(i, 1)
                    values(i, 0)
                    scores(i, 3)
                    project(i, 1)
                    turn(i, 2)
                    values(i, 1)
                    scores(i, 4)
                    turn(i, 3)
                    values(i, 2)
                    stream(i, 1)
                    scores(i, 5)
                    turn(i, 4)
                    values(i, 3)
                    scores(i, 6)
                    turn(i, 5)
                    out_project(i, 0)
                    values(i, 4)
                    scores(i, 7)
                    turn(i, 6)
                    values(i, 5)
                    turn_y(i, 0)
                    turn(i, 7)
                    values(i, 6)
                    values(i, 7)
                    out_project(i, 1)
                    turn_y(i, 1)

            @block.scalar
            def _(act):
                act.wait_ge(zero2, 2)

                def keep_queries(i, u):
                    act.wait_ge(q2_made[u], i + 1)
                    await_unit(act, s2_made, i, -1, UNITS)
                    for m in range(KT):
                        for g in range(2):
                            rows = slice(g * S, (g + 1) * S)
                            last = nc.scalar.activation(qz[rows, u, m, :, g, :],
                                                        b_q2[rows, m * P:(m + 1) * P].rearrange("p (b s) -> p b s", b=BT),
                                                        ACT.Identity, bias=l2_qb[rows, m:m + 1], scale=1.0 / L2_D)
                    last.then_inc(q2_kept[u], 1)

                def keep_stream(i, u):
                    act.wait_ge(x2tok_made[u], i + 1)
                    nc.scalar.copy(x2tok[:, SLOTS * i + u, :], b_q2[:, 0:H]).then_inc(x2tok_kept[u], 1)

                def exps(i, k):
                    await_unit(act, s2_less_max, i, k, UNITS)
                    nc.scalar.activation(sc[:, k % UT, :, :], sc[:, k % UT, :, :], ACT.Exp).then_inc(p2_made[k % UT], 1)

                def keep_turned(i, k):
                    await_unit(act, p2T_made, i, k, UNITS)
                    act.wait_ge(o2_made[1 - k // UT], i + 1 if k >= UT else i)
                    nc.scalar.copy(pT[:, k % UT, :, :], b_p2T[:, :].rearrange("p (h n) -> p h n", h=QUARTERS)).then_inc(p2T_kept[k % UT], 1)

                def keep_attT(i, u):
                    act.wait_ge(attT_made[u], i + 1)
                    act.wait_ge(ow_made[u], i)
                    nc.scalar.copy(attT[:, u, :, :], b_misc[:, 0:H].rearrange("p (k n) -> p k n", k=KT)).then_inc(attT_kept[u], 1)

                def squares(i, u):
                    act.wait_ge(res_made[u], i + 1)
                    nc.scalar.activation(sq[:, u, :], res[:, u, :], ACT.Square, accum_out=ssq[:, u:u + 1]).then_inc(ssq_made[u], 1)

                def keep_y(i, u):
                    act.wait_ge(yT_made[u], i + 1)
                    for k in range(KT):
                        last = nc.scalar.mul(yT[:, k, bass.ds((SLOTS * i + u) * P, P)], b_misc[:, k * P:(k + 1) * P],
                                             l2_pw[:, k:k + 1])
                    last.then_inc(yT_kept[u], 1)

                with act.Fori(0, TRIPS) as i:
                    keep_queries(i, 0)
                    exps(i, 0)
                    keep_stream(i, 0)
                    keep_turned(i, 0)
                    exps(i, 1)
                    keep_turned(i, 1)
                    exps(i, 2)
                    keep_queries(i, 1)
                    keep_turned(i, 2)
                    exps(i, 3)
                    keep_turned(i, 3)
                    keep_stream(i, 1)
                    exps(i, 4)
                    keep_turned(i, 4)
                    exps(i, 5)
                    keep_turned(i, 5)
                    keep_attT(i, 0)
                    exps(i, 6)
                    squares(i, 0)
                    keep_turned(i, 6)
                    exps(i, 7)
                    keep_y(i, 0)
                    keep_turned(i, 7)
                    keep_attT(i, 1)
                    squares(i, 1)
                    keep_y(i, 1)

            @block.vector
            def _(dve):
                dve.wait_ge(zero2, 2)

                def keep_keys(i, u):
                    dve.wait_ge(k2_made[u], i + 1)
                    await_unit(dve, s2_made, i, -1, UNITS)
                    for m in range(KT):
                        last = nc.vector.scalar_tensor_tensor(
                            out=kz[:, u, m, :, :], in0=spread(b_k2[:, m * H:(m + 1) * H], 1, QUARTERS),
                            scalar=l2_kb[:, m:m + 1], in1=spread(quarter_mask[:, :], 2, H), op0=ALU.add, op1=ALU.mult)
                    last.then_inc(k2_kept[u], 1)

                def keep_values(i, u):
                    dve.wait_ge(v2_made[u], i + 1)
                    dve.wait_ge(o2_made[u], i)
                    nc.vector.tensor_tensor(v2[:, u, :, :, 0:L2_D],
                                            b_v2[:, :].rearrange("p (b h d) -> p b h d", b=BT, h=L2_HEADS),
                                            spread(l2_vb[:, :].rearrange("p (h d) -> p h d", h=L2_HEADS), 1, BT),
                                            ALU.add).then_inc(v2_kept[u], 1)

                def less_max(i, k, at):
                    u, b = k // UT, k // KT % BT
                    await_unit(dve, s2_made, i, k, UNITS)
                    await_unit(dve, p2T_made, i, k - UT, UNITS)
                    nc.vector.tensor_tensor(sc[:, k % UT, :, :], b_s2[k % 2][:, :].rearrange("p (h n) -> p h n", h=QUARTERS),
                                            spread(key_bias[:, BT * (SLOTS * i + u) + b, :], 1, QUARTERS),
                                            ALU.add).then_inc(s2_kept[k % UT], 1)
                    await_unit(dve, s2_kept, i, k, UNITS)
                    nc.vector.reduce_max(nmax[:, k % UT, 0:QUARTERS], sc[:, k % UT, :, :], AX.X, negate=True).then_inc(chain2, 1)
                    dve.wait_ge(chain2, CHAIN2 * i + at + 1)
                    nc.vector.tensor_tensor(sc[:, k % UT, :, :], sc[:, k % UT, :, :], spread(nmax[:, k % UT, 0:QUARTERS], 2, P),
                                            ALU.add).then_inc(s2_less_max[k % UT], 1)

                def normalise(i, u, at):
                    dve.wait_ge(o2_made[u], i + 1)
                    dve.wait_ge(attT_made[u], i)
                    o = b_o2[:, 0:L2_HEADS * (L2_D + 1)].rearrange("p (h e) -> p h e", e=L2_D + 1)
                    nc.vector.reciprocal(rsum[:, u, 0:L2_HEADS], o[:, :, L2_D]).then_inc(chain2, 1)
                    dve.wait_ge(chain2, CHAIN2 * i + at + 1)
                    nc.vector.tensor_tensor(att[:, u, :].rearrange("p (h d) -> p h d", d=L2_D), o[:, :, 0:L2_D],
                                            spread(rsum[:, u, 0:L2_HEADS], 2, L2_D), ALU.mult).then_inc(att_made[u], 1)

                def residual(i, u, at):
                    dve.wait_ge(ow_made[u], i + 1)
                    dve.wait_ge(yT_made[u], i)
                    dve.wait_ge(x2tok_kept[u], i + 1)
                    nc.vector.tensor_tensor(res[:, u, :], b_k2[:, 0:H], x2tok[:, SLOTS * i + u, :], ALU.add).then_inc(chain2, 1)
                    dve.wait_ge(chain2, CHAIN2 * i + at + 1)
                    nc.vector.tensor_tensor(res[:, u, :], res[:, u, :], l2_ob[:, :], ALU.add).then_inc(res_made[u], 1)

                def rms_norm(i, u):
                    dve.wait_ge(rms_made[u], i + 1)
                    nc.vector.tensor_scalar(res[:, u, :], res[:, u, :], rms[:, u:u + 1], float(H) ** 0.5,
                                            ALU.mult, ALU.mult).then_inc(y_made[u], 1)

                with dve.Fori(0, TRIPS) as i:
                    keep_keys(i, 0)
                    keep_values(i, 0)
                    less_max(i, 0, 0)
                    less_max(i, 1, 1)
                    less_max(i, 2, 2)
                    keep_keys(i, 1)
                    keep_values(i, 1)
                    less_max(i, 3, 3)
                    less_max(i, 4, 4)
                    normalise(i, 0, 5)
                    less_max(i, 5, 6)
                    less_max(i, 6, 7)
                    residual(i, 0, 8)
                    less_max(i, 7, 9)
                    rms_norm(i, 0)
                    normalise(i, 1, 10)
                    residual(i, 1, 11)
                    rms_norm(i, 1)

        UPS = 4
        TOK = SLOTS * P
        next_phase()
        gT = tb("gT", [P, FT, TOK])
        up_made, gelu_made = sems("up_made", UPS), sems("gelu_made", UPS)
        down_made, x3_kept = sems("down_made", SLOTS), sems("x3_kept", SLOTS)
        x2b_made = sem("x2b_made")
        chain3 = sem("chain3")
        b_down = (bank[4], bank[5])

        with nc.Block() as block:
            @block.gpsimd
            def _(pool):
                with pool.Fori(0, TILES) as n:
                    nc.gpsimd.tensor_tensor(x2tok[:, n, :], x2tok[:, n, :], mlp_b2[:, :], ALU.add).then_inc(x2b_made, 1)

            @block.tensor
            def _(pe):
                with pe.Fori(0, TRIPS) as i:
                    for j in range(UPS):
                        pe.wait_ge(gelu_made[j], i)
                        for f in range(2):
                            for k in range(KT):
                                last = nc.tensor.matmul(bank[j][:, f * TOK:(f + 1) * TOK],
                                                        mlp_w1[:, k, (2 * j + f) * P:(2 * j + f + 1) * P],
                                                        yT[:, k, bass.ds(i * TOK, TOK)], start=(k == 0), stop=(k == KT - 1))
                        last.then_inc(up_made[j], 1)
                    for u in range(SLOTS):
                        pe.wait_ge(x3_kept[u], i)
                        for f in range(FT):
                            if u == 0 and f % 2 == 0:
                                pe.wait_ge(gelu_made[f // 2], i + 1)
                            last = nc.tensor.matmul(b_down[u][:, 0:H], gT[:, f, u * P:(u + 1) * P], mlp_w2[:, f, :],
                                                    start=(f == 0), stop=(f == FT - 1))
                        last.then_inc(down_made[u], 1)

            @block.scalar
            def _(act):
                with act.Fori(0, TRIPS) as i:
                    for j in range(UPS):
                        act.wait_ge(up_made[j], i + 1)
                        act.wait_ge(down_made[1], i)
                        for f in range(2):
                            last = nc.scalar.activation(gT[:, 2 * j + f, :], bank[j][:, f * TOK:(f + 1) * TOK],
                                                        ACT.Gelu_apprx_tanh, bias=mlp_b1[:, 2 * j + f:2 * j + f + 1])
                        last.then_inc(gelu_made[j], 1)

            @block.vector
            def _(dve):
                with dve.Fori(0, TRIPS) as i:
                    for u in range(SLOTS):
                        dve.wait_ge(down_made[u], i + 1)
                        dve.wait_ge(x2b_made, SLOTS * i + u + 1)
                        nc.vector.tensor_tensor(x3tok[:, SLOTS * i + u, :], b_down[u][:, 0:H], x2tok[:, SLOTS * i + u, :],
                                                ALU.add).then_inc(x3_kept[u], 1)

        CHAIN4 = UNITS + SLOTS * 5
        next_phase()
        x3_ring = tb("x3_ring", [P, SLOTS, H])
        x3T = tb("x3T", [P, SLOTS, KT, P])
        k3z = tb("k3z", [P, SLOTS, BT, KVH, S])
        v3z = tb("v3z", [P, SLOTS, BT, QUARTERS, 2 * (L3_D + 1)])
        stats3 = tb("stats3", [P, SLOTS, 6])
        moments3 = tb("moments3", [P, SLOTS, 2])
        rstd3 = tb("rstd3", [P, SLOTS])
        result = tb("result", [P, SLOTS, H])

        x3_in = sems("x3_in", SLOTS)
        k3z_made, v3z_made = sems("k3z_made", SLOTS), sems("v3z_made", SLOTS)
        x3T_made, x3T_kept = sems("x3T_made", SLOTS), sems("x3T_kept", SLOTS)
        q3_made, q3_kept = sems("q3_made", SLOTS), sems("q3_kept", SLOTS)
        s3_made, s3_kept, s3_less_max = sems("s3_made", UT), sems("s3_kept", UT), sems("s3_less_max", UT)
        p3_made, p3T_made, p3T_kept = sems("p3_made", UT), sems("p3T_made", UT), sems("p3T_kept", UT)
        o3_made, att3_made = sems("o3_made", SLOTS), sems("att3_made", SLOTS)
        att3T_made, att3T_kept = sems("att3T_made", SLOTS), sems("att3T_kept", SLOTS)
        wo3_made, wo3_kept = sems("wo3_made", SLOTS), sems("wo3_kept", SLOTS)
        result_made, stored = sems("result_made", SLOTS), sems("stored", SLOTS)
        with_eps = sems("with_eps_l3_", SLOTS)
        moments3_made, rstd3_made = sems("moments3_made", SLOTS), sems("rstd3_made", SLOTS)
        chain4 = sem("chain4")

        b_x3T, b_q3, b_p3T, b_o3, b_att3T, b_wo3 = (bank[k] for k in (0, 1, 4, 5, 6, 7))
        b_s3 = (bank[2], bank[3])

        with nc.Block() as block:
            @block.sync
            def _(sp):
                with sp.Fori(0, TRIPS) as i:
                    for u in range(SLOTS):
                        sp.wait_ge(x3T_made[u], i)
                        sp.wait_ge(wo3_kept[u], i)
                        sp.dma_start(x3_ring[:, u, :], x3tok[:, SLOTS * i + u, :]).then_inc(x3_in[u], 16)
                    for u in range(SLOTS):
                        sp.wait_ge(result_made[u], i + 1)
                        sp.dma_start(out[SLOTS * i + u, :, :], result[:, u, :]).then_inc(stored[u], 16)
                for u in range(SLOTS):
                    sp.wait_ge(stored[u], 16 * TRIPS)

            @block.gpsimd
            def _(pool):
                with pool.Fori(0, TRIPS) as i:
                    for u in range(SLOTS):
                        await_unit(pool, s3_made, i, -1, UNITS)
                        for b in range(BT):
                            last = nc.gpsimd.tensor_tensor(k3z[:, u, b, :, :], spread(k3T[:, SLOTS * i + u, b, :], 1, KVH),
                                                           spread(kvh_mask[:, :], 2, S), ALU.mult)
                        last.then_inc(k3z_made[u], 1)
                        pool.wait_ge(o3_made[u], i)
                        nc.gpsimd.tensor_copy(v3z[:, u, :, :, :].rearrange("p b j e -> p (b j e)"),
                                              v3[:, bass.ds(BT * (SLOTS * i + u), BT), :, :, :].rearrange("p b j g e -> p (b j g e)"))\
                            .then_inc(v3z_made[u], 1)
                    for u in range(SLOTS):
                        pool.wait_ge(moments3_made[u], i + 1)
                        nc.gpsimd.tensor_tensor(rstd3[:, u:u + 1], moments3[:, u, 1:2], l3_eps[:, :], ALU.add).then_inc(with_eps[u], 1)
                        pool.wait_ge(with_eps[u], i + 1)
                        nc.gpsimd.tensor_tensor(rstd3[:, u:u + 1], rstd3[:, u:u + 1], rsqrt_power[:, 0:1], ALU.pow)\
                            .then_inc(rstd3_made[u], 1)

            @block.tensor
            def _(pe):
                def project(i, u):
                    v = 1 - u
                    before = i + 1 if u else i
                    pe.wait_ge(x3_in[u], 16 * (i + 1))
                    pe.wait_ge(x3T_kept[v], before)
                    for k in range(KT):
                        last = nc.tensor.transpose(b_x3T[:, k * P:(k + 1) * P], x3_ring[:, u, k * P:(k + 1) * P], ident[:, :])
                    last.then_inc(x3T_made[u], 1)
                    pe.wait_ge(x3T_kept[u], i + 1)
                    pe.wait_ge(q3_kept[v], before)
                    for m in range(KT):
                        for k in range(KT):
                            last = nc.tensor.matmul(b_q3[:, m * P:(m + 1) * P], l3_wq[:, k, m * P:(m + 1) * P],
                                                    x3T[:, u, k, :], start=(k == 0), stop=(k == KT - 1))
                    last.then_inc(q3_made[u], 1)

                def scores(i, k):
                    u, b, m = k // UT, k // KT % BT, k % KT
                    pe.wait_ge(q3_kept[u], i + 1)
                    pe.wait_ge(k3z_made[u], i + 1)
                    await_unit(pe, s3_kept, i, k - 2, UNITS)
                    nc.tensor.matmul(b_s3[k % 2][:, :], qz[:, u, m, b, :, :], k3z[:, u, b, :, :], start=True, stop=True)\
                        .then_inc(s3_made[k % UT], 1)

                def turn(i, k):
                    await_unit(pe, p3_made, i, k, UNITS)
                    await_unit(pe, p3T_kept, i, k - 1, UNITS)
                    for h in range(QUARTERS):
                        last = nc.tensor.transpose(b_p3T[:, h * P:(h + 1) * P], sc[:, k % UT, h, :], ident[:, :])
                    last.then_inc(p3T_made[k % UT], 1)

                def values(i, k):
                    u, b, m = k // UT, k // KT % BT, k % KT
                    await_unit(pe, p3T_kept, i, k, UNITS)
                    if k % UT == 0:
                        pe.wait_ge(v3z_made[u], i + 1)
                        pe.wait_ge(att3_made[1 - u], i + 1 if u else i)
                    w = 2 * (L3_D + 1)
                    for j in range(QUARTERS):
                        for g in range(2):
                            at = ((2 * m + g) * QUARTERS + j) * w
                            last = nc.tensor.matmul(b_o3[b * S:(b + 1) * S, at:at + w], pT[:, k % UT, j, g * S:(g + 1) * S],
                                                    v3z[:, u, b, j, :], start=True, stop=True)
                    if k % UT == UT - 1:
                        last.then_inc(o3_made[u], 1)

                def out_project(i, u):
                    pe.wait_ge(att3_made[u], i + 1)
                    pe.wait_ge(att3T_kept[1 - u], i + 1 if u else i)
                    for k in range(KT):
                        last = nc.tensor.transpose(b_att3T[:, k * P:(k + 1) * P], att[:, u, k * P:(k + 1) * P], ident[:, :])
                    last.then_inc(att3T_made[u], 1)
                    pe.wait_ge(att3T_kept[u], i + 1)
                    pe.wait_ge(wo3_kept[1 - u], i + 1 if u else i)
                    for k in range(KT):
                        last = nc.tensor.matmul(b_wo3[:, 0:H], attT[:, u, k, :], l3_wo[:, k, :],
                                                start=(k == 0), stop=(k == KT - 1))
                    last.then_inc(wo3_made[u], 1)

                with pe.Fori(0, TRIPS) as i:
                    project(i, 0)
                    scores(i, 0)
                    scores(i, 1)
                    project(i, 1)
                    turn(i, 0)
                    scores(i, 2)
                    turn(i, 1)
                    values(i, 0)
                    scores(i, 3)
                    turn(i, 2)
                    values(i, 1)
                    scores(i, 4)
                    turn(i, 3)
                    values(i, 2)
                    scores(i, 5)
                    turn(i, 4)
                    values(i, 3)
                    scores(i, 6)
                    turn(i, 5)
                    out_project(i, 0)
                    values(i, 4)
                    scores(i, 7)
                    turn(i, 6)
                    values(i, 5)
                    turn(i, 7)
                    values(i, 6)
                    values(i, 7)
                    out_project(i, 1)

            @block.scalar
            def _(act):
                def keep_queries(i, u):
                    act.wait_ge(x3T_made[u], i + 1)
                    act.wait_ge(q3_made[u], i)
                    nc.scalar.copy(x3T[:, u, :, :], b_x3T[:, 0:H].rearrange("p (k n) -> p k n", k=KT)).then_inc(x3T_kept[u], 1)
                    act.wait_ge(q3_made[u], i + 1)
                    await_unit(act, s3_made, i, -1, UNITS)
                    for m in range(KT):
                        for g in range(2):
                            rows = slice(g * S, (g + 1) * S)
                            last = nc.scalar.activation(qz[rows, u, m, :, g, :],
                                                        b_q3[rows, m * P:(m + 1) * P].rearrange("p (b s) -> p b s", b=BT),
                                                        ACT.Identity, bias=l3_bq[rows, m:m + 1], scale=L3_D ** -0.5)
                    last.then_inc(q3_kept[u], 1)

                def exps(i, k):
                    await_unit(act, s3_less_max, i, k, UNITS)
                    nc.scalar.activation(sc[:, k % UT, :, :], sc[:, k % UT, :, :], ACT.Exp).then_inc(p3_made[k % UT], 1)

                def keep_turned(i, k):
                    await_unit(act, p3T_made, i, k, UNITS)
                    act.wait_ge(o3_made[1 - k // UT], i + 1 if k >= UT else i)
                    nc.scalar.copy(pT[:, k % UT, :, :], b_p3T[:, :].rearrange("p (h n) -> p h n", h=QUARTERS)).then_inc(p3T_kept[k % UT], 1)

                def keep_attT(i, u):
                    act.wait_ge(att3T_made[u], i + 1)
                    act.wait_ge(wo3_made[u], i)
                    nc.scalar.copy(attT[:, u, :, :], b_att3T[:, 0:H].rearrange("p (k n) -> p k n", k=KT)).then_inc(att3T_kept[u], 1)

                with act.Fori(0, TRIPS) as i:
                    keep_queries(i, 0)
                    exps(i, 0)
                    keep_queries(i, 1)
                    keep_turned(i, 0)
                    exps(i, 1)
                    keep_turned(i, 1)
                    exps(i, 2)
                    keep_turned(i, 2)
                    exps(i, 3)
                    keep_turned(i, 3)
                    exps(i, 4)
                    keep_turned(i, 4)
                    exps(i, 5)
                    keep_turned(i, 5)
                    keep_attT(i, 0)
                    exps(i, 6)
                    keep_turned(i, 6)
                    exps(i, 7)
                    keep_turned(i, 7)
                    keep_attT(i, 1)

            @block.vector
            def _(dve):
                def less_max(i, k, at):
                    u, b = k // UT, k // KT % BT
                    await_unit(dve, s3_made, i, k, UNITS)
                    await_unit(dve, p3T_made, i, k - UT, UNITS)
                    s = sc[:, k % UT, :, :].rearrange("p h (g n) -> p (h g) n", g=2)
                    nc.vector.tensor_tensor(s, b_s3[k % 2][:, :].rearrange("p (h n) -> p h n", h=KVH),
                                            spread(ff_mask[:, BT * (SLOTS * i + u) + b, :], 1, KVH),
                                            ALU.add).then_inc(s3_kept[k % UT], 1)
                    await_unit(dve, s3_kept, i, k, UNITS)
                    nc.vector.reduce_max(nmax[:, k % UT, :], s, AX.X, negate=True).then_inc(chain4, 1)
                    dve.wait_ge(chain4, CHAIN4 * i + at + 1)
                    nc.vector.tensor_tensor(s, s, spread(nmax[:, k % UT, :], 2, S), ALU.add).then_inc(s3_less_max[k % UT], 1)

                def normalise(i, u, at):
                    dve.wait_ge(o3_made[u], i + 1)
                    dve.wait_ge(att3T_made[u], i)
                    o = b_o3[:, 0:GROUPS * KVH * (L3_D + 1)].rearrange("p (g h e) -> p h g e", g=GROUPS, e=L3_D + 1)
                    r = rsum[:, u, :].rearrange("p (h g) -> p h g", h=KVH)
                    nc.vector.reciprocal(r, o[:, :, :, L3_D]).then_inc(chain4, 1)
                    dve.wait_ge(chain4, CHAIN4 * i + at + 1)
                    nc.vector.tensor_tensor(att[:, u, :].rearrange("p (h g d) -> p h g d", h=KVH, g=GROUPS),
                                            o[:, :, :, 0:L3_D], spread(r, 3, L3_D), ALU.mult).then_inc(att3_made[u], 1)

                def finish(i, u, at):
                    dve.wait_ge(wo3_made[u], i + 1)
                    dve.wait_ge(x3_in[u], 16 * (i + 1))
                    nc.vector.tensor_tensor(res[:, u, :], b_wo3[:, 0:H], x3_ring[:, u, :], ALU.add).then_inc(wo3_kept[u], 1)
                    dve.wait_ge(wo3_kept[u], i + 1)
                    nc.vector.tensor_tensor(res[:, u, :], res[:, u, :], l3_bo[:, :], ALU.add).then_inc(chain4, 1)
                    dve.wait_ge(chain4, CHAIN4 * i + at + 1)
                    nc.vector.bn_stats(stats3[:, u, :], res[:, u, :]).then_inc(chain4, 1)
                    dve.wait_ge(chain4, CHAIN4 * i + at + 2)
                    nc.vector.memset(scratch[:, :], 0.0)
                    nc.vector.bn_aggr(moments3[:, u, :], stats3[:, u, :]).then_inc(moments3_made[u], 1)
                    dve.wait_ge(rstd3_made[u], i + 1)
                    nc.vector.tensor_scalar(res[:, u, :], res[:, u, :], moments3[:, u, 0:1], rstd3[:, u:u + 1],
                                            ALU.subtract, ALU.mult).then_inc(chain4, 1)
                    dve.wait_ge(chain4, CHAIN4 * i + at + 3)
                    nc.vector.tensor_tensor(res[:, u, :], res[:, u, :], l3_gamma[:, :], ALU.mult).then_inc(chain4, 1)
                    dve.wait_ge(chain4, CHAIN4 * i + at + 4)
                    dve.wait_ge(stored[u], 16 * i)
                    nc.vector.tensor_tensor(result[:, u, :], res[:, u, :], l3_beta[:, :], ALU.add).then_inc(result_made[u], 1)

                with dve.Fori(0, TRIPS) as i:
                    less_max(i, 0, 0)
                    less_max(i, 1, 1)
                    less_max(i, 2, 2)
                    less_max(i, 3, 3)
                    less_max(i, 4, 4)
                    normalise(i, 0, 5)
                    less_max(i, 5, 6)
                    less_max(i, 6, 7)
                    less_max(i, 7, 8)
                    finish(i, 0, 9)
                    normalise(i, 1, 13)
                    finish(i, 1, 14)

        if dump is not None:
            name, ap = dump
            taken = {"hT": hT, "k3T": k3T, "v3": v3, "x2tok": x2tok, "x3tok": x3tok, "yT": yT, "key_bias": key_bias}[name]
            dumped = sem("dumped")
            with nc.Block() as block:
                @block.sync
                def _(sp):
                    sp.dma_start(ap, taken[tuple([slice(None)] * len(taken.shape))]).then_inc(dumped, 16)
                    sp.wait_ge(dumped, 16)


def layouts(inputs):
    import numpy as np
    v = {k: np.asarray(x) for k, x in inputs.items()}
    cols = lambda w, n: np.ascontiguousarray(w.reshape(n, P).T)
    row = lambda w: w.reshape(1, -1)
    twice = lambda w: np.concatenate([w, w], axis=-1)
    kv_w = v["L2_xattn_kv_w"].reshape(H, H, 2)
    kv_b = v["L2_xattn_kv_b"].reshape(H, 2)
    grouped = lambda w: w.reshape(-1, KVH, GROUPS, L3_D).transpose(0, 2, 1, 3).reshape(w.shape)
    rows = np.arange(P)
    d = {
        "x": v["x"].reshape(TILES, P, H), "ctx": v["ctx_2048"].reshape(TILES, P, H),
        "key_flags": v["mask_BxS2_ik0"].reshape(B, S), "ff_mask": v["mask_Bx1xSxS2_ff0"].reshape(B, S, S),
        "l0_wnT": v["L0_xattn_Wn"].T, "l0_wmT": v["L0_xattn_Wm"].T, "l0_wl2": twice(v["L0_xattn_Wl"]),
        "l0_woT": v["L0_xattn_Wo"].T, "l0_bl": v["L0_xattn_bl"].reshape(S, 1),
        "l0_bn": twice(v["L0_xattn_bn"]).reshape(P, 1), "l0_bm": twice(v["L0_xattn_bm"]).reshape(P, 1),
        "l0_bo": row(v["L0_xattn_bo"]),
        "l1_wk": v["L1_xattn_w_k"], "l1_wq": v["L1_xattn_w_q"], "l1_wv": v["L1_xattn_w_v"], "l1_woT": v["L1_xattn_w_o"].T,
        "l1_alpha": v["L1_xattn_alpha"].reshape(1, 1),
        "l2_qw": v["L2_xattn_q_w"], "l2_kw": kv_w[:, :, 0], "l2_vw": kv_w[:, :, 1], "l2_ow": v["L2_xattn_out_w"],
        "l2_qb": cols(v["L2_xattn_q_b"], KT), "l2_kb": cols(kv_b[:, 0], KT), "l2_vb": row(kv_b[:, 1]),
        "l2_pw": cols(v["L2_xattn_postnorm_w"], KT), "l2_ob": row(v["L2_xattn_out_b"]),
        "mlp_w1": v["L2_xattn_mlp_w1"], "mlp_b1": cols(v["L2_xattn_mlp_b1"], FT),
        "mlp_w2": v["L2_xattn_mlp_w2"], "mlp_b2": row(v["L2_xattn_mlp_b2"]),
        "l3_wq": grouped(v["L3_xattn_Wq"]), "l3_bq": cols(grouped(v["L3_xattn_bq"]), KT),
        "l3_wk": twice(v["L3_xattn_Wk"]), "l3_bk": twice(v["L3_xattn_bk"]).reshape(P, 1),
        "l3_wv": v["L3_xattn_Wv"], "l3_bv": row(v["L3_xattn_bv"]), "l3_wo": v["L3_xattn_Wo"], "l3_bo": row(v["L3_xattn_bo"]),
        "l3_gamma": row(v["L3_xattn_gamma"]), "l3_beta": row(v["L3_xattn_beta"]),
        "ident": np.eye(P, dtype=np.float32),
        "quarter_mask": (rows[:, None] // L2_D % QUARTERS == np.arange(QUARTERS)).astype(np.float32),
        "kvh_mask": (rows[:, None] // L3_D % KVH == np.arange(KVH)).astype(np.float32),
    }
    return {k: np.ascontiguousarray(x) for k, x in d.items()}


def kernel(**inputs):
    import concourse.bacc as bacc
    from concourse.bass_utils import run_bass_kernel_spmd

    nc = bacc.Bacc("TRN2", target_bir_lowering=False, num_devices=1)
    arrays = {f"in_{k}": x for k, x in layouts(inputs).items()}
    aps = {k[3:]: nc.dram_tensor(k, x.shape, mybir.dt.from_np(x.dtype), kind="ExternalInput").ap() for k, x in arrays.items()}
    out = nc.dram_tensor("out", (TILES, P, H), F32, kind="ExternalOutput").ap()
    build(nc, aps, out)
    r = run_bass_kernel_spmd(nc, [arrays], core_ids=[0])
    return r.results[0]["out"].reshape(B, S, H)
```

```python
from contextlib import ExitStack

import concourse.bass as bass
from concourse import mybir

F32 = mybir.dt.float32
I32 = mybir.dt.int32
ALU = mybir.AluOpType
ACT = mybir.ActivationFunctionType
AX = mybir.AxisListType

P = 128
B, S, H = 16, 64, 256
KT = H // P
SLOTS = 2
TILES = B * S // P
TRIPS = TILES // SLOTS
BT = P // S
L2_HEADS, L2_D = 16, 16
L2_KEYS = 2 * S
FF = 4 * H
FT = FF // P
KVH, GROUPS, L3_D = 8, 4, 8
L0_EPS, RMS_EPS, LN_EPS = 1e-5, 1e-6, 1e-6
MASKED = -1e30
UT = BT * KT
UNITS = SLOTS * UT
QUARTERS = 4


COLUMNS = {"l2_qb": KT, "l2_kb": KT, "l2_pw": KT, "mlp_b1": FT, "l3_bq": KT, "l3_bk": 1, "quarter_mask": QUARTERS, "kvh_mask": KVH}
ROWS = {"l1_alpha": 1, "l2_vb": H, "l2_ob": H, "mlp_b2": H, "l3_bv": KVH * L3_D, "l3_bo": H, "l3_gamma": H, "l3_beta": H}


def offset(widths, name):
    names = list(widths)
    return sum(widths[n] for n in names[:names.index(name)])


def each_trip(engine, body):
    body(0)
    with engine.Fori(1, TRIPS - 1) as i:
        body(i)
    body(TRIPS - 1)


def is_first(i):
    return isinstance(i, int) and i == 0


def is_last(i):
    return isinstance(i, int) and i == TRIPS - 1


def reached(i, k):
    return UNITS // UT * i + (k // UT + 1)


def spread(ap, axis, n):
    shape = list(ap.shape)
    return ap.unsqueeze(axis).broadcast_to(shape[:axis] + [n] + shape[axis:])


def build(nc, a, out, dump=None):
    ctx = ExitStack()
    with ctx:
        phase_memory = [ctx.enter_context(ExitStack())]
        phase_sems = []

        def sb(name, shape, dt=F32):
            return ctx.enter_context(nc.sbuf_tensor(name, shape, dt))

        def tb(name, shape):
            return phase_memory[0].enter_context(nc.sbuf_tensor(name, shape, F32))

        def next_phase():
            phase_memory[0].close()
            phase_memory[0] = ctx.enter_context(ExitStack())
            nc.clear_and_free_semaphores(list(phase_sems))
            phase_sems.clear()
            nc.all_engine_barrier()

        def sem(name):
            phase_sems.append(nc.alloc_semaphore(name=name))
            return phase_sems[-1]

        def sems(name, n):
            return [sem(f"{name}{k}") for k in range(n)]

        bank = [ctx.enter_context(nc.psum_tensor(f"bank{k}", [P, 512], F32)) for k in range(8)]

        ident = sb("ident", [P, P])
        columns = sb("columns", [P, sum(COLUMNS.values())])
        rows_in = sb("rows_in", [P, sum(ROWS.values())])
        column = lambda name: columns[:, offset(COLUMNS, name):offset(COLUMNS, name) + COLUMNS[name]]
        row = lambda name: rows_in[:, offset(ROWS, name):offset(ROWS, name) + ROWS[name]]
        quarter_mask = column("quarter_mask")
        kvh_mask = column("kvh_mask")
        rsqrt_power = sb("rsqrt_power", [P, 2])
        l0_eps = sb("l0_eps", [P, 2])
        l2_eps = sb("l2_eps", [P, 1])
        l3_eps = sb("l3_eps", [P, 1])
        scratch = sb("scratch", [P, 1])
        l0_wn = sb("l0_wn", [P, P])
        l0_wm = sb("l0_wm", [P, P])
        l0_first = sb("l0_first", [P, P + S + S + 1 + 2])
        l0_wl2, l0_woT = l0_first[0:S, 0:P], l0_first[0:S, P:P + S]
        l0_bo = l0_first[:, P + S:P + 2 * S]
        l0_bl = l0_first[0:S, P + 2 * S:P + 2 * S + 1]
        l0_bn, l0_bm = (l0_first[:, P + 2 * S + j:P + 2 * S + j + 1] for j in (1, 2))
        l0_wol = sb("l0_wol", [P, P])
        l0_bias = sb("l0_bias", [P, S])
        l1_weights = sb("l1_weights", [P, 4, KT, H])
        l1_wk, l1_wq, l1_wv, l1_woT = (l1_weights[:, n, :, :] for n in range(4))
        l1_kq = sb("l1_kq", [P, KT, H])
        l1_vo = sb("l1_vo", [P, KT, H])
        l1_alpha = row("l1_alpha")
        squares = sb("squares", [P, 6, KT, H])
        l2_qw, l2_kw, l2_vw, l2_ow, l3_wq, l3_wo = (squares[:, n, :, :] for n in range(6))
        l2_qb, l2_kb, l2_pw, mlp_b1, l3_bq, l3_bk = (
            column(name) for name in ("l2_qb", "l2_kb", "l2_pw", "mlp_b1", "l3_bq", "l3_bk"))
        l2_vb, l2_ob, mlp_b2, l3_bv, l3_bo, l3_gamma, l3_beta = (
            row(name) for name in ("l2_vb", "l2_ob", "mlp_b2", "l3_bv", "l3_bo", "l3_gamma", "l3_beta"))
        mlp_w1 = sb("mlp_w1", [P, KT, FF])
        mlp_w2 = sb("mlp_w2", [P, FT, H])
        l3_kvw = sb("l3_kvw", [P, KT, P + S])
        l3_wk, l3_wv = l3_kvw[:, :, 0:P], l3_kvw[:, :, P:P + S]
        key_flags = sb("key_flags", [P, B, S], I32)
        key_bias = sb("key_bias", [P, B, L2_KEYS])
        ff_mask = sb("ff_mask", [P, B, S])

        qz = sb("qz", [P, SLOTS, KT, BT, 2, S])
        sc = sb("sc", [P, UT, QUARTERS, P])
        pT = sb("pT", [P, UT, QUARTERS, P])
        nmax = sb("nmax", [P, UT, KVH])
        rsum = sb("rsum", [P, SLOTS, 2 * L2_HEADS])
        att = sb("att", [P, SLOTS, H])
        attT = sb("attT", [P, SLOTS, KT, P])
        res = sb("res", [P, SLOTS, H])

        hT = sb("hT", [P, TILES, KT, BT, 2, S])
        k3T = sb("k3T", [P, TILES, BT, S])
        v3 = sb("v3", [P, B, QUARTERS, 2, L3_D + 1])
        x2tok = sb("x2tok", [P, TILES, H])
        x3tok = sb("x3tok", [P, TILES, H])
        yT = sb("yT", [P, KT, TILES * P])

        k_p_n = lambda w: w.rearrange("(k p) n -> p k n", p=P)
        loads = [
            (ident[:, :], a["ident"]), (l0_first[:, :], a["l0_first"]),
            (l1_weights[:, :, :, :], a["l1_weights"].rearrange("w (k p) n -> p w k n", p=P)),
        ]
        middle_loads = [
            (columns[:, :], a["columns"]), (rows_in[:, :], a["rows"].partition_broadcast(P)),
            (l3_kvw[:, :, :], k_p_n(a["l3_kvw"])),
            (squares[:, :, :, :], a["squares"].rearrange("w (k p) n -> p w k n", p=P)),
        ]
        late_loads = [
            (key_flags[:, :, :], a["key_flags"].partition_broadcast(P)),
            (mlp_w1[:, :, :], k_p_n(a["mlp_w1"])), (mlp_w2[:, :, :], k_p_n(a["mlp_w2"])),
            (ff_mask[0:S, :, :], a["ff_mask"].rearrange("b q s -> q b s")),
            (ff_mask[S:P, :, :], a["ff_mask"].rearrange("b q s -> q b s")),
        ]
        middle_in = nc.alloc_semaphore(name="middle_in")
        late_in = nc.alloc_semaphore(name="late_in")
        early_in = sem("early_in")
        blocks_in = sem("blocks_in")
        blocks_zeroed = sem("blocks_zeroed")
        zeroed = sem("zeroed")
        w_made = sem("w_made")
        w_kept = sem("w_kept")
        consts_made = sem("consts_made")

        with nc.Block() as block:
            @block.sync
            def _(sp):
                for dst, src in loads:
                    sp.dma_start(dst, src).then_inc(early_in, 16)
                sp.wait_ge(blocks_zeroed, 2)
                for w, name in ((l0_wn, "l0_wnT"), (l0_wm, "l0_wmT")):
                    for b in range(BT):
                        sp.dma_start(w[b * S:(b + 1) * S, b * S:(b + 1) * S], a[name]).then_inc(blocks_in, 16)
                sp.wait_ge(blocks_in, 4 * 16)

            @block.gpsimd
            def _(pool):
                nc.gpsimd.memset(rsqrt_power[:, :], -0.5).then_inc(consts_made, 1)
                nc.gpsimd.memset(l0_eps[:, :], L0_EPS).then_inc(consts_made, 1)
                nc.gpsimd.memset(l2_eps[:, :], H * RMS_EPS).then_inc(consts_made, 1)
                nc.gpsimd.memset(l3_eps[:, :], LN_EPS).then_inc(consts_made, 1)
                nc.gpsimd.memset(l0_wn[:, :], 0.0).then_inc(blocks_zeroed, 1)
                nc.gpsimd.memset(l0_wm[:, :], 0.0).then_inc(blocks_zeroed, 1)

            @block.tensor
            def _(pe):
                pe.wait_ge(early_in, 16 * len(loads))
                nc.tensor.matmul(bank[0][:, 0:S], l0_wl2[:, :], l0_woT[:, :], start=True, stop=True).then_inc(w_made, 1)
                nc.tensor.matmul(bank[1][:, 0:S], l0_bl[:, 0:1].broadcast_to([S, P]), l0_woT[:, :],
                                 start=True, stop=True).then_inc(w_made, 1)
                for n, (w, v) in enumerate(((l1_wk, l1_wq), (l1_wv, l1_woT))):
                    for m in range(KT):
                        for k in range(KT):
                            last = nc.tensor.matmul(bank[2 + n][:, m * H:(m + 1) * H], w[:, k, m * P:(m + 1) * P],
                                                    v[:, k, :], start=(k == 0), stop=(k == KT - 1))
                    last.then_inc(w_made, 1)

            @block.scalar
            def _(act):
                act.wait_ge(w_made, 3)
                nc.scalar.mul(l1_kq[:, :, :], bank[2][:, :].rearrange("p (k n) -> p k n", k=KT), 1.0 / 16).then_inc(w_kept, 1)
                act.wait_ge(w_made, 4)
                nc.scalar.copy(l1_vo[:, :, :], bank[3][:, :].rearrange("p (k n) -> p k n", k=KT)).then_inc(w_kept, 1)

            @block.vector
            def _(dve):
                nc.vector.memset(l0_wol[:, :], 0.0).then_inc(zeroed, 1)
                nc.vector.memset(key_bias[:, :, :], 0.0).then_inc(zeroed, 1)
                nc.vector.memset(v3[:, :, :, :, :], 0.0).then_inc(zeroed, 1)
                dve.wait_ge(zeroed, 3)
                for b in range(BT):
                    nc.vector.memset(v3[b * S:(b + 1) * S, :, :, b, L3_D:L3_D + 1], 1.0).then_inc(consts_made, 1)
                dve.wait_ge(w_made, 1)
                for b in range(BT):
                    nc.vector.tensor_copy(l0_wol[b * S:(b + 1) * S, b * S:(b + 1) * S],
                                          bank[0][b * S:(b + 1) * S, 0:S]).then_inc(w_kept, 1)
                dve.wait_ge(w_made, 2)
                nc.vector.tensor_tensor(l0_bias[:, :], bank[1][:, 0:S], l0_bo[:, :], ALU.add).then_inc(w_kept, 1)

        UNITS0 = SLOTS * BT
        x_ring = tb("x_ring", [P, SLOTS, H])
        c_ring = tb("c_ring", [P, SLOTS, H])
        stats = tb("stats", [P, SLOTS, 2, 6])
        moments = tb("moments", [P, SLOTS, 2, 2])
        rstd = tb("rstd", [P, SLOTS, 2])
        normed = tb("normed", [P, SLOTS, 2, H])
        xT0 = tb("xT0", [P, SLOTS, KT, BT, S])
        mn = tb("mn", [P, SLOTS, BT, H])
        mm = tb("mm", [P, SLOTS, H])
        vp0 = tb("vp0", [P, SLOTS, KT, BT, S])
        p0 = tb("p0", [P, UNITS0, KT, H])
        p0T = tb("p0T", [P, UNITS0, KT, H])
        nmax0 = tb("nmax0", [P, UNITS0, KT])
        sum0 = tb("sum0", [P, UNITS0, KT])
        rsum0 = tb("rsum0", [P, UNITS0, KT])

        x_in, c_in = sems("x_in", SLOTS), sems("c_in", SLOTS)
        zero0 = sem("zero0")
        with_eps = sems("with_eps_l0_", SLOTS)
        moments_made, rstd_made = sems("moments_made", SLOTS), sems("rstd_made", SLOTS)
        normed_made = sems("normed_made", SLOTS)
        xT_made, cT_made = sems("xT_made", SLOTS), sems("cT_made", SLOTS)
        xT_kept, cT_kept = sems("xT_kept", SLOTS), sems("cT_kept", SLOTS)
        vp_made, vp_kept = sems("vp_made", SLOTS), sems("vp_kept", SLOTS)
        m_made, m_kept = sems("m_made", SLOTS), sems("m_kept", SLOTS)
        s0_made, max0_made, p0_made = sems("s0_made", UNITS0), sems("max0_made", UNITS0), sems("p0_made", UNITS0)
        p0T_made, p0T_kept = sems("p0T_made", UNITS0), sems("p0T_kept", UNITS0)
        o0_made, o0_kept = sems("o0_made", UNITS0), sems("o0_kept", UNITS0)
        stats_made, rsum0_made = sems("stats_made", SLOTS), sems("rsum0_made", UNITS0)

        b_m, b_xT, b_cT, b_vp, b_p0T, b_o0 = (bank[k] for k in (0, 1, 2, 3, 6, 7))
        b_s0 = (bank[4], bank[5])

        with nc.Block() as block:
            @block.sync
            def _(sp):
                def trip(i):
                    for u in range(SLOTS):
                        n = SLOTS * i + u
                        if not is_first(i):
                            sp.wait_ge(normed_made[u], 2 * i)
                        if not is_first(i):
                            sp.wait_ge(xT_made[u], i)
                        if not is_first(i):
                            sp.wait_ge(cT_made[u], i)
                        if not is_first(i):
                            sp.wait_ge(vp_made[u], i)
                        sp.dma_start(x_ring[:, u, :], a["x"][n, :, :]).then_inc(x_in[u], 16)
                        sp.dma_start(c_ring[:, u, :], a["ctx"][n, :, :]).then_inc(c_in[u], 16)
                    if is_first(i):
                        for dst, src in middle_loads:
                            sp.dma_start(dst, src).then_inc(middle_in, 16)
                    if is_last(i):
                        for dst, src in late_loads:
                            sp.dma_start(dst, src).then_inc(late_in, 16)

                each_trip(sp, trip)

            @block.gpsimd
            def _(pool):
                nc.gpsimd.memset(mn[:, :, :, :], 0.0).then_inc(zero0, 1)
                def trip(i):
                    for u in range(SLOTS):
                        pool.wait_ge(moments_made[u], i + 1)
                        nc.gpsimd.tensor_tensor(rstd[:, u, :], moments[:, u, :, 1], l0_eps[:, :], ALU.add).then_inc(with_eps[u], 1)
                        pool.wait_ge(with_eps[u], i + 1)
                        nc.gpsimd.tensor_tensor(rstd[:, u, :], rstd[:, u, :], rsqrt_power[:, :], ALU.pow).then_inc(rstd_made[u], 1)

                each_trip(pool, trip)

            @block.tensor
            def _(pe):
                def prepare(i, u):
                    v = 1 - u
                    before = i + 1 if u else i
                    pe.wait_ge(x_in[u], 16 * (i + 1))
                    if u or not is_first(i):
                        pe.wait_ge(xT_kept[v], before)
                    for k in range(KT):
                        last = nc.tensor.transpose(b_xT[:, k * P:(k + 1) * P], x_ring[:, u, k * P:(k + 1) * P], ident[:, :])
                    last.then_inc(xT_made[u], 1)
                    pe.wait_ge(c_in[u], 16 * (i + 1))
                    if u or not is_first(i):
                        pe.wait_ge(cT_kept[v], before)
                    for k in range(KT):
                        last = nc.tensor.transpose(b_cT[:, k * P:(k + 1) * P], c_ring[:, u, k * P:(k + 1) * P], ident[:, :])
                    last.then_inc(cT_made[u], 1)
                    if u or not is_first(i):
                        pe.wait_ge(vp_kept[v], before)
                    for k in range(KT):
                        last = nc.tensor.matmul(b_vp[:, k * P:(k + 1) * P], c_ring[:, u, k * P:(k + 1) * P], l0_wol[:, :],
                                                start=True, stop=True)
                    last.then_inc(vp_made[u], 1)

                def project(i, u):
                    v = 1 - u
                    before = i + 1 if u else i
                    pe.wait_ge(normed_made[u], 2 * (i + 1))
                    if u or not is_first(i):
                        pe.wait_ge(m_kept[v], before)
                    nc.tensor.matmul(b_m[:, 0:H], l0_wn[:, :], normed[:, u, 0, :], start=True, stop=True)
                    nc.tensor.matmul(b_m[:, H:2 * H], l0_wm[:, :], normed[:, u, 1, :], start=True, stop=True)\
                        .then_inc(m_made[u], 1)

                def scores(i, k):
                    u, b = k // BT, k % BT
                    pe.wait_ge(m_kept[u], i + 1)
                    if k >= 2 or not is_first(i):
                        pe.wait_ge(p0_made[(k - 2) % UNITS0], i + 1 if k >= 2 else i)
                    for t in range(KT):
                        last = nc.tensor.matmul(b_s0[k % 2][:, t * H:(t + 1) * H], mn[:, u, b, t * P:(t + 1) * P],
                                                mm[:, u, :], start=True, stop=True)
                    last.then_inc(s0_made[k], 1)

                def turn(i, k):
                    pe.wait_ge(p0_made[k], i + 1)
                    if k >= 1 or not is_first(i):
                        pe.wait_ge(p0T_kept[(k - 1) % UNITS0], i + 1 if k >= 1 else i)
                    for s in range(KT):
                        for t in range(KT):
                            last = nc.tensor.transpose(b_p0T[:, s * H + t * P:s * H + (t + 1) * P],
                                                       p0[:, k, t, s * P:(s + 1) * P], ident[:, :])
                    last.then_inc(p0T_made[k], 1)

                def values(i, k):
                    u, b = k // BT, k % BT
                    pe.wait_ge(p0T_kept[k], i + 1)
                    pe.wait_ge(vp_kept[u], i + 1)
                    if k >= 1 or not is_first(i):
                        pe.wait_ge(o0_kept[(k - 1) % UNITS0], i + 1 if k >= 1 else i)
                    for t in range(KT):
                        for s in range(KT):
                            last = nc.tensor.matmul(b_o0[:, t * S:(t + 1) * S], p0T[:, k, s, t * P:(t + 1) * P],
                                                    vp0[:, u, s, b, :], start=(s == 0), stop=(s == KT - 1))
                    last.then_inc(o0_made[k], 1)

                def slot(i, k):
                    after = not is_last(i)
                    if k + 2 < UNITS0:
                        scores(i, k + 2)
                    elif after:
                        scores(i + 1, k + 2 - UNITS0)
                    if after and k % BT == 1:
                        project(i + 1, k // BT)
                    if k + 1 < UNITS0:
                        turn(i, k + 1)
                    elif after:
                        turn(i + 1, 0)
                    if k == 0:
                        prepare(i, 1)
                    if after and k == BT:
                        prepare(i + 1, 0)
                    values(i, k)

                def trip(i):
                    if is_first(i):
                        prepare(i, 0)
                        project(i, 0)
                        project(i, 1)
                        scores(i, 0)
                        scores(i, 1)
                        turn(i, 0)
                    for k in range(UNITS0):
                        slot(i, k)

                each_trip(pe, trip)

            @block.scalar
            def _(act):
                act.wait_ge(zero0, 1)

                def prepare(i, u):
                    n = SLOTS * i + u
                    act.wait_ge(cT_made[u], i + 1)
                    nc.scalar.copy(hT[:, n, :, :, 0, :], b_cT[:, 0:H].rearrange("p (k b s) -> p k b s", k=KT, b=BT))\
                        .then_inc(cT_kept[u], 1)
                    act.wait_ge(vp_made[u], i + 1)
                    if not is_first(i):
                        act.wait_ge(o0_made[BT * u + 1], i)
                    nc.scalar.copy(vp0[:, u, :, :, :], b_vp[:, 0:H].rearrange("p (k b s) -> p k b s", k=KT, b=BT))\
                        .then_inc(vp_kept[u], 1)

                def keep_projected(i, u):
                    act.wait_ge(m_made[u], i + 1)
                    if not is_first(i):
                        act.wait_ge(s0_made[BT * u + 1], i)
                    for b in range(BT):
                        rows = slice(b * S, (b + 1) * S)
                        nc.scalar.activation(mn[rows, u, b, :], b_m[rows, 0:H], ACT.Identity, bias=l0_bn[rows, 0:1])
                    nc.scalar.activation(mm[:, u, :], b_m[:, H:2 * H], ACT.Identity, bias=l0_bm[:, 0:1])\
                        .then_inc(m_kept[u], 1)

                def exps(i, k):
                    act.wait_ge(max0_made[k], i + 1)
                    if not is_first(i):
                        act.wait_ge(p0T_made[k], i)
                    if not is_first(i):
                        act.wait_ge(o0_kept[k], i)
                    for t in range(KT):
                        last = nc.scalar.activation(p0[:, k, t, :], b_s0[k % 2][:, t * H:(t + 1) * H], ACT.Exp,
                                                    bias=nmax0[:, k, t:t + 1], accum_out=sum0[:, k, t:t + 1])
                    last.then_inc(p0_made[k], 1)

                def slot(i, k):
                    after = not is_last(i)
                    if after and k % BT == 1:
                        keep_projected(i + 1, k // BT)
                    if k + 2 < UNITS0:
                        exps(i, k + 2)
                    elif after:
                        exps(i + 1, k + 2 - UNITS0)
                    if k == 0:
                        prepare(i, 1)
                    if after and k == BT:
                        prepare(i + 1, 0)

                def trip(i):
                    if is_first(i):
                        prepare(i, 0)
                        keep_projected(i, 0)
                        keep_projected(i, 1)
                        exps(i, 0)
                        exps(i, 1)
                    for k in range(UNITS0):
                        slot(i, k)

                each_trip(act, trip)

            @block.vector
            def _(dve):
                def statistics(i, u):
                    dve.wait_ge(x_in[u], 16 * (i + 1))
                    nc.vector.bn_stats(stats[:, u, 0, :], x_ring[:, u, :])
                    dve.wait_ge(c_in[u], 16 * (i + 1))
                    nc.vector.bn_stats(stats[:, u, 1, :], c_ring[:, u, :]).then_inc(stats_made[u], 1)
                    dve.wait_ge(stats_made[u], i + 1)
                    nc.vector.memset(scratch[:, :], 0.0)
                    nc.vector.bn_aggr(moments[:, u, 0, :], stats[:, u, 0, :])
                    nc.vector.bn_aggr(moments[:, u, 1, :], stats[:, u, 1, :]).then_inc(moments_made[u], 1)

                def normalise(i, u):
                    dve.wait_ge(rstd_made[u], i + 1)
                    if not is_first(i):
                        dve.wait_ge(m_made[u], i)
                    for j, ring in enumerate((x_ring, c_ring)):
                        nc.vector.tensor_scalar(normed[:, u, j, :], ring[:, u, :], moments[:, u, j, 0:1],
                                                rstd[:, u, j:j + 1], ALU.subtract, ALU.mult).then_inc(normed_made[u], 1)

                def keep_x(i, u):
                    dve.wait_ge(xT_made[u], i + 1)
                    if not is_first(i):
                        dve.wait_ge(o0_kept[BT * u + 1], i)
                    nc.vector.tensor_tensor(xT0[:, u, :, :, :].rearrange("p k b s -> p (k b) s"),
                                            b_xT[:, 0:H].rearrange("p (n s) -> p n s", s=S),
                                            spread(l0_bias[:, :], 1, KT * BT), ALU.add).then_inc(xT_kept[u], 1)

                def maxima(i, k):
                    dve.wait_ge(s0_made[k], i + 1)
                    nc.vector.reduce_max(nmax0[:, k, :], b_s0[k % 2][:, :].rearrange("p (t s) -> p t s", t=KT), AX.X,
                                         negate=True).then_inc(max0_made[k], 1)

                def keep_turned(i, k):
                    dve.wait_ge(p0T_made[k], i + 1)
                    if not is_first(i):
                        dve.wait_ge(o0_made[k], i)
                    nc.vector.tensor_copy(p0T[:, k, :, :].rearrange("p s t -> p (s t)"), b_p0T[:, :]).then_inc(p0T_kept[k], 1)

                def finish(i, k):
                    u, b = k // BT, k % BT
                    dve.wait_ge(p0_made[k], i + 1)
                    nc.vector.reciprocal(rsum0[:, k, :], sum0[:, k, :]).then_inc(rsum0_made[k], 1)
                    dve.wait_ge(rsum0_made[k], i + 1)
                    dve.wait_ge(o0_made[k], i + 1)
                    for t in range(KT):
                        last = nc.vector.scalar_tensor_tensor(
                            out=hT[:, SLOTS * i + u, t, b, 1, :], in0=b_o0[:, t * S:(t + 1) * S],
                            scalar=rsum0[:, k, t:t + 1], in1=xT0[:, u, t, b, :], op0=ALU.mult, op1=ALU.add)
                    last.then_inc(o0_kept[k], 1)

                def slot(i, k):
                    after = not is_last(i)
                    if k + 2 < UNITS0:
                        maxima(i, k + 2)
                    elif after:
                        maxima(i + 1, k + 2 - UNITS0)
                    if k + 1 < UNITS0:
                        keep_turned(i, k + 1)
                    elif after:
                        keep_turned(i + 1, 0)
                    if after and k % BT == 0:
                        statistics(i + 1, k // BT)
                    if k == 0:
                        keep_x(i, 1)
                    if after and k == BT:
                        keep_x(i + 1, 0)
                    finish(i, k)
                    if after and k % BT == 0:
                        normalise(i + 1, k // BT)

                def trip(i):
                    if is_first(i):
                        for u in range(SLOTS):
                            statistics(i, u)
                            normalise(i, u)
                        keep_x(i, 0)
                        maxima(i, 0)
                        maxima(i, 1)
                        keep_turned(i, 0)
                    for k in range(UNITS0):
                        slot(i, k)

                each_trip(dve, trip)

        next_phase()
        c_ring1 = tb("c_ring1", [P, SLOTS, KT, BT, S])
        x_ring1 = tb("x_ring1", [P, SLOTS, KT, BT, S])
        kp1 = tb("kp1", [P, SLOTS, KT, P])
        vp1 = tb("vp1", [P, SLOTS, H])
        nmax1 = tb("nmax1", [P, SLOTS])
        sum1 = tb("sum1", [P, SLOTS])
        rsum1 = tb("rsum1", [P, SLOTS])
        p1 = tb("p1", [P, SLOTS, P])
        p1T = tb("p1T", [P, SLOTS, P])

        zero1 = sem("zero1")
        biases_scaled, key_bias_made = sem("biases_scaled"), sem("key_bias_made")
        c1_in, x1_in = sems("c1_in", SLOTS), sems("x1_in", SLOTS)
        kp_made, kp_kept = sems("kp_made", SLOTS), sems("kp_kept", SLOTS)
        vp1_made, vp1_kept = sems("vp1_made", SLOTS), sems("vp1_kept", SLOTS)
        k3_made, k3_kept = sems("k3_made", SLOTS), sems("k3_kept", SLOTS)
        v3_made, v3_kept = sems("v3_made", SLOTS), sems("v3_kept", SLOTS)
        s1_made, max1_made, p1_made = sems("s1_made", SLOTS), sems("max1_made", SLOTS), sems("p1_made", SLOTS)
        p1_scaled, p1T_made, p1T_kept = sems("p1_scaled", SLOTS), sems("p1T_made", SLOTS), sems("p1T_kept", SLOTS)
        d1_made, x2_kept = sems("d1_made", SLOTS), sems("x2_kept", SLOTS)
        rsum1_made = sems("rsum1_made", SLOTS)

        b_kp, b_vp1, b_k3, b_v3, b_p1T, b_d1 = (bank[k] for k in (0, 1, 2, 3, 6, 7))
        b_s1 = (bank[4], bank[5])

        with nc.Block() as block:
            @block.sync
            def _(sp):
                def trip(i):
                    for u in range(SLOTS):
                        if not is_first(i):
                            sp.wait_ge(v3_made[u], i)
                        sp.dma_start(c_ring1[:, u, :, :, :], hT[:, SLOTS * i + u, :, :, 0, :]).then_inc(c1_in[u], 16)
                        if not is_first(i):
                            sp.wait_ge(s1_made[u], i)
                        sp.dma_start(x_ring1[:, u, :, :, :], hT[:, SLOTS * i + u, :, :, 1, :]).then_inc(x1_in[u], 16)

                each_trip(sp, trip)

            @block.gpsimd
            def _(pool):
                nc.gpsimd.memset(p1[:, :, :], 0.0).then_inc(zero1, 1)

            @block.tensor
            def _(pe):
                def project(i, u):
                    v = 1 - u
                    before = i + 1 if u else i
                    pe.wait_ge(c1_in[u], 16 * (i + 1))
                    if u or not is_first(i):
                        pe.wait_ge(kp_kept[v], before)
                    for m in range(KT):
                        for k in range(KT):
                            last = nc.tensor.matmul(b_kp[:, m * P:(m + 1) * P], l1_kq[:, k, m * P:(m + 1) * P],
                                                    c_ring1[:, u, k, :, :], start=(k == 0), stop=(k == KT - 1))
                    last.then_inc(kp_made[u], 1)
                    if u or not is_first(i):
                        pe.wait_ge(vp1_kept[v], before)
                    for k in range(KT):
                        last = nc.tensor.matmul(b_vp1[:, 0:H], c_ring1[:, u, k, :, :], l1_vo[:, k, :],
                                                start=(k == 0), stop=(k == KT - 1))
                    last.then_inc(vp1_made[u], 1)

                def project_l3(i, u):
                    v = 1 - u
                    before = i + 1 if u else i
                    if u or not is_first(i):
                        pe.wait_ge(k3_kept[v], before)
                    for k in range(KT):
                        last = nc.tensor.matmul(b_k3[:, 0:P], l3_wk[:, k, :], c_ring1[:, u, k, :, :],
                                                start=(k == 0), stop=(k == KT - 1))
                    last.then_inc(k3_made[u], 1)
                    if u or not is_first(i):
                        pe.wait_ge(v3_kept[v], before)
                    for k in range(KT):
                        last = nc.tensor.matmul(b_v3[:, 0:S], c_ring1[:, u, k, :, :], l3_wv[:, k, :],
                                                start=(k == 0), stop=(k == KT - 1))
                    last.then_inc(v3_made[u], 1)

                def scores(i, u):
                    pe.wait_ge(x1_in[u], 16 * (i + 1))
                    pe.wait_ge(kp_kept[u], i + 1)
                    if not is_first(i):
                        pe.wait_ge(p1_made[u], i)
                    for k in range(KT):
                        last = nc.tensor.matmul(b_s1[u][:, 0:P], x_ring1[:, u, k, :, :], kp1[:, u, k, :],
                                                start=(k == 0), stop=(k == KT - 1))
                    last.then_inc(s1_made[u], 1)

                def turn(i, u):
                    pe.wait_ge(p1_scaled[u], i + 1)
                    if u or not is_first(i):
                        pe.wait_ge(p1T_kept[1 - u], i + 1 if u else i)
                    nc.tensor.transpose(b_p1T[:, 0:P], p1[:, u, :], ident[:, :]).then_inc(p1T_made[u], 1)

                def values(i, u):
                    pe.wait_ge(p1T_kept[u], i + 1)
                    pe.wait_ge(vp1_kept[u], i + 1)
                    if u or not is_first(i):
                        pe.wait_ge(x2_kept[1 - u], i + 1 if u else i)
                    for m in range(KT):
                        last = nc.tensor.matmul(b_d1[:, m * P:(m + 1) * P], vp1[:, u, m * P:(m + 1) * P], p1T[:, u, :],
                                                start=True, stop=True)
                    last.then_inc(d1_made[u], 1)

                pe.wait_ge(middle_in, 16 * len(middle_loads))

                def trip(i):
                    if is_first(i):
                        project(i, 0)
                        project_l3(i, 0)
                        scores(i, 0)
                    project(i, 1)
                    project_l3(i, 1)
                    turn(i, 0)
                    scores(i, 1)
                    values(i, 0)
                    if not is_last(i):
                        project(i + 1, 0)
                        project_l3(i + 1, 0)
                    turn(i, 1)
                    if not is_last(i):
                        scores(i + 1, 0)
                    values(i, 1)

                each_trip(pe, trip)

            @block.scalar
            def _(act):
                act.wait_ge(zero1, 1)

                def keep(i, u):
                    act.wait_ge(kp_made[u], i + 1)
                    if not is_first(i):
                        act.wait_ge(s1_made[u], i)
                    nc.scalar.copy(kp1[:, u, :, :], b_kp[:, 0:H].rearrange("p (k n) -> p k n", k=KT)).then_inc(kp_kept[u], 1)
                    act.wait_ge(vp1_made[u], i + 1)
                    if not is_first(i):
                        act.wait_ge(d1_made[u], i)
                    nc.scalar.copy(vp1[:, u, :], b_vp1[:, 0:H]).then_inc(vp1_kept[u], 1)

                def keep_l3(i, u):
                    act.wait_ge(k3_made[u], i + 1)
                    nc.scalar.activation(k3T[:, SLOTS * i + u, :, :], b_k3[:, 0:P].rearrange("p (b s) -> p b s", b=BT),
                                         ACT.Identity, bias=l3_bk[:, 0:1]).then_inc(k3_kept[u], 1)

                def exps(i, u):
                    act.wait_ge(max1_made[u], i + 1)
                    if not is_first(i):
                        act.wait_ge(p1T_made[u], i)
                    for b in range(BT):
                        rows = slice(b * S, (b + 1) * S)
                        last = nc.scalar.activation(p1[rows, u, rows], b_s1[u][rows, rows], ACT.Exp,
                                                    bias=nmax1[rows, u:u + 1], accum_out=sum1[rows, u:u + 1])
                    last.then_inc(p1_made[u], 1)

                def keep_turned(i, u):
                    act.wait_ge(p1T_made[u], i + 1)
                    if not is_first(i):
                        act.wait_ge(d1_made[u], i)
                    nc.scalar.copy(p1T[:, u, :], b_p1T[:, 0:P]).then_inc(p1T_kept[u], 1)

                act.wait_ge(middle_in, 16 * len(middle_loads))
                nc.scalar.mul(l2_qb, l2_qb, 1.0 / L2_D).then_inc(biases_scaled, 1)
                nc.scalar.mul(l3_bq, l3_bq, L3_D ** -0.5).then_inc(biases_scaled, 1)

                def trip(i):
                    if is_first(i):
                        keep(i, 0)
                        keep_l3(i, 0)
                        exps(i, 0)
                    keep(i, 1)
                    keep_l3(i, 1)
                    keep_turned(i, 0)
                    exps(i, 1)
                    if not is_last(i):
                        keep(i + 1, 0)
                        keep_l3(i + 1, 0)
                    keep_turned(i, 1)
                    if not is_last(i):
                        exps(i + 1, 0)

                each_trip(act, trip)

            @block.vector
            def _(dve):
                def maxima(i, u):
                    dve.wait_ge(s1_made[u], i + 1)
                    for b in range(BT):
                        rows = slice(b * S, (b + 1) * S)
                        last = nc.vector.reduce_max(nmax1[rows, u:u + 1], b_s1[u][rows, rows], AX.X, negate=True)
                    last.then_inc(max1_made[u], 1)

                def scale(i, u):
                    dve.wait_ge(p1_made[u], i + 1)
                    nc.vector.reciprocal(rsum1[:, u:u + 1], sum1[:, u:u + 1]).then_inc(rsum1_made[u], 1)
                    dve.wait_ge(rsum1_made[u], i + 1)
                    nc.vector.tensor_scalar(p1[:, u, :], p1[:, u, :], rsum1[:, u:u + 1], l1_alpha[:, 0:1],
                                            ALU.mult, ALU.mult).then_inc(p1_scaled[u], 1)

                def keep_values(i, u):
                    dve.wait_ge(v3_made[u], i + 1)
                    for g in range(2):
                        for b in range(BT):
                            tokens = slice(b * S, (b + 1) * S)
                            last = nc.vector.tensor_tensor(
                                v3[g * S:(g + 1) * S, BT * (SLOTS * i + u) + b, :, g, 0:L3_D],
                                b_v3[tokens, 0:S].rearrange("p (j g d) -> p j g d", j=QUARTERS, g=2)[:, :, g, :],
                                l3_bv[tokens, :].rearrange("p (j g d) -> p j g d", j=QUARTERS, g=2)[:, :, g, :], ALU.add)
                    last.then_inc(v3_kept[u], 1)

                def finish(i, u):
                    dve.wait_ge(d1_made[u], i + 1)
                    nc.vector.tensor_tensor(hT[:, SLOTS * i + u, :, :, 1, :],
                                            b_d1[:, 0:H].rearrange("p (k b s) -> p k b s", k=KT, b=BT),
                                            hT[:, SLOTS * i + u, :, :, 1, :], ALU.add).then_inc(x2_kept[u], 1)

                dve.wait_ge(middle_in, 16 * len(middle_loads))

                def trip(i):
                    if is_first(i):
                        keep_values(i, 0)
                        maxima(i, 0)
                        scale(i, 0)
                    keep_values(i, 1)
                    maxima(i, 1)
                    finish(i, 0)
                    scale(i, 1)
                    if not is_last(i):
                        keep_values(i + 1, 0)
                        maxima(i + 1, 0)
                    finish(i, 1)
                    if not is_last(i):
                        scale(i + 1, 0)

                each_trip(dve, trip)
                dve.wait_ge(late_in, 16 * len(late_loads))
                nc.vector.tensor_scalar(key_bias[:, :, 0:S], key_flags[:, :, :], 0, MASKED,
                                        ALU.is_equal, ALU.mult).then_inc(key_bias_made, 1)

        next_phase()
        ring = tb("ring", [P, SLOTS, KT, BT, 2, S])
        x_flat = tb("x_flat", [P, SLOTS, KT, BT, S])
        kz = tb("kz", [P, SLOTS, KT, QUARTERS, BT * L2_KEYS])
        v2 = tb("v2", [P, SLOTS, BT, L2_HEADS, L2_D + 1])
        sq = tb("sq", [P, SLOTS, H])
        ssq = tb("ssq", [P, SLOTS])
        rms = tb("rms", [P, SLOTS])

        zero2 = sem("zero2")
        ring2_in = sems("ring2_in", SLOTS)
        k2_made, q2_made, v2_made = sems("k2_made", SLOTS), sems("q2_made", SLOTS), sems("v2_made", SLOTS)
        k2_kept, q2_kept, v2_kept = sems("k2_kept", SLOTS), sems("q2_kept", SLOTS), sems("v2_kept", SLOTS)
        s2_made, s2_kept, s2_less_max = sems("s2_made", UT), sems("s2_kept", UT), sems("s2_less_max", UT)
        p2_made, p2T_made, p2T_kept = sems("p2_made", UT), sems("p2T_made", UT), sems("p2T_kept", UT)
        o2_made, att_made = sems("o2_made", SLOTS), sems("att_made", SLOTS)
        attT_made, attT_kept = sems("attT_made", SLOTS), sems("attT_kept", SLOTS)
        x2tok_made, x2tok_kept = sems("x2tok_made", SLOTS), sems("x2tok_kept", SLOTS)
        ow_made, res_made, ssq_made, y_made = sems("ow_made", SLOTS), sems("res_made", SLOTS), sems("ssq_made", SLOTS), sems("y_made", SLOTS)
        yT_made, yT_kept = sems("yT_made", SLOTS), sems("yT_kept", SLOTS)
        AHEAD = 3
        with_eps = sems("with_eps_l2_", SLOTS)
        rms_made = sems("rms_made", SLOTS)
        nmax2_made, rsum2_made, with_x2 = sems("nmax2_made", UT), sems("rsum2_made", SLOTS), sems("with_x2", SLOTS)

        b_kv2, b_qx2, b_p2T, b_end2 = (bank[k] for k in (0, 1, 5, 7))
        b_s2 = (bank[3], bank[4])
        b_o2 = (bank[6], bank[2])

        with nc.Block() as block:
            @block.sync
            def _(sp):
                def trip(i):
                    for u in range(SLOTS):
                        if not is_first(i):
                            sp.wait_ge(x2tok_made[u], i)
                        sp.dma_start(ring[:, u, :, :, :, :], hT[:, SLOTS * i + u, :, :, :, :]).then_inc(ring2_in[u], 16)
                        sp.dma_start(x_flat[:, u, :, :, :], hT[:, SLOTS * i + u, :, :, 1, :]).then_inc(ring2_in[u], 16)

                each_trip(sp, trip)

            @block.gpsimd
            def _(pool):
                nc.gpsimd.memset(qz[:, :, :, :, :, :], 0.0).then_inc(zero2, 1)
                nc.gpsimd.memset(v2[:, :, :, :, :], 1.0).then_inc(zero2, 1)
                def trip(i):
                    for u in range(SLOTS):
                        pool.wait_ge(ssq_made[u], i + 1)
                        nc.gpsimd.tensor_tensor(rms[:, u:u + 1], ssq[:, u:u + 1], l2_eps[:, :], ALU.add).then_inc(with_eps[u], 1)
                        pool.wait_ge(with_eps[u], i + 1)
                        nc.gpsimd.tensor_tensor(rms[:, u:u + 1], rms[:, u:u + 1], rsqrt_power[:, 0:1], ALU.pow)\
                            .then_inc(rms_made[u], 1)

                each_trip(pool, trip)

            @block.tensor
            def _(pe):
                def project_keys(i, u):
                    pe.wait_ge(ring2_in[u], 32 * (i + 1))
                    if u or not is_first(i):
                        pe.wait_ge(v2_kept[1 - u], i + u)
                    for m in range(KT):
                        for k in range(KT):
                            last = nc.tensor.matmul(b_kv2[:, m * H:(m + 1) * H], l2_kw[:, k, m * P:(m + 1) * P],
                                                    ring[:, u, k, :, :, :], start=(k == 0), stop=(k == KT - 1))
                    last.then_inc(k2_made[u], 1)

                def project_queries(i, u):
                    if u or not is_first(i):
                        pe.wait_ge(x2tok_kept[1 - u], i + u)
                    for m in range(KT):
                        for k in range(KT):
                            last = nc.tensor.matmul(b_qx2[:, m * P:(m + 1) * P], l2_qw[:, k, m * P:(m + 1) * P],
                                                    ring[:, u, k, :, 1, :], start=(k == 0), stop=(k == KT - 1))
                    last.then_inc(q2_made[u], 1)

                def project_values(i, u):
                    pe.wait_ge(k2_kept[u], i + 1)
                    for b in range(BT):
                        for k in range(KT):
                            last = nc.tensor.matmul(b_kv2[:, b * H:(b + 1) * H], ring[:, u, k, b, :, :], l2_vw[:, k, :],
                                                    start=(k == 0), stop=(k == KT - 1))
                    last.then_inc(v2_made[u], 1)

                def stream(i, u):
                    pe.wait_ge(q2_kept[u], i + 1)
                    for k in range(KT):
                        last = nc.tensor.transpose(b_qx2[:, k * P:(k + 1) * P], x_flat[:, u, k, :, :], ident[:, :])
                    last.then_inc(x2tok_made[u], 1)

                def scores(i, k):
                    u, b, m = k // UT, k // KT % BT, k % KT
                    pe.wait_ge(k2_kept[u], i + 1)
                    pe.wait_ge(q2_kept[u], i + 1)
                    if k >= 2 or not is_first(i):
                        pe.wait_ge(s2_kept[(k - 2) % UT], reached(i, k - 2))
                    nc.tensor.matmul(b_s2[k % 2][:, :], qz[:, u, m, b, :, :], kz[:, u, m, :, b * L2_KEYS:(b + 1) * L2_KEYS],
                                     start=True, stop=True).then_inc(s2_made[k % UT], 1)

                def turn(i, k):
                    pe.wait_ge(p2_made[k % UT], reached(i, k))
                    if k >= 1 or not is_first(i):
                        pe.wait_ge(p2T_kept[(k - 1) % UT], reached(i, k - 1))
                    for h in range(QUARTERS):
                        last = nc.tensor.transpose(b_p2T[:, h * P:(h + 1) * P], sc[:, k % UT, h, :], ident[:, :])
                    last.then_inc(p2T_made[k % UT], 1)

                def values(i, k):
                    u, b, m = k // UT, k // KT % BT, k % KT
                    pe.wait_ge(p2T_kept[k % UT], reached(i, k))
                    if k % UT == 0:
                        pe.wait_ge(v2_kept[u], i + 1)
                        if not is_first(i):
                            pe.wait_ge(att_made[u], i)
                    for h in range(QUARTERS):
                        for g in range(2):
                            head = m * 2 * QUARTERS + g * QUARTERS + h
                            last = nc.tensor.matmul(b_o2[u][b * S:(b + 1) * S, head * (L2_D + 1):(head + 1) * (L2_D + 1)],
                                                    pT[:, k % UT, h, g * S:(g + 1) * S], v2[:, u, b, head, :],
                                                    start=True, stop=True)
                    if k % UT == UT - 1:
                        last.then_inc(o2_made[u], 1)

                def turn_output(i, u):
                    pe.wait_ge(att_made[u], i + 1)
                    if u or not is_first(i):
                        pe.wait_ge(yT_kept[1 - u], i + u)
                    for k in range(KT):
                        last = nc.tensor.transpose(b_end2[:, k * P:(k + 1) * P], att[:, u, k * P:(k + 1) * P], ident[:, :])
                    last.then_inc(attT_made[u], 1)

                def out_project(i, u):
                    pe.wait_ge(attT_kept[u], i + 1)
                    for k in range(KT):
                        last = nc.tensor.matmul(b_end2[:, 0:H], attT[:, u, k, :], l2_ow[:, k, :],
                                                start=(k == 0), stop=(k == KT - 1))
                    last.then_inc(ow_made[u], 1)

                def turn_y(i, u):
                    pe.wait_ge(y_made[u], i + 1)
                    for k in range(KT):
                        last = nc.tensor.transpose(b_end2[:, k * P:(k + 1) * P], res[:, u, k * P:(k + 1) * P], ident[:, :])
                    last.then_inc(yT_made[u], 1)

                def slot(i, k):
                    after = not is_last(i)
                    if k == 0:
                        project_values(i, 1)
                    if k == 1:
                        stream(i, 1)
                    if k + AHEAD < UNITS:
                        scores(i, k + AHEAD)
                    elif after:
                        scores(i + 1, k + AHEAD - UNITS)
                    if k == 1 and not is_first(i):
                        turn_output(i - 1, 1)
                    if k == 2 and not is_first(i):
                        out_project(i - 1, 1)
                    if k == 3 and not is_first(i):
                        turn_y(i - 1, 1)
                    if k == 5:
                        turn_output(i, 0)
                    if k == 6:
                        out_project(i, 0)
                    if k == 7:
                        turn_y(i, 0)
                    if k + 1 < UNITS:
                        turn(i, k + 1)
                    elif after:
                        turn(i + 1, 0)
                    if after and k == 2:
                        project_keys(i + 1, 0)
                    if after and k == 3:
                        project_queries(i + 1, 0)
                    if after and k == 4:
                        project_values(i + 1, 0)
                    if after and k == 5:
                        stream(i + 1, 0)
                    if after and k == 6:
                        project_keys(i + 1, 1)
                    if after and k == 7:
                        project_queries(i + 1, 1)
                    values(i, k)

                def trip(i):
                    if is_first(i):
                        project_keys(i, 0)
                        project_queries(i, 0)
                        scores(i, 0)
                        project_values(i, 0)
                        scores(i, 1)
                        stream(i, 0)
                        turn(i, 0)
                        scores(i, 2)
                        project_keys(i, 1)
                        project_queries(i, 1)
                    for k in range(UNITS):
                        slot(i, k)

                each_trip(pe, trip)
                turn_output(TRIPS - 1, 1)
                out_project(TRIPS - 1, 1)
                turn_y(TRIPS - 1, 1)

            @block.scalar
            def _(act):
                act.wait_ge(zero2, 2)

                def keep_queries(i, u):
                    act.wait_ge(q2_made[u], i + 1)
                    if not is_first(i):
                        act.wait_ge(s2_made[UT - 1], reached(i, UT * (u + 1) - 1 - UNITS))
                    for m in range(KT):
                        for g in range(2):
                            rows = slice(g * S, (g + 1) * S)
                            last = nc.scalar.activation(qz[rows, u, m, :, g, :],
                                                        b_qx2[rows, m * P:(m + 1) * P].rearrange("p (b s) -> p b s", b=BT),
                                                        ACT.Identity, bias=l2_qb[rows, m:m + 1], scale=1.0 / L2_D)
                    last.then_inc(q2_kept[u], 1)

                def keep_stream(i, u):
                    act.wait_ge(x2tok_made[u], i + 1)
                    nc.scalar.copy(x2tok[:, SLOTS * i + u, :], b_qx2[:, 0:H]).then_inc(x2tok_kept[u], 1)

                def exps(i, k):
                    act.wait_ge(s2_less_max[k % UT], reached(i, k))
                    nc.scalar.activation(sc[:, k % UT, :, :], sc[:, k % UT, :, :], ACT.Exp).then_inc(p2_made[k % UT], 1)

                def keep_turned(i, k):
                    act.wait_ge(p2T_made[k % UT], reached(i, k))
                    if k >= UT or not is_first(i):
                        act.wait_ge(o2_made[1 - k // UT], i + 1 if k >= UT else i)
                    nc.scalar.copy(pT[:, k % UT, :, :], b_p2T[:, :].rearrange("p (h n) -> p h n", h=QUARTERS)).then_inc(p2T_kept[k % UT], 1)

                def keep_output(i, u):
                    act.wait_ge(attT_made[u], i + 1)
                    if not is_first(i):
                        act.wait_ge(ow_made[u], i)
                    nc.scalar.copy(attT[:, u, :, :], b_end2[:, 0:H].rearrange("p (k n) -> p k n", k=KT)).then_inc(attT_kept[u], 1)

                def squares(i, u):
                    act.wait_ge(res_made[u], i + 1)
                    nc.scalar.activation(sq[:, u, :], res[:, u, :], ACT.Square, accum_out=ssq[:, u:u + 1]).then_inc(ssq_made[u], 1)

                def keep_y(i, u):
                    act.wait_ge(yT_made[u], i + 1)
                    for k in range(KT):
                        last = nc.scalar.mul(yT[:, k, bass.ds((SLOTS * i + u) * P, P)], b_end2[:, k * P:(k + 1) * P],
                                             l2_pw[:, k:k + 1])
                    last.then_inc(yT_kept[u], 1)

                def slot(i, k):
                    after = not is_last(i)
                    if k == 1:
                        keep_stream(i, 1)
                    if k == 1 and not is_first(i):
                        keep_output(i - 1, 1)
                    if k == 5:
                        keep_output(i, 0)
                    if k + 2 < UNITS:
                        exps(i, k + 2)
                    elif after:
                        exps(i + 1, k + 2 - UNITS)
                    if k == 2 and not is_first(i):
                        squares(i - 1, 1)
                    if k == 6:
                        squares(i, 0)
                    if k == 3 and not is_first(i):
                        keep_y(i - 1, 1)
                    if k == 7:
                        keep_y(i, 0)
                    if k + 1 < UNITS:
                        keep_turned(i, k + 1)
                    elif after:
                        keep_turned(i + 1, 0)
                    if after and k == 3:
                        keep_queries(i + 1, 0)
                    if after and k == 5:
                        keep_stream(i + 1, 0)
                    if after and k == 7:
                        keep_queries(i + 1, 1)

                def trip(i):
                    if is_first(i):
                        keep_queries(i, 0)
                        exps(i, 0)
                        keep_stream(i, 0)
                        exps(i, 1)
                        keep_turned(i, 0)
                        keep_queries(i, 1)
                    for k in range(UNITS):
                        slot(i, k)

                each_trip(act, trip)
                keep_output(TRIPS - 1, 1)
                squares(TRIPS - 1, 1)
                keep_y(TRIPS - 1, 1)

            @block.vector
            def _(dve):
                dve.wait_ge(zero2, 2)

                def keep_keys(i, u):
                    dve.wait_ge(k2_made[u], i + 1)
                    if not is_first(i):
                        dve.wait_ge(s2_made[UT - 1], reached(i, UT * (u + 1) - 1 - UNITS))
                    for m in range(KT):
                        last = nc.vector.scalar_tensor_tensor(
                            out=kz[:, u, m, :, :], in0=spread(b_kv2[:, m * H:(m + 1) * H], 1, QUARTERS),
                            scalar=l2_kb[:, m:m + 1], in1=spread(quarter_mask[:, :], 2, H), op0=ALU.add, op1=ALU.mult)
                    last.then_inc(k2_kept[u], 1)

                def keep_values(i, u):
                    dve.wait_ge(v2_made[u], i + 1)
                    if not is_first(i):
                        dve.wait_ge(o2_made[u], i)
                    nc.vector.tensor_tensor(v2[:, u, :, :, 0:L2_D],
                                            b_kv2[:, :].rearrange("p (b h d) -> p b h d", b=BT, h=L2_HEADS),
                                            spread(l2_vb[:, :].rearrange("p (h d) -> p h d", h=L2_HEADS), 1, BT),
                                            ALU.add).then_inc(v2_kept[u], 1)

                def less_max(i, k):
                    u, b = k // UT, k // KT % BT
                    dve.wait_ge(s2_made[k % UT], reached(i, k))
                    if k >= UT or not is_first(i):
                        dve.wait_ge(p2T_made[(k - UT) % UT], reached(i, k - UT))
                    nc.vector.tensor_tensor(sc[:, k % UT, :, :], b_s2[k % 2][:, :].rearrange("p (h n) -> p h n", h=QUARTERS),
                                            spread(key_bias[:, BT * (SLOTS * i + u) + b, :], 1, QUARTERS),
                                            ALU.add).then_inc(s2_kept[k % UT], 1)
                    dve.wait_ge(s2_kept[k % UT], reached(i, k))
                    nc.vector.reduce_max(nmax[:, k % UT, 0:QUARTERS], sc[:, k % UT, :, :], AX.X, negate=True)\
                        .then_inc(nmax2_made[k % UT], 1)
                    dve.wait_ge(nmax2_made[k % UT], reached(i, k))
                    nc.vector.tensor_tensor(sc[:, k % UT, :, :], sc[:, k % UT, :, :], spread(nmax[:, k % UT, 0:QUARTERS], 2, P),
                                            ALU.add).then_inc(s2_less_max[k % UT], 1)

                def normalise(i, u):
                    dve.wait_ge(o2_made[u], i + 1)
                    if not is_first(i):
                        dve.wait_ge(attT_made[u], i)
                    o = b_o2[u][:, 0:L2_HEADS * (L2_D + 1)].rearrange("p (h e) -> p h e", e=L2_D + 1)
                    nc.vector.reciprocal(rsum[:, u, 0:L2_HEADS], o[:, :, L2_D]).then_inc(rsum2_made[u], 1)
                    dve.wait_ge(rsum2_made[u], i + 1)
                    nc.vector.tensor_tensor(att[:, u, :].rearrange("p (h d) -> p h d", d=L2_D), o[:, :, 0:L2_D],
                                            spread(rsum[:, u, 0:L2_HEADS], 2, L2_D), ALU.mult).then_inc(att_made[u], 1)

                def residual(i, u):
                    dve.wait_ge(ow_made[u], i + 1)
                    if not is_first(i):
                        dve.wait_ge(yT_made[u], i)
                    dve.wait_ge(x2tok_kept[u], i + 1)
                    nc.vector.tensor_tensor(res[:, u, :], b_end2[:, 0:H], x2tok[:, SLOTS * i + u, :], ALU.add).then_inc(with_x2[u], 1)
                    dve.wait_ge(with_x2[u], i + 1)
                    nc.vector.tensor_tensor(res[:, u, :], res[:, u, :], l2_ob[:, :], ALU.add).then_inc(res_made[u], 1)

                def rms_norm(i, u):
                    dve.wait_ge(rms_made[u], i + 1)
                    nc.vector.tensor_scalar(res[:, u, :], res[:, u, :], rms[:, u:u + 1], float(H) ** 0.5,
                                            ALU.mult, ALU.mult).then_inc(y_made[u], 1)

                def slot(i, k):
                    after = not is_last(i)
                    if k == 0:
                        keep_values(i, 1)
                        if not is_first(i):
                            normalise(i - 1, 1)
                    if k == 4:
                        normalise(i, 0)
                    if k + AHEAD < UNITS:
                        less_max(i, k + AHEAD)
                    elif after:
                        less_max(i + 1, k + AHEAD - UNITS)
                    if k == 2 and not is_first(i):
                        residual(i - 1, 1)
                    if k == 3 and not is_first(i):
                        rms_norm(i - 1, 1)
                    if k == 6:
                        residual(i, 0)
                    if k == 7:
                        rms_norm(i, 0)
                    if after and k == 2:
                        keep_keys(i + 1, 0)
                    if after and k == 4:
                        keep_values(i + 1, 0)
                    if after and k == 6:
                        keep_keys(i + 1, 1)

                def trip(i):
                    if is_first(i):
                        keep_keys(i, 0)
                        less_max(i, 0)
                        keep_values(i, 0)
                        less_max(i, 1)
                        less_max(i, 2)
                        keep_keys(i, 1)
                    for k in range(UNITS):
                        slot(i, k)

                each_trip(dve, trip)
                normalise(TRIPS - 1, 1)
                residual(TRIPS - 1, 1)
                rms_norm(TRIPS - 1, 1)

        UPS = 4
        TOK = SLOTS * P
        next_phase()
        gT = tb("gT", [P, FT, TOK])
        up_made, gelu_made = sems("up_made", UPS), sems("gelu_made", UPS)
        down_made, x3_kept = sems("down_made", SLOTS), sems("x3_kept", SLOTS)
        x2b_made = sem("x2b_made")
        chain3 = sem("chain3")
        b_down = (bank[4], bank[5])

        with nc.Block() as block:
            @block.gpsimd
            def _(pool):
                with pool.Fori(0, TILES) as n:
                    nc.gpsimd.tensor_tensor(x2tok[:, n, :], x2tok[:, n, :], mlp_b2[:, :], ALU.add).then_inc(x2b_made, 1)

            @block.tensor
            def _(pe):
                def trip(i):
                    for j in range(UPS):
                        if not is_first(i):
                            pe.wait_ge(gelu_made[j], i)
                        for f in range(2):
                            for k in range(KT):
                                last = nc.tensor.matmul(bank[j][:, f * TOK:(f + 1) * TOK],
                                                        mlp_w1[:, k, (2 * j + f) * P:(2 * j + f + 1) * P],
                                                        yT[:, k, bass.ds(i * TOK, TOK)], start=(k == 0), stop=(k == KT - 1))
                        last.then_inc(up_made[j], 1)
                    for u in range(SLOTS):
                        if not is_first(i):
                            pe.wait_ge(x3_kept[u], i)
                        for f in range(FT):
                            if u == 0 and f % 2 == 0:
                                pe.wait_ge(gelu_made[f // 2], i + 1)
                            last = nc.tensor.matmul(b_down[u][:, 0:H], gT[:, f, u * P:(u + 1) * P], mlp_w2[:, f, :],
                                                    start=(f == 0), stop=(f == FT - 1))
                        last.then_inc(down_made[u], 1)

                each_trip(pe, trip)

            @block.scalar
            def _(act):
                def trip(i):
                    for j in range(UPS):
                        act.wait_ge(up_made[j], i + 1)
                        if not is_first(i):
                            act.wait_ge(down_made[1], i)
                        for f in range(2):
                            last = nc.scalar.activation(gT[:, 2 * j + f, :], bank[j][:, f * TOK:(f + 1) * TOK],
                                                        ACT.Gelu_apprx_tanh, bias=mlp_b1[:, 2 * j + f:2 * j + f + 1])
                        last.then_inc(gelu_made[j], 1)

                each_trip(act, trip)

            @block.vector
            def _(dve):
                def trip(i):
                    for u in range(SLOTS):
                        dve.wait_ge(down_made[u], i + 1)
                        dve.wait_ge(x2b_made, SLOTS * i + u + 1)
                        nc.vector.tensor_tensor(x3tok[:, SLOTS * i + u, :], b_down[u][:, 0:H], x2tok[:, SLOTS * i + u, :],
                                                ALU.add).then_inc(x3_kept[u], 1)

                each_trip(dve, trip)

        next_phase()
        x3_ring = tb("x3_ring", [P, SLOTS, H])
        x3T = tb("x3T", [P, SLOTS, KT, P])
        k3z = tb("k3z", [P, SLOTS, BT, KVH, S])
        v3z = tb("v3z", [P, SLOTS, BT, QUARTERS, 2 * (L3_D + 1)])
        stats3 = tb("stats3", [P, SLOTS, 6])
        moments3 = tb("moments3", [P, SLOTS, 2])
        rstd3 = tb("rstd3", [P, SLOTS])
        result = tb("result", [P, SLOTS, H])

        x3_in = sems("x3_in", SLOTS)
        k3z_made, v3z_made = sems("k3z_made", SLOTS), sems("v3z_made", SLOTS)
        x3T_made, x3T_kept = sems("x3T_made", SLOTS), sems("x3T_kept", SLOTS)
        q3_made, q3_kept = sems("q3_made", SLOTS), sems("q3_kept", SLOTS)
        s3_made, s3_kept, s3_less_max = sems("s3_made", UT), sems("s3_kept", UT), sems("s3_less_max", UT)
        p3_made, p3T_made, p3T_kept = sems("p3_made", UT), sems("p3T_made", UT), sems("p3T_kept", UT)
        o3_made, att3_made = sems("o3_made", SLOTS), sems("att3_made", SLOTS)
        att3T_made, att3T_kept = sems("att3T_made", SLOTS), sems("att3T_kept", SLOTS)
        wo3_made, wo3_kept = sems("wo3_made", SLOTS), sems("wo3_kept", SLOTS)
        result_made, stored = sems("result_made", SLOTS), sems("stored", SLOTS)
        with_eps = sems("with_eps_l3_", SLOTS)
        moments3_made, rstd3_made = sems("moments3_made", SLOTS), sems("rstd3_made", SLOTS)
        nmax3_made, rsum3_made = sems("nmax3_made", UT), sems("rsum3_made", SLOTS)
        with_bo, stats3_made, centred, scaled = (sems(n, SLOTS) for n in ("with_bo", "stats3_made", "centred", "scaled"))

        b_x3T, b_q3, b_p3T, b_end3 = (bank[k] for k in (0, 1, 5, 7))
        b_s3 = (bank[3], bank[4])
        b_o3 = (bank[6], bank[2])

        with nc.Block() as block:
            @block.sync
            def _(sp):
                def load(i, u):
                    if not is_first(i):
                        sp.wait_ge(x3T_made[u], i)
                    sp.dma_start(x3_ring[:, u, :], x3tok[:, SLOTS * i + u, :]).then_inc(x3_in[u], 16)

                def store(i, u):
                    sp.wait_ge(result_made[u], i + 1)
                    sp.dma_start(out[SLOTS * i + u, :, :], result[:, u, :]).then_inc(stored[u], 16)

                def trip(i):
                    if is_first(i):
                        load(i, 0)
                        load(i, 1)
                    if not is_last(i):
                        load(i + 1, 0)
                        load(i + 1, 1)
                    if not is_first(i):
                        store(i - 1, 1)
                    store(i, 0)

                each_trip(sp, trip)
                store(TRIPS - 1, 1)
                for u in range(SLOTS):
                    sp.wait_ge(stored[u], 16 * TRIPS)

            @block.gpsimd
            def _(pool):
                def keys(i, u):
                    if not is_first(i):
                        pool.wait_ge(s3_made[UT - 1], reached(i, UT * (u + 1) - 1 - UNITS))
                    for b in range(BT):
                        last = nc.gpsimd.tensor_tensor(k3z[:, u, b, :, :], spread(k3T[:, SLOTS * i + u, b, :], 1, KVH),
                                                       spread(kvh_mask[:, :], 2, S), ALU.mult)
                    last.then_inc(k3z_made[u], 1)

                def values(i, u):
                    if not is_first(i):
                        pool.wait_ge(o3_made[u], i)
                    nc.gpsimd.tensor_copy(v3z[:, u, :, :, :].rearrange("p b j e -> p (b j e)"),
                                          v3[:, bass.ds(BT * (SLOTS * i + u), BT), :, :, :].rearrange("p b j g e -> p (b j g e)"))\
                        .then_inc(v3z_made[u], 1)

                def deviation(i, u):
                    pool.wait_ge(moments3_made[u], i + 1)
                    nc.gpsimd.tensor_tensor(rstd3[:, u:u + 1], moments3[:, u, 1:2], l3_eps[:, :], ALU.add).then_inc(with_eps[u], 1)
                    pool.wait_ge(with_eps[u], i + 1)
                    nc.gpsimd.tensor_tensor(rstd3[:, u:u + 1], rstd3[:, u:u + 1], rsqrt_power[:, 0:1], ALU.pow)\
                        .then_inc(rstd3_made[u], 1)

                def trip(i):
                    if is_first(i):
                        for u in range(SLOTS):
                            keys(i, u)
                            values(i, u)
                    else:
                        deviation(i - 1, 1)
                    if not is_last(i):
                        keys(i + 1, 0)
                        values(i + 1, 0)
                        keys(i + 1, 1)
                    deviation(i, 0)
                    if not is_last(i):
                        values(i + 1, 1)

                each_trip(pool, trip)
                deviation(TRIPS - 1, 1)

            @block.tensor
            def _(pe):
                def turn_stream(i, u):
                    pe.wait_ge(x3_in[u], 16 * (i + 1))
                    if u or not is_first(i):
                        pe.wait_ge(x3T_kept[1 - u], i + u)
                    for k in range(KT):
                        last = nc.tensor.transpose(b_x3T[:, k * P:(k + 1) * P], x3_ring[:, u, k * P:(k + 1) * P], ident[:, :])
                    last.then_inc(x3T_made[u], 1)

                def project_queries(i, u):
                    pe.wait_ge(x3T_kept[u], i + 1)
                    if u or not is_first(i):
                        pe.wait_ge(q3_kept[1 - u], i + u)
                    for m in range(KT):
                        for k in range(KT):
                            last = nc.tensor.matmul(b_q3[:, m * P:(m + 1) * P], l3_wq[:, k, m * P:(m + 1) * P],
                                                    x3T[:, u, k, :], start=(k == 0), stop=(k == KT - 1))
                    last.then_inc(q3_made[u], 1)

                def scores(i, k):
                    u, b, m = k // UT, k // KT % BT, k % KT
                    pe.wait_ge(q3_kept[u], i + 1)
                    pe.wait_ge(k3z_made[u], i + 1)
                    if k >= 2 or not is_first(i):
                        pe.wait_ge(s3_kept[(k - 2) % UT], reached(i, k - 2))
                    nc.tensor.matmul(b_s3[k % 2][:, :], qz[:, u, m, b, :, :], k3z[:, u, b, :, :], start=True, stop=True)\
                        .then_inc(s3_made[k % UT], 1)

                def turn(i, k):
                    pe.wait_ge(p3_made[k % UT], reached(i, k))
                    if k >= 1 or not is_first(i):
                        pe.wait_ge(p3T_kept[(k - 1) % UT], reached(i, k - 1))
                    for h in range(QUARTERS):
                        last = nc.tensor.transpose(b_p3T[:, h * P:(h + 1) * P], sc[:, k % UT, h, :], ident[:, :])
                    last.then_inc(p3T_made[k % UT], 1)

                def values(i, k):
                    u, b, m = k // UT, k // KT % BT, k % KT
                    pe.wait_ge(p3T_kept[k % UT], reached(i, k))
                    if k % UT == 0:
                        pe.wait_ge(v3z_made[u], i + 1)
                        if not is_first(i):
                            pe.wait_ge(att3_made[u], i)
                    w = 2 * (L3_D + 1)
                    for j in range(QUARTERS):
                        for g in range(2):
                            at = ((2 * m + g) * QUARTERS + j) * w
                            last = nc.tensor.matmul(b_o3[u][b * S:(b + 1) * S, at:at + w], pT[:, k % UT, j, g * S:(g + 1) * S],
                                                    v3z[:, u, b, j, :], start=True, stop=True)
                    if k % UT == UT - 1:
                        last.then_inc(o3_made[u], 1)

                def turn_output(i, u):
                    pe.wait_ge(att3_made[u], i + 1)
                    if u or not is_first(i):
                        pe.wait_ge(wo3_kept[1 - u], i + u)
                    for k in range(KT):
                        last = nc.tensor.transpose(b_end3[:, k * P:(k + 1) * P], att[:, u, k * P:(k + 1) * P], ident[:, :])
                    last.then_inc(att3T_made[u], 1)

                def out_project(i, u):
                    pe.wait_ge(att3T_kept[u], i + 1)
                    for k in range(KT):
                        last = nc.tensor.matmul(b_end3[:, 0:H], attT[:, u, k, :], l3_wo[:, k, :],
                                                start=(k == 0), stop=(k == KT - 1))
                    last.then_inc(wo3_made[u], 1)

                def slot(i, k):
                    after = not is_last(i)
                    if k + AHEAD < UNITS:
                        scores(i, k + AHEAD)
                    elif after:
                        scores(i + 1, k + AHEAD - UNITS)
                    if k == 1 and not is_first(i):
                        turn_output(i - 1, 1)
                    if k == 2 and not is_first(i):
                        out_project(i - 1, 1)
                    if k == 5:
                        turn_output(i, 0)
                    if k == 6:
                        out_project(i, 0)
                    if k + 1 < UNITS:
                        turn(i, k + 1)
                    elif after:
                        turn(i + 1, 0)
                    if after and k == 2:
                        turn_stream(i + 1, 0)
                    if after and k == 3:
                        project_queries(i + 1, 0)
                    if after and k == 6:
                        turn_stream(i + 1, 1)
                    if after and k == 7:
                        project_queries(i + 1, 1)
                    values(i, k)

                def trip(i):
                    if is_first(i):
                        turn_stream(i, 0)
                        project_queries(i, 0)
                        turn_stream(i, 1)
                        scores(i, 0)
                        scores(i, 1)
                        project_queries(i, 1)
                        turn(i, 0)
                        scores(i, 2)
                    for k in range(UNITS):
                        slot(i, k)

                each_trip(pe, trip)
                turn_output(TRIPS - 1, 1)
                out_project(TRIPS - 1, 1)

            @block.scalar
            def _(act):
                def keep_stream(i, u):
                    act.wait_ge(x3T_made[u], i + 1)
                    if not is_first(i):
                        act.wait_ge(q3_made[u], i)
                    nc.scalar.copy(x3T[:, u, :, :], b_x3T[:, 0:H].rearrange("p (k n) -> p k n", k=KT)).then_inc(x3T_kept[u], 1)

                def keep_queries(i, u):
                    act.wait_ge(q3_made[u], i + 1)
                    if not is_first(i):
                        act.wait_ge(s3_made[UT - 1], reached(i, UT * (u + 1) - 1 - UNITS))
                    for m in range(KT):
                        for g in range(2):
                            rows = slice(g * S, (g + 1) * S)
                            last = nc.scalar.activation(qz[rows, u, m, :, g, :],
                                                        b_q3[rows, m * P:(m + 1) * P].rearrange("p (b s) -> p b s", b=BT),
                                                        ACT.Identity, bias=l3_bq[rows, m:m + 1], scale=L3_D ** -0.5)
                    last.then_inc(q3_kept[u], 1)

                def exps(i, k):
                    act.wait_ge(s3_less_max[k % UT], reached(i, k))
                    nc.scalar.activation(sc[:, k % UT, :, :], sc[:, k % UT, :, :], ACT.Exp).then_inc(p3_made[k % UT], 1)

                def keep_turned(i, k):
                    act.wait_ge(p3T_made[k % UT], reached(i, k))
                    if k >= UT or not is_first(i):
                        act.wait_ge(o3_made[1 - k // UT], i + 1 if k >= UT else i)
                    nc.scalar.copy(pT[:, k % UT, :, :], b_p3T[:, :].rearrange("p (h n) -> p h n", h=QUARTERS)).then_inc(p3T_kept[k % UT], 1)

                def keep_output(i, u):
                    act.wait_ge(att3T_made[u], i + 1)
                    if not is_first(i):
                        act.wait_ge(wo3_made[u], i)
                    nc.scalar.copy(attT[:, u, :, :], b_end3[:, 0:H].rearrange("p (k n) -> p k n", k=KT)).then_inc(att3T_kept[u], 1)

                def slot(i, k):
                    after = not is_last(i)
                    if k == 1 and not is_first(i):
                        keep_output(i - 1, 1)
                    if k == 5:
                        keep_output(i, 0)
                    if k + 2 < UNITS:
                        exps(i, k + 2)
                    elif after:
                        exps(i + 1, k + 2 - UNITS)
                    if k + 1 < UNITS:
                        keep_turned(i, k + 1)
                    elif after:
                        keep_turned(i + 1, 0)
                    if after and k == 2:
                        keep_stream(i + 1, 0)
                    if after and k == 3:
                        keep_queries(i + 1, 0)
                    if after and k == 6:
                        keep_stream(i + 1, 1)
                    if after and k == 7:
                        keep_queries(i + 1, 1)

                def trip(i):
                    if is_first(i):
                        keep_stream(i, 0)
                        keep_queries(i, 0)
                        keep_stream(i, 1)
                        exps(i, 0)
                        keep_queries(i, 1)
                        exps(i, 1)
                        keep_turned(i, 0)
                    for k in range(UNITS):
                        slot(i, k)

                each_trip(act, trip)
                keep_output(TRIPS - 1, 1)

            @block.vector
            def _(dve):
                def less_max(i, k):
                    u, b = k // UT, k // KT % BT
                    dve.wait_ge(s3_made[k % UT], reached(i, k))
                    if k >= UT or not is_first(i):
                        dve.wait_ge(p3T_made[(k - UT) % UT], reached(i, k - UT))
                    s = sc[:, k % UT, :, :].rearrange("p h (g n) -> p (h g) n", g=2)
                    nc.vector.tensor_tensor(s, b_s3[k % 2][:, :].rearrange("p (h n) -> p h n", h=KVH),
                                            spread(ff_mask[:, BT * (SLOTS * i + u) + b, :], 1, KVH),
                                            ALU.add).then_inc(s3_kept[k % UT], 1)
                    dve.wait_ge(s3_kept[k % UT], reached(i, k))
                    nc.vector.reduce_max(nmax[:, k % UT, :], s, AX.X, negate=True).then_inc(nmax3_made[k % UT], 1)
                    dve.wait_ge(nmax3_made[k % UT], reached(i, k))
                    nc.vector.tensor_tensor(s, s, spread(nmax[:, k % UT, :], 2, S), ALU.add).then_inc(s3_less_max[k % UT], 1)

                def normalise(i, u):
                    dve.wait_ge(o3_made[u], i + 1)
                    if not is_first(i):
                        dve.wait_ge(att3T_made[u], i)
                    o = b_o3[u][:, 0:GROUPS * KVH * (L3_D + 1)].rearrange("p (g h e) -> p h g e", g=GROUPS, e=L3_D + 1)
                    r = rsum[:, u, :].rearrange("p (h g) -> p h g", h=KVH)
                    nc.vector.reciprocal(r, o[:, :, :, L3_D]).then_inc(rsum3_made[u], 1)
                    dve.wait_ge(rsum3_made[u], i + 1)
                    nc.vector.tensor_tensor(att[:, u, :].rearrange("p (h g d) -> p h g d", h=KVH, g=GROUPS),
                                            o[:, :, :, 0:L3_D], spread(r, 3, L3_D), ALU.mult).then_inc(att3_made[u], 1)

                def finish(i, u):
                    dve.wait_ge(wo3_made[u], i + 1)
                    nc.vector.tensor_tensor(res[:, u, :], b_end3[:, 0:H], x3tok[:, SLOTS * i + u, :], ALU.add).then_inc(wo3_kept[u], 1)
                    dve.wait_ge(wo3_kept[u], i + 1)
                    nc.vector.tensor_tensor(res[:, u, :], res[:, u, :], l3_bo[:, :], ALU.add).then_inc(with_bo[u], 1)
                    dve.wait_ge(with_bo[u], i + 1)
                    nc.vector.bn_stats(stats3[:, u, :], res[:, u, :]).then_inc(stats3_made[u], 1)
                    dve.wait_ge(stats3_made[u], i + 1)
                    nc.vector.memset(scratch[:, :], 0.0)
                    nc.vector.bn_aggr(moments3[:, u, :], stats3[:, u, :]).then_inc(moments3_made[u], 1)
                    dve.wait_ge(rstd3_made[u], i + 1)
                    nc.vector.tensor_scalar(res[:, u, :], res[:, u, :], moments3[:, u, 0:1], rstd3[:, u:u + 1],
                                            ALU.subtract, ALU.mult).then_inc(centred[u], 1)
                    dve.wait_ge(centred[u], i + 1)
                    nc.vector.tensor_tensor(res[:, u, :], res[:, u, :], l3_gamma[:, :], ALU.mult).then_inc(scaled[u], 1)
                    dve.wait_ge(scaled[u], i + 1)
                    if not is_first(i):
                        dve.wait_ge(stored[u], 16 * i)
                    nc.vector.tensor_tensor(result[:, u, :], res[:, u, :], l3_beta[:, :], ALU.add).then_inc(result_made[u], 1)

                def slot(i, k):
                    after = not is_last(i)
                    if k == 0 and not is_first(i):
                        normalise(i - 1, 1)
                    if k == 4:
                        normalise(i, 0)
                    if k + AHEAD < UNITS:
                        less_max(i, k + AHEAD)
                    elif after:
                        less_max(i + 1, k + AHEAD - UNITS)
                    if k == 3 and not is_first(i):
                        finish(i - 1, 1)
                    if k == 7:
                        finish(i, 0)

                def trip(i):
                    if is_first(i):
                        less_max(i, 0)
                        less_max(i, 1)
                        less_max(i, 2)
                    for k in range(UNITS):
                        slot(i, k)

                each_trip(dve, trip)
                normalise(TRIPS - 1, 1)
                finish(TRIPS - 1, 1)

        if dump is not None:
            name, ap = dump
            taken = {"hT": hT, "k3T": k3T, "v3": v3, "x2tok": x2tok, "x3tok": x3tok, "yT": yT, "key_bias": key_bias}[name]
            dumped = sem("dumped")
            with nc.Block() as block:
                @block.sync
                def _(sp):
                    sp.dma_start(ap, taken[tuple([slice(None)] * len(taken.shape))]).then_inc(dumped, 16)
                    sp.wait_ge(dumped, 16)


def layouts(inputs):
    import numpy as np
    v = {k: np.asarray(x) for k, x in inputs.items()}
    cols = lambda w, n: np.ascontiguousarray(w.reshape(n, P).T)
    row = lambda w: w.reshape(1, -1)
    twice = lambda w: np.concatenate([w, w], axis=-1)
    kv_w = v["L2_xattn_kv_w"].reshape(H, H, 2)
    kv_b = v["L2_xattn_kv_b"].reshape(H, 2)
    grouped = lambda w: w.reshape(-1, KVH, GROUPS, L3_D).transpose(0, 2, 1, 3).reshape(w.shape)
    on_p = lambda w: np.concatenate([w, w], axis=0)
    rows = np.arange(P)
    columns_of = {
        "l2_qb": cols(v["L2_xattn_q_b"], KT), "l2_kb": cols(kv_b[:, 0], KT), "l2_pw": cols(v["L2_xattn_postnorm_w"], KT),
        "mlp_b1": cols(v["L2_xattn_mlp_b1"], FT), "l3_bq": cols(grouped(v["L3_xattn_bq"]), KT),
        "l3_bk": twice(v["L3_xattn_bk"]).reshape(P, 1),
        "quarter_mask": (rows[:, None] // L2_D % QUARTERS == np.arange(QUARTERS)).astype(np.float32),
        "kvh_mask": (rows[:, None] // L3_D % KVH == np.arange(KVH)).astype(np.float32),
    }
    rows_of = {
        "l1_alpha": v["L1_xattn_alpha"].reshape(1, 1), "l2_vb": row(kv_b[:, 1]), "l2_ob": row(v["L2_xattn_out_b"]),
        "mlp_b2": row(v["L2_xattn_mlp_b2"]), "l3_bv": row(v["L3_xattn_bv"]), "l3_bo": row(v["L3_xattn_bo"]),
        "l3_gamma": row(v["L3_xattn_gamma"]), "l3_beta": row(v["L3_xattn_beta"]),
    }
    d = {
        "x": v["x"].reshape(TILES, P, H), "ctx": v["ctx_2048"].reshape(TILES, P, H),
        "key_flags": v["mask_BxS2_ik0"].reshape(B, S), "ff_mask": v["mask_Bx1xSxS2_ff0"].reshape(B, S, S),
        "l0_wnT": v["L0_xattn_Wn"].T, "l0_wmT": v["L0_xattn_Wm"].T,
        "l0_first": np.concatenate([on_p(twice(v["L0_xattn_Wl"])), on_p(v["L0_xattn_Wo"].T), np.repeat(row(v["L0_xattn_bo"]), P, 0),
                                    on_p(v["L0_xattn_bl"].reshape(S, 1)), twice(v["L0_xattn_bn"]).reshape(P, 1),
                                    twice(v["L0_xattn_bm"]).reshape(P, 1)], axis=1),
        "l1_weights": np.stack([v["L1_xattn_w_k"], v["L1_xattn_w_q"], v["L1_xattn_w_v"], v["L1_xattn_w_o"].T]),
        "squares": np.stack([v["L2_xattn_q_w"], kv_w[:, :, 0], kv_w[:, :, 1], v["L2_xattn_out_w"],
                             grouped(v["L3_xattn_Wq"]), v["L3_xattn_Wo"]]),
        "mlp_w1": v["L2_xattn_mlp_w1"], "mlp_w2": v["L2_xattn_mlp_w2"],
        "l3_kvw": np.concatenate([twice(v["L3_xattn_Wk"]), v["L3_xattn_Wv"]], axis=1),
        "rows": np.concatenate([rows_of[name] for name in ROWS], axis=1),
        "columns": np.concatenate([columns_of[name] for name in COLUMNS], axis=1),
        "ident": np.eye(P, dtype=np.float32),
    }
    return {k: np.ascontiguousarray(x) for k, x in d.items()}


def kernel(**inputs):
    import concourse.bacc as bacc
    from concourse.bass_utils import run_bass_kernel_spmd

    nc = bacc.Bacc("TRN2", target_bir_lowering=False, num_devices=1)
    arrays = {f"in_{k}": x for k, x in layouts(inputs).items()}
    aps = {k[3:]: nc.dram_tensor(k, x.shape, mybir.dt.from_np(x.dtype), kind="ExternalInput").ap() for k, x in arrays.items()}
    out = nc.dram_tensor("out", (TILES, P, H), F32, kind="ExternalOutput").ap()
    build(nc, aps, out)
    r = run_bass_kernel_spmd(nc, [arrays], core_ids=[0])
    return r.results[0]["out"].reshape(B, S, H)
```

```python
from contextlib import ExitStack

import concourse.bass as bass
from concourse import mybir

F32 = mybir.dt.float32
I32 = mybir.dt.int32
ALU = mybir.AluOpType
ACT = mybir.ActivationFunctionType
AX = mybir.AxisListType

P = 128
B, S, H = 16, 64, 256
KT = H // P
SLOTS = 2
TILES = B * S // P
TRIPS = TILES // SLOTS
BT = P // S
L2_HEADS, L2_D = 16, 16
L2_KEYS = 2 * S
FF = 4 * H
FT = FF // P
KVH, GROUPS, L3_D = 8, 4, 8
L0_EPS, RMS_EPS, LN_EPS = 1e-5, 1e-6, 1e-6
MASKED = -1e30
UT = BT * KT
UNITS = SLOTS * UT
QUARTERS = 4


COLUMNS = {"l2_qb": KT, "l2_kb": KT, "l2_pw": KT, "mlp_b1": FT, "l3_bq": KT, "l3_bk": 1, "quarter_mask": QUARTERS, "kvh_mask": KVH}
ROWS = {"l1_alpha": 1, "l2_vb": H, "l2_ob": H, "mlp_b2": H, "l3_bv": KVH * L3_D, "l3_bo": H, "l3_gamma": H, "l3_beta": H}


def offset(widths, name):
    names = list(widths)
    return sum(widths[n] for n in names[:names.index(name)])


def each_trip(engine, body):
    body(0)
    with engine.Fori(1, TRIPS - 1) as i:
        body(i)
    body(TRIPS - 1)


def is_first(i):
    return isinstance(i, int) and i == 0


def is_last(i):
    return isinstance(i, int) and i == TRIPS - 1


def reached(i, k):
    return UNITS // UT * i + (k // UT + 1)


def spread(ap, axis, n):
    shape = list(ap.shape)
    return ap.unsqueeze(axis).broadcast_to(shape[:axis] + [n] + shape[axis:])


def build(nc, a, out):
    ctx = ExitStack()
    with ctx:
        phase_memory = [ctx.enter_context(ExitStack())]
        phase_sems = []

        def sb(name, shape, dt=F32):
            return ctx.enter_context(nc.sbuf_tensor(name, shape, dt))

        def tb(name, shape):
            return phase_memory[0].enter_context(nc.sbuf_tensor(name, shape, F32))

        def next_phase():
            phase_memory[0].close()
            phase_memory[0] = ctx.enter_context(ExitStack())
            nc.clear_and_free_semaphores(list(phase_sems))
            phase_sems.clear()
            nc.all_engine_barrier()

        def sem(name):
            phase_sems.append(nc.alloc_semaphore(name=name))
            return phase_sems[-1]

        def sems(name, n):
            return [sem(f"{name}{k}") for k in range(n)]

        bank = [ctx.enter_context(nc.psum_tensor(f"bank{k}", [P, 512], F32)) for k in range(8)]

        ident = sb("ident", [P, P])
        columns = sb("columns", [P, sum(COLUMNS.values())])
        rows_in = sb("rows_in", [P, sum(ROWS.values())])
        column = lambda name: columns[:, offset(COLUMNS, name):offset(COLUMNS, name) + COLUMNS[name]]
        row = lambda name: rows_in[:, offset(ROWS, name):offset(ROWS, name) + ROWS[name]]
        quarter_mask = column("quarter_mask")
        kvh_mask = column("kvh_mask")
        rsqrt_power = sb("rsqrt_power", [P, 2])
        l0_eps = sb("l0_eps", [P, 2])
        l2_eps = sb("l2_eps", [P, 1])
        l3_eps = sb("l3_eps", [P, 1])
        scratch = sb("scratch", [P, 1])
        l0_wn = sb("l0_wn", [P, P])
        l0_wm = sb("l0_wm", [P, P])
        l0_first = sb("l0_first", [P, P + S + S + 1 + 2])
        l0_wl2, l0_woT = l0_first[0:S, 0:P], l0_first[0:S, P:P + S]
        l0_bo = l0_first[:, P + S:P + 2 * S]
        l0_bl = l0_first[0:S, P + 2 * S:P + 2 * S + 1]
        l0_bn, l0_bm = (l0_first[:, P + 2 * S + j:P + 2 * S + j + 1] for j in (1, 2))
        l0_wol = sb("l0_wol", [P, P])
        l0_bias = sb("l0_bias", [P, S])
        l1_weights = sb("l1_weights", [P, 4, KT, H])
        l1_wk, l1_wq, l1_wv, l1_woT = (l1_weights[:, n, :, :] for n in range(4))
        l1_kq = sb("l1_kq", [P, KT, H])
        l1_vo = sb("l1_vo", [P, KT, H])
        l1_alpha = row("l1_alpha")
        squares = sb("squares", [P, 6, KT, H])
        l2_qw, l2_kw, l2_vw, l2_ow, l3_wq, l3_wo = (squares[:, n, :, :] for n in range(6))
        l2_qb, l2_kb, l2_pw, mlp_b1, l3_bq, l3_bk = (
            column(name) for name in ("l2_qb", "l2_kb", "l2_pw", "mlp_b1", "l3_bq", "l3_bk"))
        l2_vb, l2_ob, mlp_b2, l3_bv, l3_bo, l3_gamma, l3_beta = (
            row(name) for name in ("l2_vb", "l2_ob", "mlp_b2", "l3_bv", "l3_bo", "l3_gamma", "l3_beta"))
        mlp_w1 = sb("mlp_w1", [P, KT, FF])
        mlp_w2 = sb("mlp_w2", [P, FT, H])
        l3_kvw = sb("l3_kvw", [P, KT, P + S])
        l3_wk, l3_wv = l3_kvw[:, :, 0:P], l3_kvw[:, :, P:P + S]
        key_flags = sb("key_flags", [P, B, S], I32)
        key_bias = sb("key_bias", [P, B, L2_KEYS])
        ff_mask = sb("ff_mask", [P, B, S])

        qz = sb("qz", [P, SLOTS, KT, BT, 2, S])
        sc = sb("sc", [P, UT, QUARTERS, P])
        pT = sb("pT", [P, UT, QUARTERS, P])
        nmax = sb("nmax", [P, UT, KVH])
        rsum = sb("rsum", [P, SLOTS, H])
        attT = sb("attT", [P, SLOTS, H])
        ones2 = sb("ones2", [P, 2, 2, L2_D])
        ones3 = sb("ones3", [P, 2, 2, 2 * L3_D])
        res = sb("res", [P, SLOTS, H])

        ring = sb("ring", [P, SLOTS, KT, BT, 2, S])
        x_flat = sb("x_flat", [P, SLOTS, KT, BT, S])
        v2 = sb("v2", [P, SLOTS, BT, L2_HEADS // 2, 4, L2_D])
        x3_ring = sb("x3_ring", [P, SLOTS, H])
        k3z = sb("k3z", [P, SLOTS, BT, KVH, S])
        ring2_in = [nc.alloc_semaphore(name=f"ring2_in{u}") for u in range(SLOTS)]
        x3_in = [nc.alloc_semaphore(name=f"x3_in{u}") for u in range(SLOTS)]
        k3z_made = [nc.alloc_semaphore(name=f"k3z_made{u}") for u in range(SLOTS)]
        zero2 = nc.alloc_semaphore(name="zero2")

        hT = sb("hT", [P, TILES, KT, BT, 2, S])
        k3T = sb("k3T", [P, TILES, BT, S])
        v3 = sb("v3", [P, B, QUARTERS // 2, 4, 2 * L3_D])
        x_tok = sb("x_tok", [P, TILES, H])
        yT = sb("yT", [P, KT, TILES * P])

        k_p_n = lambda w: w.rearrange("(k p) n -> p k n", p=P)
        loads = [
            (ident[:, :], a["ident"]), (l0_first[:, :], a["l0_first"]),
        ]
        middle_loads = [
            (l1_weights[:, :, :, :], a["l1_weights"].rearrange("w (k p) n -> p w k n", p=P)),
            (columns[:, :], a["columns"]), (rows_in[:, :], a["rows"].partition_broadcast(P)),
            (l3_kvw[:, :, :], k_p_n(a["l3_kvw"])),
            (squares[:, :, :, :], a["squares"].rearrange("w (k p) n -> p w k n", p=P)),
        ]
        late_loads = [
            (key_flags[:, :, :], a["key_flags"].partition_broadcast(P)),
            (mlp_w1[:, :, :], k_p_n(a["mlp_w1"])), (mlp_w2[:, :, :], k_p_n(a["mlp_w2"])),
            (ff_mask[0:S, :, :], a["ff_mask"].rearrange("b q s -> q b s")),
            (ff_mask[S:P, :, :], a["ff_mask"].rearrange("b q s -> q b s")),
        ]
        middle_in = nc.alloc_semaphore(name="middle_in")
        late_in = nc.alloc_semaphore(name="late_in")
        early_in = sem("early_in")
        blocks_in = sem("blocks_in")
        blocks_zeroed = sem("blocks_zeroed")
        zeroed = sem("zeroed")
        w_made = sem("w_made")
        w_kept = sem("w_kept")
        ones_made = sem("ones_made")
        powers_made = sem("powers_made")
        tail_zeroed = sem("tail_zeroed")

        UNITS0 = SLOTS * BT
        x_ring = tb("x_ring", [P, SLOTS, H])
        c_ring = tb("c_ring", [P, SLOTS, H])
        stats = tb("stats", [P, SLOTS, 2, 6])
        moments = tb("moments", [P, SLOTS, 2, 2])
        rstd = tb("rstd", [P, SLOTS, 2])
        normed = tb("normed", [P, SLOTS, 2, H])
        xT0 = tb("xT0", [P, SLOTS, KT, BT, S])
        mn = tb("mn", [P, SLOTS, BT, H])
        mm = tb("mm", [P, SLOTS, H])
        vp0 = tb("vp0", [P, SLOTS, KT, BT, S])
        p0 = tb("p0", [P, UNITS0, KT, H])
        p0T = tb("p0T", [P, UNITS0, KT, H])
        nmax0 = tb("nmax0", [P, UNITS0, KT])
        sum0 = tb("sum0", [P, UNITS0, KT])
        warm = tb("warm", [P, 1])
        rsum0 = tb("rsum0", [P, UNITS0, KT])

        x_in, c_in = sems("x_in", SLOTS), sems("c_in", SLOTS)
        zero0 = sem("zero0")
        with_eps = sems("with_eps_l0_", SLOTS)
        moments_made, rstd_made = sems("moments_made", SLOTS), sems("rstd_made", SLOTS)
        normed_made = sems("normed_made", SLOTS)
        xT_made, cT_made = sems("xT_made", SLOTS), sems("cT_made", SLOTS)
        xT_kept, cT_kept = sems("xT_kept", SLOTS), sems("cT_kept", SLOTS)
        vp_made, vp_kept = sems("vp_made", SLOTS), sems("vp_kept", SLOTS)
        m_made, m_kept = sems("m_made", SLOTS), sems("m_kept", SLOTS)
        s0_made, max0_made, p0_made = sems("s0_made", UNITS0), sems("max0_made", UNITS0), sems("p0_made", UNITS0)
        p0T_made, p0T_kept = sems("p0T_made", UNITS0), sems("p0T_kept", UNITS0)
        o0_made, o0_kept = sems("o0_made", UNITS0), sems("o0_kept", UNITS0)
        stats_made, rsum0_made = sems("stats_made", SLOTS), sems("rsum0_made", UNITS0)

        b_m, b_xT, b_cT, b_vp, b_p0T, b_o0 = (bank[k] for k in (0, 1, 2, 3, 6, 7))
        b_s0 = (bank[4], bank[5])
        b_l1 = ((bank[1], bank[2]), (bank[3], bank[0]))
        l1_made, l1_kept = sem("l1_made"), sem("l1_kept")

        c_ring1 = tb("c_ring1", [P, SLOTS, KT, BT, S])
        x_ring1 = tb("x_ring1", [P, SLOTS, KT, BT, S])
        kp1 = tb("kp1", [P, SLOTS, KT, P])
        vp1 = tb("vp1", [P, SLOTS, H])
        nmax1 = tb("nmax1", [P, SLOTS])
        sum1 = tb("sum1", [P, SLOTS])
        rsum1 = tb("rsum1", [P, SLOTS])
        p1 = tb("p1", [P, SLOTS, P])
        p1T = tb("p1T", [P, SLOTS, P])

        zero1 = sem("zero1")
        biases_scaled, key_bias_made = sem("biases_scaled"), sem("key_bias_made")
        c1_in, x1_in = sems("c1_in", SLOTS), sems("x1_in", SLOTS)
        kp_made, kp_kept = sems("kp_made", SLOTS), sems("kp_kept", SLOTS)
        vp1_made, vp1_kept = sems("vp1_made", SLOTS), sems("vp1_kept", SLOTS)
        k3_made, k3_kept = sems("k3_made", SLOTS), sems("k3_kept", SLOTS)
        v3_made, v3_kept = sems("v3_made", SLOTS), sems("v3_kept", SLOTS)
        s1_made, max1_made, p1_made = sems("s1_made", SLOTS), sems("max1_made", SLOTS), sems("p1_made", SLOTS)
        p1_scaled, p1T_made, p1T_kept = sems("p1_scaled", SLOTS), sems("p1T_made", SLOTS), sems("p1T_kept", SLOTS)
        d1_made, x2_kept = sems("d1_made", SLOTS), sems("x2_kept", SLOTS)
        rsum1_made = sems("rsum1_made", SLOTS)

        b_kp, b_vp1, b_k3, b_v3, b_p1T, b_d1 = (bank[k] for k in (0, 1, 2, 3, 6, 7))
        b_s1 = (bank[4], bank[5])

        with nc.Block() as block:
            @block.sync
            def _(sp):
                for dst, src in loads:
                    sp.dma_start(dst, src).then_inc(early_in, 16)

                def trip(i):
                    for u in range(SLOTS):
                        n = SLOTS * i + u
                        if not is_first(i):
                            sp.wait_ge(normed_made[u], 2 * i)
                        if not is_first(i):
                            sp.wait_ge(xT_made[u], i)
                        if not is_first(i):
                            sp.wait_ge(cT_made[u], i)
                        if not is_first(i):
                            sp.wait_ge(vp_made[u], i)
                        sp.dma_start(x_ring[:, u, :], a["x"][n, :, :]).then_inc(x_in[u], 16)
                        sp.dma_start(c_ring[:, u, :], a["ctx"][n, :, :]).then_inc(c_in[u], 16)
                    if is_first(i):
                        sp.wait_ge(blocks_zeroed, 2)
                        for w, name in ((l0_wn, "l0_wnT"), (l0_wm, "l0_wmT")):
                            for b in range(BT):
                                sp.dma_start(w[b * S:(b + 1) * S, b * S:(b + 1) * S], a[name]).then_inc(blocks_in, 16)
                        for dst, src in middle_loads:
                            sp.dma_start(dst, src).then_inc(middle_in, 16)
                    if is_last(i):
                        for dst, src in late_loads:
                            sp.dma_start(dst, src).then_inc(late_in, 16)

                each_trip(sp, trip)

                def trip(i):
                    for u in range(SLOTS):
                        sp.wait_ge(cT_kept[u], i + 1)
                        if not is_first(i):
                            sp.wait_ge(v3_made[u], i)
                        sp.dma_start(c_ring1[:, u, :, :, :], hT[:, SLOTS * i + u, :, :, 0, :]).then_inc(c1_in[u], 16)
                        sp.wait_ge(o0_kept[BT * u + BT - 1], i + 1)
                        if not is_first(i):
                            sp.wait_ge(s1_made[u], i)
                        sp.dma_start(x_ring1[:, u, :, :, :], hT[:, SLOTS * i + u, :, :, 1, :]).then_inc(x1_in[u], 16)

                each_trip(sp, trip)
                for u in range(SLOTS):
                    sp.wait_ge(x2_kept[u], 1)
                    sp.dma_start(ring[:, u, :, :, :, :], hT[:, u, :, :, :, :]).then_inc(ring2_in[u], 16)
                    sp.dma_start(x_flat[:, u, :, :, :], hT[:, u, :, :, 1, :]).then_inc(ring2_in[u], 16)

            @block.gpsimd
            def _(pool):
                nc.gpsimd.memset(l0_wn[:, :], 0.0).then_inc(blocks_zeroed, 1)
                nc.gpsimd.memset(l0_wm[:, :], 0.0).then_inc(blocks_zeroed, 1)
                nc.gpsimd.memset(rsqrt_power[:, :], -0.5).then_inc(powers_made, 1)
                nc.gpsimd.memset(l0_eps[:, :], L0_EPS).then_inc(powers_made, 1)
                nc.gpsimd.memset(l2_eps[:, :], H * RMS_EPS).then_inc(powers_made, 1)
                nc.gpsimd.memset(l3_eps[:, :], LN_EPS).then_inc(powers_made, 1)
                nc.gpsimd.memset(mn[:, :, :, :], 0.0).then_inc(zero0, 1)
                nc.gpsimd.memset(p1[:, :, :], 0.0).then_inc(zero1, 1)
                pool.wait_ge(powers_made, 4)

                def trip(i):
                    for u in range(SLOTS):
                        pool.wait_ge(moments_made[u], i + 1)
                        nc.gpsimd.tensor_tensor(rstd[:, u, :], moments[:, u, :, 1], l0_eps[:, :], ALU.add).then_inc(with_eps[u], 1)
                        pool.wait_ge(with_eps[u], i + 1)
                        nc.gpsimd.tensor_tensor(rstd[:, u, :], rstd[:, u, :], rsqrt_power[:, :], ALU.pow).then_inc(rstd_made[u], 1)

                each_trip(pool, trip)
                nc.gpsimd.memset(v3[:, :, :, :, :], 0.0).then_inc(tail_zeroed, 1)
                nc.gpsimd.memset(key_bias[:, :, :], 0.0).then_inc(tail_zeroed, 1)

                nc.gpsimd.memset(qz[:, :, :, :, :, :], 0.0).then_inc(zero2, 1)
                nc.gpsimd.memset(v2[:, :, :, :, :, :], 0.0).then_inc(zero2, 1)

            @block.tensor
            def _(pe):
                pe.wait_ge(early_in, 16 * len(loads))
                nc.tensor.matmul(bank[0][:, 0:S], l0_wl2, l0_woT, start=True, stop=True).then_inc(w_made, 1)
                nc.tensor.matmul(bank[1][:, 0:S], l0_bl.broadcast_to([S, P]), l0_woT,
                                 start=True, stop=True).then_inc(w_made, 1)
                pe.wait_ge(w_kept, BT + 1)

                def prepare(i, u):
                    v = 1 - u
                    before = i + 1 if u else i
                    pe.wait_ge(x_in[u], 16 * (i + 1))
                    if u or not is_first(i):
                        pe.wait_ge(xT_kept[v], before)
                    for k in range(KT):
                        last = nc.tensor.transpose(b_xT[:, k * P:(k + 1) * P], x_ring[:, u, k * P:(k + 1) * P], ident[:, :])
                    last.then_inc(xT_made[u], 1)
                    pe.wait_ge(c_in[u], 16 * (i + 1))
                    if u or not is_first(i):
                        pe.wait_ge(cT_kept[v], before)
                    for k in range(KT):
                        last = nc.tensor.transpose(b_cT[:, k * P:(k + 1) * P], c_ring[:, u, k * P:(k + 1) * P], ident[:, :])
                    last.then_inc(cT_made[u], 1)
                    if u or not is_first(i):
                        pe.wait_ge(vp_kept[v], before)
                    for k in range(KT):
                        last = nc.tensor.matmul(b_vp[:, k * P:(k + 1) * P], c_ring[:, u, k * P:(k + 1) * P], l0_wol[:, :],
                                                start=True, stop=True)
                    last.then_inc(vp_made[u], 1)

                def project(i, u):
                    v = 1 - u
                    before = i + 1 if u else i
                    pe.wait_ge(normed_made[u], 2 * (i + 1))
                    if u or not is_first(i):
                        pe.wait_ge(m_kept[v], before)
                    nc.tensor.matmul(b_m[:, 0:H], l0_wn[:, :], normed[:, u, 0, :], start=True, stop=True)
                    nc.tensor.matmul(b_m[:, H:2 * H], l0_wm[:, :], normed[:, u, 1, :], start=True, stop=True)\
                        .then_inc(m_made[u], 1)

                def scores(i, k):
                    u, b = k // BT, k % BT
                    pe.wait_ge(m_kept[u], i + 1)
                    if k >= 2 or not is_first(i):
                        pe.wait_ge(p0_made[(k - 2) % UNITS0], i + 1 if k >= 2 else i)
                    for t in range(KT):
                        last = nc.tensor.matmul(b_s0[k % 2][:, t * H:(t + 1) * H], mn[:, u, b, t * P:(t + 1) * P],
                                                mm[:, u, :], start=True, stop=True)
                    last.then_inc(s0_made[k], 1)

                def turn(i, k):
                    pe.wait_ge(p0_made[k], i + 1)
                    if k >= 1 or not is_first(i):
                        pe.wait_ge(p0T_kept[(k - 1) % UNITS0], i + 1 if k >= 1 else i)
                    for s in range(KT):
                        for t in range(KT):
                            last = nc.tensor.transpose(b_p0T[:, s * H + t * P:s * H + (t + 1) * P],
                                                       p0[:, k, t, s * P:(s + 1) * P], ident[:, :])
                    last.then_inc(p0T_made[k], 1)

                def values(i, k):
                    u, b = k // BT, k % BT
                    pe.wait_ge(p0T_kept[k], i + 1)
                    pe.wait_ge(vp_kept[u], i + 1)
                    if k >= 1 or not is_first(i):
                        pe.wait_ge(o0_kept[(k - 1) % UNITS0], i + 1 if k >= 1 else i)
                    for t in range(KT):
                        for s in range(KT):
                            last = nc.tensor.matmul(b_o0[:, t * S:(t + 1) * S], p0T[:, k, s, t * P:(t + 1) * P],
                                                    vp0[:, u, s, b, :], start=(s == 0), stop=(s == KT - 1))
                    last.then_inc(o0_made[k], 1)

                def products_for_l1():
                    pe.wait_ge(middle_in, 16 * len(middle_loads))
                    pe.wait_ge(xT_kept[SLOTS - 1], TRIPS)
                    pe.wait_ge(cT_kept[SLOTS - 1], TRIPS)
                    pe.wait_ge(vp_kept[SLOTS - 1], TRIPS)
                    pe.wait_ge(m_kept[SLOTS - 1], TRIPS)
                    for (w, v), banks in zip(((l1_wk, l1_wq), (l1_wv, l1_woT)), b_l1):
                        for m in range(KT):
                            for k in range(KT):
                                last = nc.tensor.matmul(banks[m][:, H:2 * H], w[:, k, m * P:(m + 1) * P],
                                                        v[:, k, :], start=(k == 0), stop=(k == KT - 1))
                        last.then_inc(l1_made, 1)

                def slot(i, k):
                    after = not is_last(i)
                    if k + 2 < UNITS0:
                        scores(i, k + 2)
                    elif after:
                        scores(i + 1, k + 2 - UNITS0)
                    if after and k % BT == 1:
                        project(i + 1, k // BT)
                    if k + 1 < UNITS0:
                        turn(i, k + 1)
                    elif after:
                        turn(i + 1, 0)
                    if k == 0:
                        prepare(i, 1)
                    if after and k == BT:
                        prepare(i + 1, 0)
                    values(i, k)
                    if is_last(i) and k == BT:
                        products_for_l1()

                def trip(i):
                    if is_first(i):
                        prepare(i, 0)
                        pe.wait_ge(blocks_in, 16 * 2 * BT)
                        project(i, 0)
                        scores(i, 0)
                        project(i, 1)
                        scores(i, 1)
                        turn(i, 0)
                    for k in range(UNITS0):
                        slot(i, k)

                each_trip(pe, trip)

                def project(i, u):
                    v = 1 - u
                    before = i + 1 if u else i
                    pe.wait_ge(c1_in[u], 16 * (i + 1))
                    if u or not is_first(i):
                        pe.wait_ge(kp_kept[v], before)
                    for m in range(KT):
                        for k in range(KT):
                            last = nc.tensor.matmul(b_kp[:, m * P:(m + 1) * P], l1_kq[:, k, m * P:(m + 1) * P],
                                                    c_ring1[:, u, k, :, :], start=(k == 0), stop=(k == KT - 1))
                    last.then_inc(kp_made[u], 1)
                    if u or not is_first(i):
                        pe.wait_ge(vp1_kept[v], before)
                    for k in range(KT):
                        last = nc.tensor.matmul(b_vp1[:, 0:H], c_ring1[:, u, k, :, :], l1_vo[:, k, :],
                                                start=(k == 0), stop=(k == KT - 1))
                    last.then_inc(vp1_made[u], 1)

                def project_l3(i, u):
                    v = 1 - u
                    before = i + 1 if u else i
                    if u or not is_first(i):
                        pe.wait_ge(k3_kept[v], before)
                    for k in range(KT):
                        last = nc.tensor.matmul(b_k3[:, 0:P], l3_wk[:, k, :], c_ring1[:, u, k, :, :],
                                                start=(k == 0), stop=(k == KT - 1))
                    last.then_inc(k3_made[u], 1)
                    if u or not is_first(i):
                        pe.wait_ge(v3_kept[v], before)
                    for k in range(KT):
                        last = nc.tensor.matmul(b_v3[:, 0:S], c_ring1[:, u, k, :, :], l3_wv[:, k, :],
                                                start=(k == 0), stop=(k == KT - 1))
                    last.then_inc(v3_made[u], 1)

                def scores(i, u):
                    pe.wait_ge(x1_in[u], 16 * (i + 1))
                    pe.wait_ge(kp_kept[u], i + 1)
                    if not is_first(i):
                        pe.wait_ge(p1_made[u], i)
                    else:
                        pe.wait_ge(p0_made[UNITS0 - SLOTS + u], TRIPS)
                    for k in range(KT):
                        last = nc.tensor.matmul(b_s1[u][:, 0:P], x_ring1[:, u, k, :, :], kp1[:, u, k, :],
                                                start=(k == 0), stop=(k == KT - 1))
                    last.then_inc(s1_made[u], 1)

                def turn(i, u):
                    pe.wait_ge(p1_scaled[u], i + 1)
                    if u or not is_first(i):
                        pe.wait_ge(p1T_kept[1 - u], i + 1 if u else i)
                    else:
                        pe.wait_ge(p0T_kept[UNITS0 - 1], TRIPS)
                    nc.tensor.transpose(b_p1T[:, 0:P], p1[:, u, :], ident[:, :]).then_inc(p1T_made[u], 1)

                def values(i, u):
                    pe.wait_ge(p1T_kept[u], i + 1)
                    pe.wait_ge(vp1_kept[u], i + 1)
                    if u or not is_first(i):
                        pe.wait_ge(x2_kept[1 - u], i + 1 if u else i)
                    else:
                        pe.wait_ge(o0_kept[UNITS0 - 1], TRIPS)
                    for m in range(KT):
                        last = nc.tensor.matmul(b_d1[:, m * P:(m + 1) * P], vp1[:, u, m * P:(m + 1) * P], p1T[:, u, :],
                                                start=True, stop=True)
                    last.then_inc(d1_made[u], 1)

                pe.wait_ge(middle_in, 16 * len(middle_loads))

                pe.wait_ge(l1_kept, 2 * KT)

                def trip(i):
                    if is_first(i):
                        project(i, 0)
                        project_l3(i, 0)
                        scores(i, 0)
                    project(i, 1)
                    project_l3(i, 1)
                    turn(i, 0)
                    scores(i, 1)
                    values(i, 0)
                    if not is_last(i):
                        project(i + 1, 0)
                        project_l3(i + 1, 0)
                    turn(i, 1)
                    if not is_last(i):
                        scores(i + 1, 0)
                    values(i, 1)

                each_trip(pe, trip)

            @block.scalar
            def _(act):
                act.wait_ge(zero0, 1)
                act.wait_ge(powers_made, 4)
                nc.scalar.activation(warm[:, :], l2_eps[:, :], ACT.Exp)
                act.wait_ge(early_in, 16 * len(loads))

                def prepare(i, u):
                    n = SLOTS * i + u
                    act.wait_ge(cT_made[u], i + 1)
                    nc.scalar.copy(hT[:, n, :, :, 0, :], b_cT[:, 0:H].rearrange("p (k b s) -> p k b s", k=KT, b=BT))\
                        .then_inc(cT_kept[u], 1)
                    act.wait_ge(vp_made[u], i + 1)
                    if not is_first(i):
                        act.wait_ge(o0_made[BT * u + 1], i)
                    nc.scalar.copy(vp0[:, u, :, :, :], b_vp[:, 0:H].rearrange("p (k b s) -> p k b s", k=KT, b=BT))\
                        .then_inc(vp_kept[u], 1)

                def keep_projected(i, u):
                    act.wait_ge(m_made[u], i + 1)
                    if not is_first(i):
                        act.wait_ge(s0_made[BT * u + 1], i)
                    for b in range(BT):
                        rows = slice(b * S, (b + 1) * S)
                        nc.scalar.activation(mn[rows, u, b, :], b_m[rows, 0:H], ACT.Identity, bias=l0_bn[rows, 0:1])
                    nc.scalar.activation(mm[:, u, :], b_m[:, H:2 * H], ACT.Identity, bias=l0_bm[:, 0:1])\
                        .then_inc(m_kept[u], 1)

                def exps(i, k):
                    act.wait_ge(max0_made[k], i + 1)
                    if not is_first(i):
                        act.wait_ge(p0T_made[k], i)
                    if not is_first(i):
                        act.wait_ge(o0_kept[k], i)
                    for t in range(KT):
                        last = nc.scalar.activation(p0[:, k, t, :], b_s0[k % 2][:, t * H:(t + 1) * H], ACT.Exp,
                                                    bias=nmax0[:, k, t:t + 1], accum_out=sum0[:, k, t:t + 1])
                    last.then_inc(p0_made[k], 1)

                def slot(i, k):
                    after = not is_last(i)
                    if after and k % BT == 1:
                        keep_projected(i + 1, k // BT)
                    if k + 2 < UNITS0:
                        exps(i, k + 2)
                    elif after:
                        exps(i + 1, k + 2 - UNITS0)
                    if k == 0:
                        prepare(i, 1)
                    if after and k == BT:
                        prepare(i + 1, 0)

                def trip(i):
                    if is_first(i):
                        prepare(i, 0)
                        keep_projected(i, 0)
                        exps(i, 0)
                        keep_projected(i, 1)
                        exps(i, 1)
                    for k in range(UNITS0):
                        slot(i, k)

                each_trip(act, trip)
                act.wait_ge(l1_made, 1)
                for m in range(KT):
                    nc.scalar.mul(l1_kq[:, m, :], b_l1[0][m][:, H:2 * H], 1.0 / 16).then_inc(l1_kept, 1)
                act.wait_ge(l1_made, 2)
                for m in range(KT):
                    nc.scalar.copy(l1_vo[:, m, :], b_l1[1][m][:, H:2 * H]).then_inc(l1_kept, 1)

                act.wait_ge(zero1, 1)

                def keep(i, u):
                    act.wait_ge(kp_made[u], i + 1)
                    if not is_first(i):
                        act.wait_ge(s1_made[u], i)
                    nc.scalar.copy(kp1[:, u, :, :], b_kp[:, 0:H].rearrange("p (k n) -> p k n", k=KT)).then_inc(kp_kept[u], 1)
                    act.wait_ge(vp1_made[u], i + 1)
                    if not is_first(i):
                        act.wait_ge(d1_made[u], i)
                    nc.scalar.copy(vp1[:, u, :], b_vp1[:, 0:H]).then_inc(vp1_kept[u], 1)

                def keep_l3(i, u):
                    act.wait_ge(k3_made[u], i + 1)
                    nc.scalar.activation(k3T[:, SLOTS * i + u, :, :], b_k3[:, 0:P].rearrange("p (b s) -> p b s", b=BT),
                                         ACT.Identity, bias=l3_bk[:, 0:1]).then_inc(k3_kept[u], 1)

                def exps(i, u):
                    act.wait_ge(max1_made[u], i + 1)
                    if not is_first(i):
                        act.wait_ge(p1T_made[u], i)
                    for b in range(BT):
                        rows = slice(b * S, (b + 1) * S)
                        last = nc.scalar.activation(p1[rows, u, rows], b_s1[u][rows, rows], ACT.Exp,
                                                    bias=nmax1[rows, u:u + 1], accum_out=sum1[rows, u:u + 1])
                    last.then_inc(p1_made[u], 1)

                def keep_turned(i, u):
                    act.wait_ge(p1T_made[u], i + 1)
                    if not is_first(i):
                        act.wait_ge(d1_made[u], i)
                    nc.scalar.copy(p1T[:, u, :], b_p1T[:, 0:P]).then_inc(p1T_kept[u], 1)

                act.wait_ge(middle_in, 16 * len(middle_loads))
                nc.scalar.mul(l2_qb, l2_qb, 1.0 / L2_D).then_inc(biases_scaled, 1)
                nc.scalar.mul(l3_bq, l3_bq, L3_D ** -0.5).then_inc(biases_scaled, 1)

                def trip(i):
                    if is_first(i):
                        keep(i, 0)
                        keep_l3(i, 0)
                        exps(i, 0)
                    keep(i, 1)
                    keep_l3(i, 1)
                    keep_turned(i, 0)
                    exps(i, 1)
                    if not is_last(i):
                        keep(i + 1, 0)
                        keep_l3(i + 1, 0)
                    keep_turned(i, 1)
                    if not is_last(i):
                        exps(i + 1, 0)

                each_trip(act, trip)

            @block.vector
            def _(dve):
                nc.vector.memset(l0_wol[:, :], 0.0).then_inc(zeroed, 1)
                nc.vector.memset(ones2[:, :, :, :], 0.0).then_inc(zeroed, 1)
                nc.vector.memset(ones3[:, :, :, :], 0.0).then_inc(zeroed, 1)
                dve.wait_ge(zeroed, 3)
                for odd in range(2):
                    nc.vector.memset(ones2[:, odd, odd, :], 1.0).then_inc(ones_made, 1)
                    for g in range(2):
                        nc.vector.memset(ones3[g * S:(g + 1) * S, odd, odd, g * L3_D:(g + 1) * L3_D], 1.0)\
                            .then_inc(ones_made, 1)
                dve.wait_ge(w_made, 1)
                for b in range(BT):
                    nc.vector.tensor_copy(l0_wol[b * S:(b + 1) * S, b * S:(b + 1) * S],
                                          bank[0][b * S:(b + 1) * S, 0:S]).then_inc(w_kept, 1)
                dve.wait_ge(w_made, 2)
                nc.vector.tensor_tensor(l0_bias[:, :], bank[1][:, 0:S], l0_bo, ALU.add).then_inc(w_kept, 1)
                dve.wait_ge(w_kept, BT + 1)

                def statistics(i, u):
                    dve.wait_ge(x_in[u], 16 * (i + 1))
                    nc.vector.bn_stats(stats[:, u, 0, :], x_ring[:, u, :])
                    dve.wait_ge(c_in[u], 16 * (i + 1))
                    nc.vector.bn_stats(stats[:, u, 1, :], c_ring[:, u, :]).then_inc(stats_made[u], 1)
                    dve.wait_ge(stats_made[u], i + 1)
                    nc.vector.memset(scratch[:, :], 0.0)
                    nc.vector.bn_aggr(moments[:, u, 0, :], stats[:, u, 0, :])
                    nc.vector.bn_aggr(moments[:, u, 1, :], stats[:, u, 1, :]).then_inc(moments_made[u], 1)

                def normalise(i, u):
                    dve.wait_ge(rstd_made[u], i + 1)
                    if not is_first(i):
                        dve.wait_ge(m_made[u], i)
                    for j, ring in enumerate((x_ring, c_ring)):
                        nc.vector.tensor_scalar(normed[:, u, j, :], ring[:, u, :], moments[:, u, j, 0:1],
                                                rstd[:, u, j:j + 1], ALU.subtract, ALU.mult).then_inc(normed_made[u], 1)

                def keep_x(i, u):
                    dve.wait_ge(xT_made[u], i + 1)
                    if not is_first(i):
                        dve.wait_ge(o0_kept[BT * u + 1], i)
                    nc.vector.tensor_tensor(xT0[:, u, :, :, :].rearrange("p k b s -> p (k b) s"),
                                            b_xT[:, 0:H].rearrange("p (n s) -> p n s", s=S),
                                            spread(l0_bias[:, :], 1, KT * BT), ALU.add).then_inc(xT_kept[u], 1)

                def maxima(i, k):
                    dve.wait_ge(s0_made[k], i + 1)
                    nc.vector.reduce_max(nmax0[:, k, :], b_s0[k % 2][:, :].rearrange("p (t s) -> p t s", t=KT), AX.X,
                                         negate=True).then_inc(max0_made[k], 1)

                def keep_turned(i, k):
                    dve.wait_ge(p0T_made[k], i + 1)
                    if not is_first(i):
                        dve.wait_ge(o0_made[k], i)
                    nc.vector.tensor_copy(p0T[:, k, :, :].rearrange("p s t -> p (s t)"), b_p0T[:, :]).then_inc(p0T_kept[k], 1)

                def finish(i, k):
                    u, b = k // BT, k % BT
                    dve.wait_ge(p0_made[k], i + 1)
                    nc.vector.reciprocal(rsum0[:, k, :], sum0[:, k, :]).then_inc(rsum0_made[k], 1)
                    dve.wait_ge(rsum0_made[k], i + 1)
                    dve.wait_ge(o0_made[k], i + 1)
                    for t in range(KT):
                        last = nc.vector.scalar_tensor_tensor(
                            out=hT[:, SLOTS * i + u, t, b, 1, :], in0=b_o0[:, t * S:(t + 1) * S],
                            scalar=rsum0[:, k, t:t + 1], in1=xT0[:, u, t, b, :], op0=ALU.mult, op1=ALU.add)
                    last.then_inc(o0_kept[k], 1)

                def slot(i, k):
                    after = not is_last(i)
                    if after and k % BT == 0:
                        statistics(i + 1, k // BT)
                    if k + 2 < UNITS0:
                        maxima(i, k + 2)
                    elif after:
                        maxima(i + 1, k + 2 - UNITS0)
                    if k + 1 < UNITS0:
                        keep_turned(i, k + 1)
                    elif after:
                        keep_turned(i + 1, 0)
                    if k == 0:
                        keep_x(i, 1)
                    if after and k == BT:
                        keep_x(i + 1, 0)
                    if after and k % BT == 0:
                        normalise(i + 1, k // BT)
                    finish(i, k)

                def trip(i):
                    if is_first(i):
                        statistics(i, 0)
                        statistics(i, 1)
                        normalise(i, 0)
                        keep_x(i, 0)
                        normalise(i, 1)
                        maxima(i, 0)
                        maxima(i, 1)
                        keep_turned(i, 0)
                    for k in range(UNITS0):
                        slot(i, k)

                each_trip(dve, trip)

                def maxima(i, u):
                    dve.wait_ge(s1_made[u], i + 1)
                    for b in range(BT):
                        rows = slice(b * S, (b + 1) * S)
                        last = nc.vector.reduce_max(nmax1[rows, u:u + 1], b_s1[u][rows, rows], AX.X, negate=True)
                    last.then_inc(max1_made[u], 1)

                def scale(i, u):
                    dve.wait_ge(p1_made[u], i + 1)
                    nc.vector.reciprocal(rsum1[:, u:u + 1], sum1[:, u:u + 1]).then_inc(rsum1_made[u], 1)
                    dve.wait_ge(rsum1_made[u], i + 1)
                    nc.vector.tensor_scalar(p1[:, u, :], p1[:, u, :], rsum1[:, u:u + 1], l1_alpha[:, 0:1],
                                            ALU.mult, ALU.mult).then_inc(p1_scaled[u], 1)

                def keep_values(i, u):
                    dve.wait_ge(v3_made[u], i + 1)
                    for g in range(2):
                        for b in range(BT):
                            tokens = slice(b * S, (b + 1) * S)
                            last = nc.vector.tensor_tensor(
                                v3[g * S:(g + 1) * S, BT * (SLOTS * i + u) + b, :, 0:4:3, g * L3_D:(g + 1) * L3_D],
                                b_v3[tokens, 0:S].rearrange("p (j o g d) -> p j o g d", o=2, g=2, d=L3_D)[:, :, :, g, :],
                                l3_bv[tokens, :].rearrange("p (j o g d) -> p j o g d", o=2, g=2, d=L3_D)[:, :, :, g, :], ALU.add)
                    last.then_inc(v3_kept[u], 1)

                def finish(i, u):
                    dve.wait_ge(d1_made[u], i + 1)
                    nc.vector.tensor_tensor(hT[:, SLOTS * i + u, :, :, 1, :],
                                            b_d1[:, 0:H].rearrange("p (k b s) -> p k b s", k=KT, b=BT),
                                            hT[:, SLOTS * i + u, :, :, 1, :], ALU.add).then_inc(x2_kept[u], 1)

                dve.wait_ge(middle_in, 16 * len(middle_loads))
                dve.wait_ge(tail_zeroed, 2)

                def trip(i):
                    if is_first(i):
                        keep_values(i, 0)
                        maxima(i, 0)
                        scale(i, 0)
                    keep_values(i, 1)
                    maxima(i, 1)
                    finish(i, 0)
                    scale(i, 1)
                    if not is_last(i):
                        keep_values(i + 1, 0)
                        maxima(i + 1, 0)
                    finish(i, 1)
                    if not is_last(i):
                        scale(i + 1, 0)

                each_trip(dve, trip)
                dve.wait_ge(late_in, 16 * len(late_loads))
                nc.vector.tensor_scalar(key_bias[:, :, 0:S], key_flags[:, :, :], 0, MASKED,
                                        ALU.is_equal, ALU.mult).then_inc(key_bias_made, 1)

        next_phase()
        kz = tb("kz", [P, SLOTS, KT, QUARTERS, BT * L2_KEYS])
        keys2 = tb("keys2", [P, SLOTS, KT, BT * L2_KEYS])
        sq = tb("sq", [P, SLOTS, H])
        ssq = tb("ssq", [P, SLOTS])
        rms = tb("rms", [P, SLOTS])

        k2_made, q2_made, v2_made = sems("k2_made", SLOTS), sems("q2_made", SLOTS), sems("v2_made", SLOTS)
        k2_kept, q2_kept, v2_kept = sems("k2_kept", SLOTS), sems("q2_kept", SLOTS), sems("v2_kept", SLOTS)
        s2_made, s2_kept = sems("s2_made", UT), sems("s2_kept", UT)
        p2_made, p2T_made, p2T_kept = sems("p2_made", UT), sems("p2T_made", UT), sems("p2T_kept", UT)
        o2_made, att_made = sems("o2_made", SLOTS), sems("att_made", SLOTS)
        x2tok_made, x2tok_kept = sems("x2tok_made", SLOTS), sems("x2tok_kept", SLOTS)
        ow_made, res_made, ssq_made, y_made = sems("ow_made", SLOTS), sems("res_made", SLOTS), sems("ssq_made", SLOTS), sems("y_made", SLOTS)
        yT_made, yT_kept = sems("yT_made", SLOTS), sems("yT_kept", SLOTS)
        kz_made = sems("kz_made", SLOTS)
        AHEAD = 3
        with_eps = sems("with_eps_l2_", SLOTS)
        rms_made = sems("rms_made", SLOTS)
        nmax2_made, rsum2_made, with_x2 = sems("nmax2_made", UT), sems("rsum2_made", SLOTS), sems("with_x2", SLOTS)

        b_kv2, b_qx2, b_p2T, b_end2 = (bank[k] for k in (0, 1, 5, 7))
        b_s2 = (bank[3], bank[4])
        b_o2 = (bank[6], bank[2])

        x3T = tb("x3T", [P, SLOTS, KT, P])
        v3z = tb("v3z", [P, SLOTS, BT, QUARTERS // 2, 4, 2 * L3_D])
        stats3 = tb("stats3", [P, SLOTS, 6])
        moments3 = tb("moments3", [P, SLOTS, 2])
        rstd3 = tb("rstd3", [P, SLOTS])
        result = tb("result", [P, SLOTS, H])

        v3z_made = sems("v3z_made", SLOTS)
        x3T_made, x3T_kept = sems("x3T_made", SLOTS), sems("x3T_kept", SLOTS)
        q3_made, q3_kept = sems("q3_made", SLOTS), sems("q3_kept", SLOTS)
        s3_made, s3_kept, s3_less_max = sems("s3_made", UT), sems("s3_kept", UT), sems("s3_less_max", UT)
        p3_made, p3T_made, p3T_kept = sems("p3_made", UT), sems("p3T_made", UT), sems("p3T_kept", UT)
        o3_made, att3_made = sems("o3_made", SLOTS), sems("att3_made", SLOTS)
        wo3_made, wo3_kept = sems("wo3_made", SLOTS), sems("wo3_kept", SLOTS)
        result_made, stored = sems("result_made", SLOTS), sems("stored", SLOTS)
        with_eps3 = sems("with_eps_l3_", SLOTS)
        moments3_made, rstd3_made = sems("moments3_made", SLOTS), sems("rstd3_made", SLOTS)
        nmax3_made, rsum3_made = sems("nmax3_made", UT), sems("rsum3_made", SLOTS)
        with_bo, stats3_made, centred, scaled = (sems(n, SLOTS) for n in ("with_bo", "stats3_made", "centred", "scaled"))

        b_x3T, b_q3, b_p3T, b_end3 = (bank[k] for k in (0, 1, 5, 7))
        b_s3 = (bank[3], bank[4])
        b_o3 = (bank[6], bank[2])

        UPS = 4
        TOK = SLOTS * P
        gT = tb("gT", [P, FT, TOK])
        up_made, gelu_made = sems("up_made", UPS), sems("gelu_made", UPS)
        down_made, x3_kept = sems("down_made", SLOTS), sems("x3_kept", SLOTS)
        x2b_made = sem("x2b_made")
        b_up = (bank[0], bank[1], bank[3], bank[4])
        b_down = (bank[5], bank[2])

        with nc.Block() as block:
            @block.sync
            def _(sp):
                def trip(i):
                    for u in range(SLOTS if not is_first(i) else 0):
                        sp.wait_ge(x2tok_made[u], i)
                        sp.dma_start(ring[:, u, :, :, :, :], hT[:, SLOTS * i + u, :, :, :, :]).then_inc(ring2_in[u], 16)
                        sp.dma_start(x_flat[:, u, :, :, :], hT[:, SLOTS * i + u, :, :, 1, :]).then_inc(ring2_in[u], 16)

                each_trip(sp, trip)
                for u in range(SLOTS):
                    sp.wait_ge(x3_kept[u], 1)
                    sp.dma_start(x3_ring[:, u, :], x_tok[:, u, :]).then_inc(x3_in[u], 16)

                def load3(i, u):
                    if not is_first(i):
                        sp.wait_ge(x3T_made[u], i)
                    sp.dma_start(x3_ring[:, u, :], x_tok[:, SLOTS * i + u, :]).then_inc(x3_in[u], 16)

                def store3(i, u):
                    sp.wait_ge(result_made[u], i + 1)
                    sp.dma_start(out[SLOTS * i + u, :, :], result[:, u, :]).then_inc(stored[u], 16)

                def trip3(i):
                    if not is_last(i):
                        load3(i + 1, 0)
                        load3(i + 1, 1)
                    if not is_first(i):
                        store3(i - 1, 0)
                        store3(i - 1, 1)

                each_trip(sp, trip3)
                store3(TRIPS - 1, 0)
                store3(TRIPS - 1, 1)
                for u in range(SLOTS):
                    sp.wait_ge(stored[u], 16 * TRIPS)

            @block.gpsimd
            def _(pool):
                def mask_keys(i, u, m):
                    if m == 0:
                        pool.wait_ge(k2_kept[u], i + 1)
                        if not is_first(i):
                            pool.wait_ge(s2_made[UT - 1], reached(i, UT * (u + 1) - 1 - UNITS))
                    nc.gpsimd.tensor_tensor(kz[:, u, m, :, :], spread(keys2[:, u, m, :], 1, QUARTERS),
                                            spread(quarter_mask[:, :], 2, H), ALU.mult).then_inc(kz_made[u], 1)

                def rms_of(i, u):
                    pool.wait_ge(ssq_made[u], i + 1)
                    nc.gpsimd.tensor_tensor(rms[:, u:u + 1], ssq[:, u:u + 1], l2_eps[:, :], ALU.add).then_inc(with_eps[u], 1)
                    pool.wait_ge(with_eps[u], i + 1)
                    nc.gpsimd.tensor_tensor(rms[:, u:u + 1], rms[:, u:u + 1], rsqrt_power[:, 0:1], ALU.pow)\
                        .then_inc(rms_made[u], 1)

                def trip(i):
                    if is_first(i):
                        for u in range(SLOTS):
                            for m in range(KT):
                                mask_keys(i, u, m)
                    if not is_last(i):
                        mask_keys(i + 1, 0, 0)
                    if not is_first(i):
                        rms_of(i - 1, 1)
                    if not is_last(i):
                        mask_keys(i + 1, 0, 1)
                        mask_keys(i + 1, 1, 0)
                    rms_of(i, 0)
                    if not is_last(i):
                        mask_keys(i + 1, 1, 1)

                each_trip(pool, trip)
                rms_of(TRIPS - 1, 1)
                for u in range(SLOTS):
                    pool.wait_ge(with_x2[u], TRIPS)
                with pool.Fori(0, TILES) as n:
                    nc.gpsimd.tensor_tensor(x_tok[:, n, :], x_tok[:, n, :], mlp_b2[:, :], ALU.add).then_inc(x2b_made, 1)
                for u in range(SLOTS):
                    for b in range(BT):
                        last = nc.gpsimd.tensor_tensor(k3z[:, u, b, :, :], spread(k3T[:, u, b, :], 1, KVH),
                                                       spread(kvh_mask[:, :], 2, S), ALU.mult)
                    last.then_inc(k3z_made[u], 1)

                def keys3(i, u):
                    if not is_first(i):
                        pool.wait_ge(s3_made[UT - 1], reached(i, UT * (u + 1) - 1 - UNITS))
                    for b in range(BT):
                        last = nc.gpsimd.tensor_tensor(k3z[:, u, b, :, :], spread(k3T[:, SLOTS * i + u, b, :], 1, KVH),
                                                       spread(kvh_mask[:, :], 2, S), ALU.mult)
                    last.then_inc(k3z_made[u], 1)

                def values3(i, u):
                    if not is_first(i):
                        pool.wait_ge(o3_made[u], i)
                    nc.gpsimd.tensor_copy(v3z[:, u, :, :, :, :].rearrange("p b j e f -> p (b j e f)"),
                                          v3[:, bass.ds(BT * (SLOTS * i + u), BT), :, :, :].rearrange("p b j g e -> p (b j g e)"))\
                        .then_inc(v3z_made[u], 1)

                def deviation3(i, u):
                    pool.wait_ge(moments3_made[u], i + 1)
                    nc.gpsimd.tensor_tensor(rstd3[:, u:u + 1], moments3[:, u, 1:2], l3_eps[:, :], ALU.add).then_inc(with_eps3[u], 1)
                    pool.wait_ge(with_eps3[u], i + 1)
                    nc.gpsimd.tensor_tensor(rstd3[:, u:u + 1], rstd3[:, u:u + 1], rsqrt_power[:, 0:1], ALU.pow)\
                        .then_inc(rstd3_made[u], 1)

                def less_max3(i, k):
                    pool.wait_ge(nmax3_made[k % UT], reached(i, k))
                    s = sc[:, k % UT, :, :].rearrange("p h (g n) -> p (h g) n", g=2)
                    nc.gpsimd.tensor_tensor(s, s, spread(nmax[:, k % UT, :], 2, S), ALU.add).then_inc(s3_less_max[k % UT], 1)

                def slot3(i, k):
                    after = not is_last(i)
                    if k == 0 and not is_first(i):
                        values3(i, 1)
                    if k + AHEAD < UNITS:
                        less_max3(i, k + AHEAD)
                    elif after:
                        less_max3(i + 1, k + AHEAD - UNITS)
                    if after and k == 1:
                        keys3(i + 1, 0)
                    if k == 3 and not is_first(i):
                        deviation3(i - 1, 1)
                    if after and k == 4:
                        values3(i + 1, 0)
                    if after and k == 5:
                        keys3(i + 1, 1)
                    if k == 7:
                        deviation3(i, 0)

                def trip3(i):
                    if is_first(i):
                        less_max3(i, 0)
                        values3(i, 0)
                        less_max3(i, 1)
                        less_max3(i, 2)
                        values3(i, 1)
                    for k in range(UNITS):
                        slot3(i, k)

                each_trip(pool, trip3)
                deviation3(TRIPS - 1, 1)

            @block.tensor
            def _(pe):
                def project_keys(i, u):
                    pe.wait_ge(ring2_in[u], 32 * (i + 1))
                    if u or not is_first(i):
                        pe.wait_ge(v2_kept[1 - u], i + u)
                    for m in range(KT):
                        for k in range(KT):
                            last = nc.tensor.matmul(b_kv2[:, m * H:(m + 1) * H], l2_kw[:, k, m * P:(m + 1) * P],
                                                    ring[:, u, k, :, :, :], start=(k == 0), stop=(k == KT - 1))
                    last.then_inc(k2_made[u], 1)

                def project_queries(i, u):
                    if u or not is_first(i):
                        pe.wait_ge(x2tok_kept[1 - u], i + u)
                    for m in range(KT):
                        for k in range(KT):
                            last = nc.tensor.matmul(b_qx2[:, m * P:(m + 1) * P], l2_qw[:, k, m * P:(m + 1) * P],
                                                    ring[:, u, k, :, 1, :], start=(k == 0), stop=(k == KT - 1))
                    last.then_inc(q2_made[u], 1)

                def project_values(i, u):
                    pe.wait_ge(k2_kept[u], i + 1)
                    for b in range(BT):
                        for k in range(KT):
                            last = nc.tensor.matmul(b_kv2[:, b * H:(b + 1) * H], ring[:, u, k, b, :, :], l2_vw[:, k, :],
                                                    start=(k == 0), stop=(k == KT - 1))
                    last.then_inc(v2_made[u], 1)

                def stream(i, u):
                    pe.wait_ge(q2_kept[u], i + 1)
                    for k in range(KT):
                        last = nc.tensor.transpose(b_qx2[:, k * P:(k + 1) * P], x_flat[:, u, k, :, :], ident[:, :])
                    last.then_inc(x2tok_made[u], 1)

                def scores(i, k):
                    u, b, m = k // UT, k // KT % BT, k % KT
                    pe.wait_ge(kz_made[u], KT * i + m + 1)
                    pe.wait_ge(q2_kept[u], i + 1)
                    if k >= 2 or not is_first(i):
                        pe.wait_ge(s2_kept[(k - 2) % UT], reached(i, k - 2))
                    nc.tensor.matmul(b_s2[k % 2][:, :], qz[:, u, m, b, :, :], kz[:, u, m, :, b * L2_KEYS:(b + 1) * L2_KEYS],
                                     start=True, stop=True).then_inc(s2_made[k % UT], 1)

                def turn(i, k):
                    pe.wait_ge(p2_made[k % UT], reached(i, k))
                    if k >= 1 or not is_first(i):
                        pe.wait_ge(p2T_kept[(k - 1) % UT], reached(i, k - 1))
                    for h in range(QUARTERS):
                        last = nc.tensor.transpose(b_p2T[:, h * P:(h + 1) * P], sc[:, k % UT, h, :], ident[:, :])
                    last.then_inc(p2T_made[k % UT], 1)

                def values(i, k):
                    u, b, m = k // UT, k // KT % BT, k % KT
                    pe.wait_ge(p2T_kept[k % UT], reached(i, k))
                    if k % UT == 0:
                        pe.wait_ge(v2_kept[u], i + 1)
                        if not is_first(i):
                            pe.wait_ge(att_made[u], i)
                    for w, col in ((v2[:, u, b, :, :, :], 0), (None, H)):
                        for h in range(QUARTERS):
                            for g in range(2):
                                pair = (m * 2 * QUARTERS + g * QUARTERS + h) // 2
                                row = g * S + h // 2 * 2 * L2_D
                                at = col + m * P + b * S
                                o = h % 2
                                last = nc.tensor.matmul(b_o2[u][row:row + 2 * L2_D, at:at + S],
                                                        w[:, pair, 2 * o:2 * o + 2, :] if w is not None else ones2[:, o, :, :],
                                                        pT[:, k % UT, h, g * S:(g + 1) * S], start=(o == 0), stop=(o == 1))
                    if k % UT == UT - 1:
                        last.then_inc(o2_made[u], 1)

                def out_project(i, u):
                    pe.wait_ge(att_made[u], i + 1)
                    if u or not is_first(i):
                        pe.wait_ge(yT_kept[1 - u], i + u)
                    for k in range(KT):
                        last = nc.tensor.matmul(b_end2[:, 0:H], attT[:, u, k * P:(k + 1) * P], l2_ow[:, k, :],
                                                start=(k == 0), stop=(k == KT - 1))
                    last.then_inc(ow_made[u], 1)

                def turn_y(i, u):
                    pe.wait_ge(y_made[u], i + 1)
                    for k in range(KT):
                        last = nc.tensor.transpose(b_end2[:, k * P:(k + 1) * P], res[:, u, k * P:(k + 1) * P], ident[:, :])
                    last.then_inc(yT_made[u], 1)

                def slot(i, k):
                    after = not is_last(i)
                    if k + AHEAD < UNITS:
                        scores(i, k + AHEAD)
                    elif after:
                        scores(i + 1, k + AHEAD - UNITS)
                    if k + 1 < UNITS:
                        turn(i, k + 1)
                    elif after:
                        turn(i + 1, 0)
                    values(i, k)
                    if k == 0:
                        stream(i, 1)
                    if k == 1:
                        if not is_first(i):
                            turn_y(i - 1, 0)
                        if after:
                            project_keys(i + 1, 0)
                    if k == 2:
                        if after:
                            project_queries(i + 1, 0)
                        if not is_first(i):
                            out_project(i - 1, 1)
                    if after and k == 3:
                        project_values(i + 1, 0)
                    if after and k == 4:
                        stream(i + 1, 0)
                    if k == 5:
                        if not is_first(i):
                            turn_y(i - 1, 1)
                        if after:
                            project_keys(i + 1, 1)
                    if k == 6:
                        if after:
                            project_queries(i + 1, 1)
                        out_project(i, 0)
                    if after and k == 7:
                        project_values(i + 1, 1)

                def trip(i):
                    if is_first(i):
                        project_keys(i, 0)
                        project_queries(i, 0)
                        project_values(i, 0)
                        stream(i, 0)
                        scores(i, 0)
                        project_keys(i, 1)
                        scores(i, 1)
                        project_queries(i, 1)
                        turn(i, 0)
                        scores(i, 2)
                        project_values(i, 1)
                    for k in range(UNITS):
                        slot(i, k)

                each_trip(pe, trip)
                turn_y(TRIPS - 1, 0)

                def up(i, j):
                    for u in range(SLOTS):
                        pe.wait_ge(yT_kept[u], i + 1)
                    if not is_first(i):
                        pe.wait_ge(gelu_made[j], i)
                    elif j == 0:
                        pe.wait_ge(v2_kept[SLOTS - 1], TRIPS)
                    elif j == 1:
                        pe.wait_ge(x2tok_kept[SLOTS - 1], TRIPS)
                    else:
                        pe.wait_ge(s2_kept[UT - 4 + j], reached(TRIPS - 1, UNITS - 4 + j))
                    for f in range(2):
                        for k in range(KT):
                            last = nc.tensor.matmul(b_up[j][:, f * TOK:(f + 1) * TOK],
                                                    mlp_w1[:, k, (2 * j + f) * P:(2 * j + f + 1) * P],
                                                    yT[:, k, bass.ds(i * TOK, TOK)], start=(k == 0), stop=(k == KT - 1))
                    last.then_inc(up_made[j], 1)

                def down(i, u):
                    if not is_first(i):
                        pe.wait_ge(x3_kept[u], i)
                    elif u == 0:
                        pe.wait_ge(p2T_kept[UT - 1], reached(TRIPS - 1, UNITS - 1))
                    else:
                        pe.wait_ge(att_made[SLOTS - 1], TRIPS)
                    for f in range(FT):
                        if u == 0 and f % 2 == 0:
                            pe.wait_ge(gelu_made[f // 2], i + 1)
                        last = nc.tensor.matmul(b_down[u][:, 0:H], gT[:, f, u * P:(u + 1) * P], mlp_w2[:, f, :],
                                                start=(f == 0), stop=(f == FT - 1))
                    last.then_inc(down_made[u], 1)

                def turn_stream3(i, u):
                    pe.wait_ge(x3_in[u], 16 * (i + 1))
                    if u or not is_first(i):
                        pe.wait_ge(x3T_kept[1 - u], i + u)
                    else:
                        pe.wait_ge(gelu_made[0], TRIPS)
                    for k in range(KT):
                        last = nc.tensor.transpose(b_x3T[:, k * P:(k + 1) * P], x3_ring[:, u, k * P:(k + 1) * P], ident[:, :])
                    last.then_inc(x3T_made[u], 1)

                def project_queries3(i, u):
                    pe.wait_ge(x3T_kept[u], i + 1)
                    if u or not is_first(i):
                        pe.wait_ge(q3_kept[1 - u], i + u)
                    else:
                        pe.wait_ge(gelu_made[1], TRIPS)
                    for m in range(KT):
                        for k in range(KT):
                            last = nc.tensor.matmul(b_q3[:, m * P:(m + 1) * P], l3_wq[:, k, m * P:(m + 1) * P],
                                                    x3T[:, u, k, :], start=(k == 0), stop=(k == KT - 1))
                    last.then_inc(q3_made[u], 1)

                def scores3(i, k):
                    u, b, m = k // UT, k // KT % BT, k % KT
                    pe.wait_ge(q3_kept[u], i + 1)
                    pe.wait_ge(k3z_made[u], i + 1)
                    if k >= 2 or not is_first(i):
                        pe.wait_ge(s3_kept[(k - 2) % UT], reached(i, k - 2))
                    else:
                        pe.wait_ge(gelu_made[2 + k], TRIPS)
                    nc.tensor.matmul(b_s3[k % 2][:, :], qz[:, u, m, b, :, :], k3z[:, u, b, :, :], start=True, stop=True)\
                        .then_inc(s3_made[k % UT], 1)

                def turn3(i, k):
                    pe.wait_ge(p3_made[k % UT], reached(i, k))
                    if k >= 1 or not is_first(i):
                        pe.wait_ge(p3T_kept[(k - 1) % UT], reached(i, k - 1))
                    else:
                        pe.wait_ge(x3_kept[0], TRIPS)
                    for h in range(QUARTERS):
                        last = nc.tensor.transpose(b_p3T[:, h * P:(h + 1) * P], sc[:, k % UT, h, :], ident[:, :])
                    last.then_inc(p3T_made[k % UT], 1)

                def values3(i, k):
                    u, b, m = k // UT, k // KT % BT, k % KT
                    pe.wait_ge(p3T_kept[k % UT], reached(i, k))
                    if k % UT == 0:
                        pe.wait_ge(v3z_made[u], i + 1)
                        if not is_first(i):
                            pe.wait_ge(att3_made[u], i)
                        else:
                            pe.wait_ge((att_made[0], x3_kept[1])[u], TRIPS)
                    for w, col in ((v3z[:, u, b, :, :, :], 0), (None, H)):
                        for j in range(QUARTERS):
                            for g in range(2):
                                row = g * S + j // 2 * 4 * L3_D
                                at = col + m * P + b * S
                                o = j % 2
                                last = nc.tensor.matmul(b_o3[u][row:row + 4 * L3_D, at:at + S],
                                                        w[:, j // 2, 2 * o:2 * o + 2, :] if w is not None else ones3[:, o, :, :],
                                                        pT[:, k % UT, j, g * S:(g + 1) * S], start=(o == 0), stop=(o == 1))
                    if k % UT == UT - 1:
                        last.then_inc(o3_made[u], 1)

                def out_project3(i, u):
                    pe.wait_ge(att3_made[u], i + 1)
                    if u or not is_first(i):
                        pe.wait_ge(wo3_kept[1 - u], i + u)
                    else:
                        pe.wait_ge(yT_kept[1], TRIPS)
                    for k in range(KT):
                        last = nc.tensor.matmul(b_end3[:, 0:H], attT[:, u, k * P:(k + 1) * P], l3_wo[:, k, :],
                                                start=(k == 0), stop=(k == KT - 1))
                    last.then_inc(wo3_made[u], 1)

                def slot3(i, k):
                    after = not is_last(i)
                    if k + AHEAD < UNITS:
                        scores3(i, k + AHEAD)
                    elif after:
                        scores3(i + 1, k + AHEAD - UNITS)
                    if k + 1 < UNITS:
                        turn3(i, k + 1)
                    elif after:
                        turn3(i + 1, 0)
                    values3(i, k)
                    if after and k == 1:
                        turn_stream3(i + 1, 0)
                    if k == 2 and not is_first(i):
                        out_project3(i - 1, 1)
                    if after and k == 3:
                        project_queries3(i + 1, 0)
                    if after and k == 5:
                        turn_stream3(i + 1, 1)
                    if k == 6:
                        out_project3(i, 0)
                    if after and k == 7:
                        project_queries3(i + 1, 1)

                def trip3(i):
                    if is_first(i):
                        project_queries3(i, 1)
                        turn3(i, 0)
                        scores3(i, 2)
                    for k in range(UNITS):
                        slot3(i, k)

                def mlp_trip(i):
                    for j in range(UPS):
                        if is_first(i) and j == 2:
                            out_project(TRIPS - 1, 1)
                        if is_last(i) and j == 3:
                            turn_stream3(0, 0)
                        up(i, j)
                    if is_first(i):
                        turn_y(TRIPS - 1, 1)
                    if is_last(i):
                        project_queries3(0, 0)
                    down(i, 0)
                    if is_last(i):
                        turn_stream3(0, 1)
                        scores3(0, 0)
                        scores3(0, 1)
                    down(i, 1)

                each_trip(pe, mlp_trip)
                each_trip(pe, trip3)
                out_project3(TRIPS - 1, 1)

            @block.scalar
            def _(act):
                act.wait_ge(zero2, 2)

                def keep_keys(i, u):
                    act.wait_ge(k2_made[u], i + 1)
                    if not is_first(i):
                        act.wait_ge(kz_made[u], KT * i)
                    for m in range(KT):
                        last = nc.scalar.activation(keys2[:, u, m, :], b_kv2[:, m * H:(m + 1) * H], ACT.Identity,
                                                    bias=l2_kb[:, m:m + 1])
                    last.then_inc(k2_kept[u], 1)

                def keep_queries(i, u):
                    act.wait_ge(q2_made[u], i + 1)
                    if not is_first(i):
                        act.wait_ge(s2_made[UT - 1], reached(i, UT * (u + 1) - 1 - UNITS))
                    for m in range(KT):
                        for g in range(2):
                            rows = slice(g * S, (g + 1) * S)
                            last = nc.scalar.activation(qz[rows, u, m, :, g, :],
                                                        b_qx2[rows, m * P:(m + 1) * P].rearrange("p (b s) -> p b s", b=BT),
                                                        ACT.Identity, bias=l2_qb[rows, m:m + 1], scale=1.0 / L2_D)
                    last.then_inc(q2_kept[u], 1)

                def keep_stream(i, u):
                    act.wait_ge(x2tok_made[u], i + 1)
                    nc.scalar.copy(x_tok[:, SLOTS * i + u, :], b_qx2[:, 0:H]).then_inc(x2tok_kept[u], 1)

                def exps(i, k):
                    act.wait_ge(nmax2_made[k % UT], reached(i, k))
                    for h in range(QUARTERS):
                        last = nc.scalar.activation(sc[:, k % UT, h, :], sc[:, k % UT, h, :], ACT.Exp,
                                                    bias=nmax[:, k % UT, h:h + 1])
                    last.then_inc(p2_made[k % UT], 1)

                def keep_turned(i, k):
                    act.wait_ge(p2T_made[k % UT], reached(i, k))
                    if k >= UT or not is_first(i):
                        act.wait_ge(o2_made[1 - k // UT], i + 1 if k >= UT else i)
                    nc.scalar.copy(pT[:, k % UT, :, :], b_p2T[:, :].rearrange("p (h n) -> p h n", h=QUARTERS)).then_inc(p2T_kept[k % UT], 1)

                def squares(i, u):
                    act.wait_ge(res_made[u], i + 1)
                    nc.scalar.activation(sq[:, u, :], res[:, u, :], ACT.Square, accum_out=ssq[:, u:u + 1]).then_inc(ssq_made[u], 1)

                def keep_y(i, u):
                    act.wait_ge(yT_made[u], i + 1)
                    for k in range(KT):
                        last = nc.scalar.mul(yT[:, k, bass.ds((SLOTS * i + u) * P, P)], b_end2[:, k * P:(k + 1) * P],
                                             l2_pw[:, k:k + 1])
                    last.then_inc(yT_kept[u], 1)
                def slot(i, k):
                    after = not is_last(i)
                    if k + 2 < UNITS:
                        exps(i, k + 2)
                    elif after:
                        exps(i + 1, k + 2 - UNITS)
                    if k + 1 < UNITS:
                        keep_turned(i, k + 1)
                    elif after:
                        keep_turned(i + 1, 0)
                    if k == 1:
                        keep_stream(i, 1)
                    if k == 2:
                        if not is_first(i):
                            keep_y(i - 1, 0)
                        if after:
                            keep_keys(i + 1, 0)
                    if k == 3:
                        if after:
                            keep_queries(i + 1, 0)
                        if not is_first(i):
                            squares(i - 1, 1)
                    if after and k == 5:
                        keep_stream(i + 1, 0)
                    if k == 6:
                        if not is_first(i):
                            keep_y(i - 1, 1)
                        if after:
                            keep_keys(i + 1, 1)
                    if k == 7:
                        if after:
                            keep_queries(i + 1, 1)
                        squares(i, 0)

                def trip(i):
                    if is_first(i):
                        keep_keys(i, 0)
                        keep_queries(i, 0)
                        keep_stream(i, 0)
                        keep_keys(i, 1)
                        exps(i, 0)
                        keep_queries(i, 1)
                        exps(i, 1)
                        keep_turned(i, 0)
                    for k in range(UNITS):
                        slot(i, k)

                each_trip(act, trip)
                keep_y(TRIPS - 1, 0)

                def gelus(i, j):
                    act.wait_ge(up_made[j], i + 1)
                    if not is_first(i):
                        act.wait_ge(down_made[1], i)
                    for f in range(2):
                        last = nc.scalar.activation(gT[:, 2 * j + f, :], b_up[j][:, f * TOK:(f + 1) * TOK],
                                                    ACT.Gelu_apprx_tanh, bias=mlp_b1[:, 2 * j + f:2 * j + f + 1])
                    last.then_inc(gelu_made[j], 1)

                def keep_stream3(i, u):
                    act.wait_ge(x3T_made[u], i + 1)
                    if not is_first(i):
                        act.wait_ge(q3_made[u], i)
                    nc.scalar.copy(x3T[:, u, :, :], b_x3T[:, 0:H].rearrange("p (k n) -> p k n", k=KT)).then_inc(x3T_kept[u], 1)

                def keep_queries3(i, u):
                    act.wait_ge(q3_made[u], i + 1)
                    if not is_first(i):
                        act.wait_ge(s3_made[UT - 1], reached(i, UT * (u + 1) - 1 - UNITS))
                    for m in range(KT):
                        for g in range(2):
                            rows = slice(g * S, (g + 1) * S)
                            last = nc.scalar.activation(qz[rows, u, m, :, g, :],
                                                        b_q3[rows, m * P:(m + 1) * P].rearrange("p (b s) -> p b s", b=BT),
                                                        ACT.Identity, bias=l3_bq[rows, m:m + 1], scale=L3_D ** -0.5)
                    last.then_inc(q3_kept[u], 1)

                def exps3(i, k):
                    act.wait_ge(s3_less_max[k % UT], reached(i, k))
                    nc.scalar.activation(sc[:, k % UT, :, :], sc[:, k % UT, :, :], ACT.Exp).then_inc(p3_made[k % UT], 1)

                def keep_turned3(i, k):
                    act.wait_ge(p3T_made[k % UT], reached(i, k))
                    if k >= UT or not is_first(i):
                        act.wait_ge(o3_made[1 - k // UT], i + 1 if k >= UT else i)
                    nc.scalar.copy(pT[:, k % UT, :, :], b_p3T[:, :].rearrange("p (h n) -> p h n", h=QUARTERS)).then_inc(p3T_kept[k % UT], 1)
                def slot3(i, k):
                    after = not is_last(i)
                    if after and k == 4:
                        keep_queries3(i + 1, 0)
                    if k == 0 and not is_first(i):
                        keep_queries3(i, 1)
                    if k + 2 < UNITS:
                        exps3(i, k + 2)
                    elif after:
                        exps3(i + 1, k + 2 - UNITS)
                    if k + 1 < UNITS:
                        keep_turned3(i, k + 1)
                    elif after:
                        keep_turned3(i + 1, 0)
                    if after and k == 2:
                        keep_stream3(i + 1, 0)
                    if after and k == 6:
                        keep_stream3(i + 1, 1)

                def trip3(i):
                    if is_first(i):
                        keep_queries3(i, 0)
                        keep_stream3(i, 1)
                        exps3(i, 0)
                        keep_queries3(i, 1)
                        exps3(i, 1)
                        keep_turned3(i, 0)
                    for k in range(UNITS):
                        slot3(i, k)

                def mlp_trip(i):
                    for j in range(UPS):
                        if is_first(i) and j == 2:
                            squares(TRIPS - 1, 1)
                        if is_last(i) and j == 3:
                            keep_stream3(0, 0)
                        gelus(i, j)
                    if is_first(i):
                        keep_y(TRIPS - 1, 1)

                each_trip(act, mlp_trip)
                each_trip(act, trip3)

            @block.vector
            def _(dve):
                dve.wait_ge(zero2, 2)

                def keep_values(i, u):
                    dve.wait_ge(v2_made[u], i + 1)
                    if not is_first(i):
                        dve.wait_ge(o2_made[u], i)
                    for b in range(BT):
                        last = nc.vector.tensor_tensor(v2[:, u, b, :, 0:4:3, :],
                                                       b_kv2[:, b * H:(b + 1) * H].rearrange("p (h o d) -> p h o d", o=2, d=L2_D),
                                                       l2_vb[:, :].rearrange("p (h o d) -> p h o d", o=2, d=L2_D), ALU.add)
                    last.then_inc(v2_kept[u], 1)

                def maxima(i, k):
                    u, b = k // UT, k // KT % BT
                    dve.wait_ge(s2_made[k % UT], reached(i, k))
                    if k >= UT or not is_first(i):
                        dve.wait_ge(p2T_made[(k - UT) % UT], reached(i, k - UT))
                    nc.vector.tensor_tensor(sc[:, k % UT, :, :], b_s2[k % 2][:, :].rearrange("p (h n) -> p h n", h=QUARTERS),
                                            spread(key_bias[:, BT * (SLOTS * i + u) + b, :], 1, QUARTERS),
                                            ALU.add).then_inc(s2_kept[k % UT], 1)
                    dve.wait_ge(s2_kept[k % UT], reached(i, k))
                    nc.vector.reduce_max(nmax[:, k % UT, 0:QUARTERS], sc[:, k % UT, :, :], AX.X, negate=True)\
                        .then_inc(nmax2_made[k % UT], 1)

                def normalise(i, u):
                    dve.wait_ge(o2_made[u], i + 1)
                    if not is_first(i):
                        dve.wait_ge(ow_made[u], i)
                    nc.vector.reciprocal(rsum[:, u, :], b_o2[u][:, H:2 * H]).then_inc(rsum2_made[u], 1)
                    dve.wait_ge(rsum2_made[u], i + 1)
                    nc.vector.tensor_tensor(attT[:, u, :], b_o2[u][:, 0:H], rsum[:, u, :], ALU.mult).then_inc(att_made[u], 1)

                def residual(i, u):
                    dve.wait_ge(ow_made[u], i + 1)
                    if not is_first(i):
                        dve.wait_ge(yT_made[u], i)
                    dve.wait_ge(x2tok_kept[u], i + 1)
                    nc.vector.tensor_tensor(res[:, u, :], b_end2[:, 0:H], x_tok[:, SLOTS * i + u, :], ALU.add).then_inc(with_x2[u], 1)
                    dve.wait_ge(with_x2[u], i + 1)
                    nc.vector.tensor_tensor(res[:, u, :], res[:, u, :], l2_ob[:, :], ALU.add).then_inc(res_made[u], 1)

                def rms_norm(i, u):
                    dve.wait_ge(rms_made[u], i + 1)
                    nc.vector.tensor_scalar(res[:, u, :], res[:, u, :], rms[:, u:u + 1], float(H) ** 0.5,
                                            ALU.mult, ALU.mult).then_inc(y_made[u], 1)
                def slot(i, k):
                    after = not is_last(i)
                    if k == 1:
                        if not is_first(i):
                            rms_norm(i - 1, 0)
                        keep_values(i, 1)
                    if k == 5 and not is_first(i):
                        rms_norm(i - 1, 1)
                    if after and k == 5:
                        keep_values(i + 1, 0)
                    if k + AHEAD < UNITS:
                        maxima(i, k + AHEAD)
                    elif after:
                        maxima(i + 1, k + AHEAD - UNITS)
                    if k == 1 and not is_first(i):
                        normalise(i - 1, 1)
                    if k == 3 and not is_first(i):
                        residual(i - 1, 1)
                    if k == 5:
                        normalise(i, 0)
                    if k == 7:
                        residual(i, 0)

                def trip(i):
                    if is_first(i):
                        keep_values(i, 0)
                        maxima(i, 0)
                        maxima(i, 1)
                        maxima(i, 2)
                    for k in range(UNITS):
                        slot(i, k)

                each_trip(dve, trip)
                rms_norm(TRIPS - 1, 0)
                normalise(TRIPS - 1, 1)
                residual(TRIPS - 1, 1)
                rms_norm(TRIPS - 1, 1)

                def maxima3(i, k):
                    u, b = k // UT, k // KT % BT
                    dve.wait_ge(s3_made[k % UT], reached(i, k))
                    if k >= UT or not is_first(i):
                        dve.wait_ge(p3T_made[(k - UT) % UT], reached(i, k - UT))
                    s = sc[:, k % UT, :, :].rearrange("p h (g n) -> p (h g) n", g=2)
                    nc.vector.tensor_tensor(s, b_s3[k % 2][:, :].rearrange("p (h n) -> p h n", h=KVH),
                                            spread(ff_mask[:, BT * (SLOTS * i + u) + b, :], 1, KVH),
                                            ALU.add).then_inc(s3_kept[k % UT], 1)
                    dve.wait_ge(s3_kept[k % UT], reached(i, k))
                    nc.vector.reduce_max(nmax[:, k % UT, :], s, AX.X, negate=True).then_inc(nmax3_made[k % UT], 1)

                def normalise3(i, u):
                    dve.wait_ge(o3_made[u], i + 1)
                    if not is_first(i):
                        dve.wait_ge(wo3_made[u], i)
                    nc.vector.reciprocal(rsum[:, u, :], b_o3[u][:, H:2 * H]).then_inc(rsum3_made[u], 1)
                    dve.wait_ge(rsum3_made[u], i + 1)
                    nc.vector.tensor_tensor(attT[:, u, :], b_o3[u][:, 0:H], rsum[:, u, :], ALU.mult).then_inc(att3_made[u], 1)

                def finish3(i, u):
                    dve.wait_ge(wo3_made[u], i + 1)
                    nc.vector.tensor_tensor(res[:, u, :], b_end3[:, 0:H], x_tok[:, SLOTS * i + u, :], ALU.add).then_inc(wo3_kept[u], 1)
                    dve.wait_ge(wo3_kept[u], i + 1)
                    nc.vector.tensor_tensor(res[:, u, :], res[:, u, :], l3_bo[:, :], ALU.add).then_inc(with_bo[u], 1)
                    dve.wait_ge(with_bo[u], i + 1)
                    nc.vector.bn_stats(stats3[:, u, :], res[:, u, :]).then_inc(stats3_made[u], 1)
                    dve.wait_ge(stats3_made[u], i + 1)
                    nc.vector.memset(scratch[:, :], 0.0)
                    nc.vector.bn_aggr(moments3[:, u, :], stats3[:, u, :]).then_inc(moments3_made[u], 1)

                def deliver3(i, u):
                    dve.wait_ge(rstd3_made[u], i + 1)
                    nc.vector.tensor_scalar(res[:, u, :], res[:, u, :], moments3[:, u, 0:1], rstd3[:, u:u + 1],
                                            ALU.subtract, ALU.mult).then_inc(centred[u], 1)
                    dve.wait_ge(centred[u], i + 1)
                    nc.vector.tensor_tensor(res[:, u, :], res[:, u, :], l3_gamma[:, :], ALU.mult).then_inc(scaled[u], 1)
                    dve.wait_ge(scaled[u], i + 1)
                    if not is_first(i):
                        dve.wait_ge(stored[u], 16 * i)
                    nc.vector.tensor_tensor(result[:, u, :], res[:, u, :], l3_beta[:, :], ALU.add).then_inc(result_made[u], 1)

                def slot3(i, k):
                    after = not is_last(i)
                    if k + AHEAD < UNITS:
                        maxima3(i, k + AHEAD)
                    elif after:
                        maxima3(i + 1, k + AHEAD - UNITS)
                    if k == 0 and not is_first(i):
                        normalise3(i - 1, 1)
                    if k == 1 and not is_first(i):
                        deliver3(i - 1, 0)
                    if k == 3 and not is_first(i):
                        finish3(i - 1, 1)
                    if k == 4:
                        normalise3(i, 0)
                    if k == 5 and not is_first(i):
                        deliver3(i - 1, 1)
                    if k == 7:
                        finish3(i, 0)

                def trip3(i):
                    if is_first(i):
                        maxima3(i, 2)
                    for k in range(UNITS):
                        slot3(i, k)

                def mlp_trip(i):
                    for u in range(SLOTS):
                        dve.wait_ge(down_made[u], i + 1)
                        dve.wait_ge(x2b_made, SLOTS * i + u + 1)
                        nc.vector.tensor_tensor(x_tok[:, SLOTS * i + u, :], b_down[u][:, 0:H], x_tok[:, SLOTS * i + u, :],
                                                ALU.add).then_inc(x3_kept[u], 1)
                        if is_last(i) and u == 0:
                            maxima3(0, 0)
                            maxima3(0, 1)

                each_trip(dve, mlp_trip)
                each_trip(dve, trip3)
                normalise3(TRIPS - 1, 1)
                deliver3(TRIPS - 1, 0)
                finish3(TRIPS - 1, 1)
                deliver3(TRIPS - 1, 1)


def layouts(inputs):
    import numpy as np
    v = {k: np.asarray(x) for k, x in inputs.items()}
    cols = lambda w, n: np.ascontiguousarray(w.reshape(n, P).T)
    row = lambda w: w.reshape(1, -1)
    twice = lambda w: np.concatenate([w, w], axis=-1)
    kv_w = v["L2_xattn_kv_w"].reshape(H, H, 2)
    kv_b = v["L2_xattn_kv_b"].reshape(H, 2)
    grouped = lambda w: w.reshape(-1, KVH, GROUPS, L3_D).transpose(0, 2, 1, 3).reshape(w.shape)
    on_p = lambda w: np.concatenate([w, w], axis=0)
    rows = np.arange(P)
    columns_of = {
        "l2_qb": cols(v["L2_xattn_q_b"], KT), "l2_kb": cols(kv_b[:, 0], KT), "l2_pw": cols(v["L2_xattn_postnorm_w"], KT),
        "mlp_b1": cols(v["L2_xattn_mlp_b1"], FT), "l3_bq": cols(grouped(v["L3_xattn_bq"]), KT),
        "l3_bk": twice(v["L3_xattn_bk"]).reshape(P, 1),
        "quarter_mask": (rows[:, None] // L2_D % QUARTERS == np.arange(QUARTERS)).astype(np.float32),
        "kvh_mask": (rows[:, None] // L3_D % KVH == np.arange(KVH)).astype(np.float32),
    }
    rows_of = {
        "l1_alpha": v["L1_xattn_alpha"].reshape(1, 1), "l2_vb": row(kv_b[:, 1]), "l2_ob": row(v["L2_xattn_out_b"]),
        "mlp_b2": row(v["L2_xattn_mlp_b2"]), "l3_bv": row(v["L3_xattn_bv"]), "l3_bo": row(v["L3_xattn_bo"]),
        "l3_gamma": row(v["L3_xattn_gamma"]), "l3_beta": row(v["L3_xattn_beta"]),
    }
    d = {
        "x": v["x"].reshape(TILES, P, H), "ctx": v["ctx_2048"].reshape(TILES, P, H),
        "key_flags": v["mask_BxS2_ik0"].reshape(B, S), "ff_mask": v["mask_Bx1xSxS2_ff0"].reshape(B, S, S),
        "l0_wnT": v["L0_xattn_Wn"].T, "l0_wmT": v["L0_xattn_Wm"].T,
        "l0_first": np.concatenate([on_p(twice(v["L0_xattn_Wl"])), on_p(v["L0_xattn_Wo"].T), np.repeat(row(v["L0_xattn_bo"]), P, 0),
                                    on_p(v["L0_xattn_bl"].reshape(S, 1)), twice(v["L0_xattn_bn"]).reshape(P, 1),
                                    twice(v["L0_xattn_bm"]).reshape(P, 1)], axis=1),
        "l1_weights": np.stack([v["L1_xattn_w_k"], v["L1_xattn_w_q"], v["L1_xattn_w_v"], v["L1_xattn_w_o"].T]),
        "squares": np.stack([v["L2_xattn_q_w"], kv_w[:, :, 0], kv_w[:, :, 1], v["L2_xattn_out_w"],
                             grouped(v["L3_xattn_Wq"]), grouped(v["L3_xattn_Wo"].T).T]),
        "mlp_w1": v["L2_xattn_mlp_w1"], "mlp_w2": v["L2_xattn_mlp_w2"],
        "l3_kvw": np.concatenate([twice(v["L3_xattn_Wk"]), v["L3_xattn_Wv"]], axis=1),
        "rows": np.concatenate([rows_of[name] for name in ROWS], axis=1),
        "columns": np.concatenate([columns_of[name] for name in COLUMNS], axis=1),
        "ident": np.eye(P, dtype=np.float32),
    }
    return {k: np.ascontiguousarray(x) for k, x in d.items()}


def kernel(**inputs):
    import concourse.bacc as bacc
    from concourse.bass_utils import run_bass_kernel_spmd

    nc = bacc.Bacc("TRN2", target_bir_lowering=False, num_devices=1)
    arrays = {f"in_{k}": x for k, x in layouts(inputs).items()}
    aps = {k[3:]: nc.dram_tensor(k, x.shape, mybir.dt.from_np(x.dtype), kind="ExternalInput").ap() for k, x in arrays.items()}
    out = nc.dram_tensor("out", (TILES, P, H), F32, kind="ExternalOutput").ap()
    build(nc, aps, out)
    r = run_bass_kernel_spmd(nc, [arrays], core_ids=[0])
    return r.results[0]["out"].reshape(B, S, H)
```
